# Optimizing a Trainium2 kernel written in Bass

```python
import numpy as np
import jax
import jax.numpy as jnp

def _softmax(x, axis=-1):
    return jax.nn.softmax(x, axis=axis)

def _gelu(x):
    return jax.nn.gelu(x, approximate=True)

def _silu(x):
    return jax.nn.silu(x)

def _sigmoid(x):
    return jax.nn.sigmoid(x)

def _layernorm(x, axis=-1, eps=1e-05):
    m = jnp.mean(x, axis=axis, keepdims=True)
    v = jnp.var(x, axis=axis, keepdims=True)
    return (x - m) / jnp.sqrt(v + eps)

def _scatter_add(tgt, idx, src, axis=0):
    return tgt.at[idx].add(src)

def _segment_sum(src, seg, n):
    return jax.ops.segment_sum(src, seg, n)
kernel_name = 'mk_gnn_resnorm_d4_gnn_r8_bb08ed'

def setup_inputs(seed: int=0):
    np.random.seed(seed)
    _w = jnp.asarray

    def _rec_inputs():
        import jax
        import jax.numpy as jnp
        _gk = jax.random.key(seed)
        x = -8.776e-05 + 1 * jax.random.normal(jax.random.fold_in(_gk, 1), (1250, 512), jnp.float32)
        src = jax.random.randint(jax.random.fold_in(_gk, 2), (20000,), 0, 1250, jnp.int32)
        dst = jax.random.randint(jax.random.fold_in(_gk, 3), (20000,), 0, 1250, jnp.int32)
        _o = jnp.argsort(dst, stable=True)
        src = src[_o]
        dst = dst[_o]
        edge_type_2 = jax.random.randint(jax.random.fold_in(_gk, 15), (20000,), 0, 2, jnp.int32)
        edge_type_8 = jax.random.randint(jax.random.fold_in(_gk, 16), (20000,), 0, 8, jnp.int32)
        edge_weight = jax.random.uniform(jax.random.fold_in(_gk, 17), (20000,), jnp.float32, 0.0, 0.999999)
        return (x, src, dst, edge_type_2, edge_type_8, edge_weight)
    x, src, dst, edge_type_2, edge_type_8, edge_weight = _rec_inputs()

    def _L0_gnn_setup():
        import jax, jax.numpy as jnp
        import numpy as np
        N_NODES = 1250
        N_EDGES = 20000
        D_FEAT = 512
        OUT_CH = 512
        key = jax.random.key(seed)
        k1, k2, k3, k4 = jax.random.split(key, 4)
        x = jax.random.normal(k1, (N_NODES, D_FEAT), dtype=jnp.float32)
        edge_index = jax.random.randint(k2, (N_EDGES, 2), 0, N_NODES, dtype=jnp.int64)
        W = jax.random.normal(k3, (OUT_CH, 2 * D_FEAT), dtype=jnp.float32) / np.sqrt(2 * D_FEAT)
        b = jax.random.normal(k4, (OUT_CH,), dtype=jnp.float32) * 0.01
        return {'x': x, 'edge_index': edge_index, 'num_local_nodes': N_NODES, 'W': W, 'b': b}
    _L0_gnn_all = _L0_gnn_setup()
    _L0_gnn_in = {k: v for k, v in _L0_gnn_all.items() if k in ('W', 'b')}
    del _L0_gnn_all

    def _L1_gnn_setup():
        import jax, jax.numpy as jnp
        import numpy as np
        N, IN_DIM, H, D, E = (6250, 512, 8, 64, 100000)
        NEG_SLOPE = 0.2
        LN_EPS = 1e-05
        key = jax.random.key(seed)
        ks = jax.random.split(key, 8)
        x = jax.random.normal(ks[0], (N, IN_DIM), dtype=jnp.float32)
        edge_index = jax.random.randint(ks[1], (2, E), 0, N, dtype=jnp.int64)
        edge_type = jax.random.randint(ks[2], (E,), 0, 8, dtype=jnp.int64)
        edge_weight = jax.random.uniform(ks[3], (E,), dtype=jnp.float32)
        W = jax.random.normal(ks[4], (H * D, IN_DIM), dtype=jnp.float32) * (1.0 / np.sqrt(IN_DIM))
        a_src = jax.random.normal(ks[5], (H, D), dtype=jnp.float32) * (1.0 / np.sqrt(D))
        a_dst = jax.random.normal(ks[6], (H, D), dtype=jnp.float32) * (1.0 / np.sqrt(D))
        et_emb = jax.random.normal(ks[7], (8, H), dtype=jnp.float32)
        ln_gamma = jnp.ones((H * D,), dtype=jnp.float32)
        ln_beta = jnp.zeros((H * D,), dtype=jnp.float32)
        return {'x': x, 'edge_index': edge_index, 'edge_type': edge_type, 'edge_weight': edge_weight, 'W': W, 'a_src': a_src, 'a_dst': a_dst, 'et_emb': et_emb, 'ln_gamma': ln_gamma, 'ln_beta': ln_beta}
    _L1_gnn_all = _L1_gnn_setup()
    _L1_gnn_in = {k: v for k, v in _L1_gnn_all.items() if k in ('W', 'a_src', 'a_dst', 'et_emb', 'ln_gamma', 'ln_beta')}
    del _L1_gnn_all

    def _L2_gnn_setup():
        import jax, jax.numpy as jnp
        import numpy as np
        N_NODES = 1250
        N_EDGES = 20000
        IN_DIM = 512
        OUT_DIM = 512
        LN_EPS = 1e-05
        key = jax.random.key(seed)
        k_x, k_src, k_ws, k_wn = jax.random.split(key, 4)
        x = jax.random.normal(k_x, (N_NODES, IN_DIM), dtype=jnp.float32)
        edge_src = jax.random.randint(k_src, (N_EDGES,), 0, N_NODES, dtype=jnp.int32)
        edge_dst = jnp.repeat(jnp.arange(N_NODES, dtype=jnp.int32), N_EDGES // N_NODES)
        deg = jnp.full((N_NODES,), float(N_EDGES // N_NODES), dtype=jnp.float32)
        scale = 1.0 / np.sqrt(IN_DIM)
        W_self = jax.random.normal(k_ws, (OUT_DIM, IN_DIM), dtype=jnp.float32) * scale
        W_neigh = jax.random.normal(k_wn, (OUT_DIM, IN_DIM), dtype=jnp.float32) * scale
        bias = jnp.zeros((OUT_DIM,), dtype=jnp.float32)
        gamma = jnp.ones((OUT_DIM,), dtype=jnp.float32)
        beta = jnp.zeros((OUT_DIM,), dtype=jnp.float32)
        return {'x': x, 'edge_src': edge_src, 'edge_dst': edge_dst, 'deg': deg, 'W_self': W_self, 'W_neigh': W_neigh, 'bias': bias, 'gamma': gamma, 'beta': beta}
    _L2_gnn_all = _L2_gnn_setup()
    _L2_gnn_in = {k: v for k, v in _L2_gnn_all.items() if k in ('W_self', 'W_neigh', 'bias', 'gamma', 'beta')}
    del _L2_gnn_all

    def _L3_gnn_setup():
        import jax, jax.numpy as jnp
        import numpy as np
        NUM_RELATIONS = 2
        NUM_BASES = 30
        HIDDEN = 512
        N_NODES = 1250
        N_EDGES = 20000

        def rgcn_gate_layer(x, row, col, edge_type, basis, att, gate_w, root, bias):
            H = x.shape[1]
            w = jnp.einsum('rb,bio->rio', att, basis)
            x_j = x[col]
            msgs = []
            for r in range(NUM_RELATIONS):
                gate = jax.nn.sigmoid(x_j @ gate_w[r, :, 0])
                msgs.append(gate[:, None] * x_j @ w[r])
            msg = jnp.where((edge_type == 0)[:, None], msgs[0], msgs[1])
            agg = jax.ops.segment_sum(msg, row, num_segments=x.shape[0])
            return agg + x @ root + bias
        key = jax.random.key(seed)
        ks = jax.random.split(key, 16)
        H, R, B = (HIDDEN, NUM_RELATIONS, NUM_BASES)
        bound = 1.0 / np.sqrt(B * H)
        u = lambda k, shape: jax.random.uniform(k, shape, jnp.float32, -bound, bound)
        inp = {'x': jax.random.normal(ks[0], (N_NODES, H), jnp.float32), 'edge_index': jax.random.randint(ks[1], (2, N_EDGES), 0, N_NODES, jnp.int32), 'edge_type': jax.random.randint(ks[2], (N_EDGES,), 0, R, jnp.int32), 'basis1': u(ks[3], (B, H, H)), 'att1': u(ks[4], (R, B)), 'gate_w1': u(ks[5], (R, H, 1)), 'root1': u(ks[6], (H, H)), 'bias1': u(ks[7], (H,)), 'basis2': u(ks[8], (B, H, H)), 'att2': u(ks[9], (R, B)), 'gate_w2': u(ks[10], (R, H, 1)), 'root2': u(ks[11], (H, H)), 'bias2': u(ks[12], (H,))}
        return inp
    _L3_gnn_all = _L3_gnn_setup()
    _L3_gnn_in = {k: v for k, v in _L3_gnn_all.items() if k in ('basis1', 'att1', 'gate_w1', 'root1', 'bias1', 'basis2', 'att2', 'gate_w2', 'root2', 'bias2')}
    del _L3_gnn_all
    return {'x': x, 'src': src, 'dst': dst, 'edge_type_2': edge_type_2, 'edge_type_8': edge_type_8, 'edge_weight': edge_weight, 'L0_gnn_W': _L0_gnn_in['W'], 'L0_gnn_b': _L0_gnn_in['b'], 'L1_gnn_W': _L1_gnn_in['W'], 'L1_gnn_a_src': _L1_gnn_in['a_src'], 'L1_gnn_a_dst': _L1_gnn_in['a_dst'], 'L1_gnn_et_emb': _L1_gnn_in['et_emb'], 'L1_gnn_ln_gamma': _L1_gnn_in['ln_gamma'], 'L1_gnn_ln_beta': _L1_gnn_in['ln_beta'], 'L2_gnn_W_self': _L2_gnn_in['W_self'], 'L2_gnn_W_neigh': _L2_gnn_in['W_neigh'], 'L2_gnn_bias': _L2_gnn_in['bias'], 'L2_gnn_gamma': _L2_gnn_in['gamma'], 'L2_gnn_beta': _L2_gnn_in['beta'], 'L3_gnn_basis1': _L3_gnn_in['basis1'], 'L3_gnn_att1': _L3_gnn_in['att1'], 'L3_gnn_gate_w1': _L3_gnn_in['gate_w1'], 'L3_gnn_root1': _L3_gnn_in['root1'], 'L3_gnn_bias1': _L3_gnn_in['bias1'], 'L3_gnn_basis2': _L3_gnn_in['basis2'], 'L3_gnn_att2': _L3_gnn_in['att2'], 'L3_gnn_gate_w2': _L3_gnn_in['gate_w2'], 'L3_gnn_root2': _L3_gnn_in['root2'], 'L3_gnn_bias2': _L3_gnn_in['bias2']}

def reference(x, src, dst, edge_type_2, edge_type_8, edge_weight, L0_gnn_W, L0_gnn_b, L1_gnn_W, L1_gnn_a_src, L1_gnn_a_dst, L1_gnn_et_emb, L1_gnn_ln_gamma, L1_gnn_ln_beta, L2_gnn_W_self, L2_gnn_W_neigh, L2_gnn_bias, L2_gnn_gamma, L2_gnn_beta, L3_gnn_basis1, L3_gnn_att1, L3_gnn_gate_w1, L3_gnn_root1, L3_gnn_bias1, L3_gnn_basis2, L3_gnn_att2, L3_gnn_gate_w2, L3_gnn_root2, L3_gnn_bias2):
    import jax
    import jax.numpy as jnp

    def _L0_gnn_ref(x, edge_index, num_local_nodes, W, b):
        import jax, jax.numpy as jnp
        import numpy as np
        N_NODES = 1250
        N_EDGES = 20000
        D_FEAT = 512
        OUT_CH = 512
        src = edge_index[:, 0]
        tgt = edge_index[:, 1]
        x_i = x[src]
        x_j = x[tgt]
        x_ij = jnp.concatenate([x_i, x_j], axis=1)
        m_ij = jax.nn.relu(x_ij @ W.T + b)
        out = jax.ops.segment_sum(m_ij, src, num_segments=num_local_nodes)
        return out

    def _L1_gnn_ref(x, edge_index, edge_type, edge_weight, W, a_src, a_dst, et_emb, ln_gamma, ln_beta):
        import jax, jax.numpy as jnp
        import numpy as np
        N, IN_DIM, H, D, E = (6250, 512, 8, 64, 100000)
        NEG_SLOPE = 0.2
        LN_EPS = 1e-05
        n, h_, d_ = (x.shape[0], a_src.shape[0], a_src.shape[1])
        h = (x @ W.T).reshape(n, h_, d_)
        src, dst = (edge_index[0], edge_index[1])
        h_src = h[src]
        e_src = jnp.einsum('ehd,hd->eh', h_src, a_src)
        e_dst = jnp.einsum('ehd,hd->eh', h[dst], a_dst)
        e = jax.nn.leaky_relu(e_src + e_dst, NEG_SLOPE)
        e = e * (1.0 + et_emb[edge_type])
        e = e * edge_weight[:, None]
        e_max = jnp.zeros((n, h_), x.dtype).at[dst].max(e)
        e = jnp.exp(e - e_max[dst])
        e_sum = jnp.zeros((n, h_), x.dtype).at[dst].add(e)
        alpha = e / (e_sum[dst] + 1e-10)
        msg = h_src * alpha[:, :, None]
        out = jnp.zeros((n, h_, d_), x.dtype).at[dst].add(msg).reshape(n, h_ * d_)
        out = out + x
        mu = jnp.mean(out, axis=-1, keepdims=True)
        var = jnp.var(out, axis=-1, keepdims=True)
        return (out - mu) / jnp.sqrt(var + LN_EPS) * ln_gamma + ln_beta

    def _L2_gnn_ref(x, edge_src, edge_dst, deg, W_self, W_neigh, bias, gamma, beta):
        import jax, jax.numpy as jnp
        import numpy as np
        N_NODES = 1250
        N_EDGES = 20000
        IN_DIM = 512
        OUT_DIM = 512
        LN_EPS = 1e-05
        n = x.shape[0]
        h_self = jnp.einsum('nd,od->no', x, W_self)
        neigh_sum = jax.ops.segment_sum(x[edge_src], edge_dst, num_segments=n)
        neigh_mean = neigh_sum / jnp.maximum(deg, 1.0)[:, None]
        h_neigh = jnp.einsum('nd,od->no', neigh_mean, W_neigh)
        h = h_self + h_neigh + bias
        mu = jnp.mean(h, axis=-1, keepdims=True)
        var = jnp.mean(jnp.square(h - mu), axis=-1, keepdims=True)
        h = (h - mu) * jax.lax.rsqrt(var + LN_EPS)
        return h * gamma + beta

    def _L3_gnn_ref(x, edge_index, edge_type, basis1, att1, gate_w1, root1, bias1, basis2, att2, gate_w2, root2, bias2):
        import jax, jax.numpy as jnp
        import numpy as np
        NUM_RELATIONS = 2
        NUM_BASES = 30
        HIDDEN = 512
        N_NODES = 1250
        N_EDGES = 20000

        def rgcn_gate_layer(x, row, col, edge_type, basis, att, gate_w, root, bias):
            H = x.shape[1]
            w = jnp.einsum('rb,bio->rio', att, basis)
            x_j = x[col]
            msgs = []
            for r in range(NUM_RELATIONS):
                gate = jax.nn.sigmoid(x_j @ gate_w[r, :, 0])
                msgs.append(gate[:, None] * x_j @ w[r])
            msg = jnp.where((edge_type == 0)[:, None], msgs[0], msgs[1])
            agg = jax.ops.segment_sum(msg, row, num_segments=x.shape[0])
            return agg + x @ root + bias
        row, col = (edge_index[0], edge_index[1])
        h = jax.nn.relu(rgcn_gate_layer(x, row, col, edge_type, basis1, att1, gate_w1, root1, bias1))
        out = rgcn_gate_layer(h, row, col, edge_type, basis2, att2, gate_w2, root2, bias2)
        return out
    edge_index = jnp.stack([src, dst])
    edge_index_t = jnp.stack([src, dst], axis=1)
    deg = jnp.maximum(jax.ops.segment_sum(jnp.ones(dst.shape, jnp.float32), dst, num_segments=1250), 1.0)
    x = _layernorm(x + _L0_gnn_ref(x, edge_index_t, 1250, L0_gnn_W, L0_gnn_b), axis=-1)
    x = _layernorm(x + _L1_gnn_ref(x, edge_index, edge_type_8, edge_weight, L1_gnn_W, L1_gnn_a_src, L1_gnn_a_dst, L1_gnn_et_emb, L1_gnn_ln_gamma, L1_gnn_ln_beta), axis=-1)
    x = _layernorm(x + _L2_gnn_ref(x, src, dst, deg, L2_gnn_W_self, L2_gnn_W_neigh, L2_gnn_bias, L2_gnn_gamma, L2_gnn_beta), axis=-1)
    x = _layernorm(x + _L3_gnn_ref(x, edge_index, edge_type_2, L3_gnn_basis1, L3_gnn_att1, L3_gnn_gate_w1, L3_gnn_root1, L3_gnn_bias1, L3_gnn_basis2, L3_gnn_att2, L3_gnn_gate_w2, L3_gnn_root2, L3_gnn_bias2), axis=-1)
    return x

_drawn_inputs = setup_inputs


def setup_inputs(seed=0):
    import zlib

    import numpy as np

    out = dict(_drawn_inputs(seed))
    spreads = {'L1_gnn_ln_gamma': (1.0, 0.2),
     'L1_gnn_ln_beta': (0.0, 0.1),
     'L2_gnn_bias': (0.0, 0.1),
     'L2_gnn_gamma': (1.0, 0.2),
     'L2_gnn_beta': (0.0, 0.1)}
    factors = {'L0_gnn_b': 3.003,
     'L3_gnn_basis1': 8.0,
     'L3_gnn_att1': 8.0,
     'L3_gnn_gate_w1': 8.0,
     'L3_gnn_root1': 8.0,
     'L3_gnn_bias1': 8.0,
     'L3_gnn_basis2': 8.0,
     'L3_gnn_att2': 8.0,
     'L3_gnn_gate_w2': 8.0,
     'L3_gnn_root2': 7.226,
     'L3_gnn_bias2': 8.0}
    for name, (base, spread) in spreads.items():
        noise = np.random.default_rng([zlib.crc32(name.encode()), seed]).standard_normal(out[name].shape)
        drawn = base * np.exp(spread * noise) if base else spread * noise
        out[name] = jnp.asarray(drawn.astype(out[name].dtype))
    for name, factor in factors.items():
        out[name] = (out[name] * factor).astype(out[name].dtype)
    return out
```

```python
import concourse.bass as bass
from concourse import mybir
from contextlib import ExitStack
import numpy as np

F32, BF16, I32 = mybir.dt.float32, mybir.dt.bfloat16, mybir.dt.int32
ALU, ACT, AX = mybir.AluOpType, mybir.ActivationFunctionType, mybir.AxisListType

P = 128
N, E, D = 1250, 20000, 512
NB = -(-N // P)
NP = NB * P
EP, T = 125, 160
GT = 16
HI, LO = NP // 32, 32
KO = HI + LO
PAIRS = E // 256 + NB
SLOTS = 2 * PAIRS
ROWS = SLOTS * P
RC = 8
LOC, COL1, COL2, COL3, COL4, ROW = 0, 1, 2, 3, 4, 7
H, DH = 8, 64


def stage_semaphores(nc, ctx, name):
    taken = []

    def give_back():
        nc.clear_and_free_semaphores(taken)
        nc.all_engine_barrier(sem_only=True)

    ctx.callback(give_back)

    def sem(what):
        taken.append(nc.alloc_semaphore(name=f"{name}_{what}_{nc.next_id()}"))
        return taken[-1]

    return sem


def chain(eng, sem):
    count = [0]

    def link(ins):
        count[0] += 1
        ins.then_inc(sem, 1)
        eng.wait_ge(sem, count[0])

    return link


def wait(eng, sem, value):
    if isinstance(value, int) and value <= 0:
        return
    eng.wait_ge(sem, value)


def peeled(eng, n, body):
    body(0)
    with eng.Fori(1, n) as i:
        body(i)


def constants():
    m = np.arange(HI)
    c = {}
    c["ident"] = np.eye(P)
    e = np.arange(P)
    c["earlier"] = (e[None, :] < e[:, None]) * 1.0
    c["iota_hi"] = np.tile(np.arange(HI), (P, 1))
    c["iota_lo"] = np.tile(np.arange(LO), (P, 1))
    c["iota_p"] = np.tile(np.arange(P), (P, 1))
    c["pair_start"] = np.tile(np.arange(PAIRS) * 256, (P, 1))
    def rows40(a):
        out = np.zeros((P, a.shape[1]))
        out[:HI] = a
        return out
    c["same_block"] = rows40((m[:, None] // 4 == m[None, :] // 4) * 1.0)
    c["lower_in_block"] = rows40(((m[:, None] // 4 == m[None, :] // 4) & (m[:, None] < m[None, :])) * 1.0)
    c["first_of_lower_block"] = rows40(((m[:, None] % 4 == 0) & (m[:, None] // 4 < m[None, :] // 4)) * 1.0)
    c["block_head"] = rows40(((m % 4 == 0) & (m > 0))[:, None] * 1.0)
    cols, at = [], {}
    n = 0
    for k, v in c.items():
        at[k] = (n, n + v.shape[1])
        n += v.shape[1]
        cols.append(v)
    return np.concatenate(cols, 1).astype(np.float32), at


CONSTS, CAT = constants()


class Const:
    def __init__(self, tile, tileb):
        self.t, self.b = tile, tileb

    def f(self, name, parts=P):
        a, b = CAT[name]
        return self.t[0:parts, a:b]


def rank_edges(nc, name, C, identb, key, fields, rec, pair_block, row_major):
    with ExitStack() as ctx:
        sb = lambda n, s, d: ctx.enter_context(nc.sbuf_tensor(f"{name}_{n}", s, d))
        ki = sb("key_int", [EP, T], I32)
        ti = sb("int_tmp", [EP, T], I32)
        hif = sb("hi_f", [EP, T], F32)
        lof = sb("lo_f", [EP, T], F32)
        onehot = sb("onehot", [EP, T, KO], BF16)
        onehotT = sb("onehotT", [KO, T, EP], BF16)
        cnt = sb("cnt", [HI, LO, T], F32)
        inc = sb("inc", [HI, LO, T], F32)
        prea = sb("prefix_rounded", [HI, LO, T], BF16)
        preb = sb("prefix_rest", [HI, LO, T], BF16)
        rankin = sb("rank_in_tile", [EP, T], F32)
        rankto = sb("rank_to_tile", [EP, T], F32)
        tmp = sb("gather_tmp", [EP, GT, LO], F32)
        small = sb("small", [HI, 8], F32)
        smalli = sb("small_i", [HI, 2], I32)
        atleast = sb("pair_at_least", [HI, PAIRS], F32)
        eqtmp = sb("eq_tmp", [EP, 4, EP], F32)
        tot = small[:, 0:1]

        with ExitStack() as c1:
            sem = stage_semaphores(nc, c1, name)
            pt = c1.enter_context(nc.psum_tensor(f"{name}_pT", [KO, 2, 8, 128], BF16))
            pc = c1.enter_context(nc.psum_tensor(f"{name}_pC", [HI, GT, LO], F32))
            pe_ = c1.enter_context(nc.psum_tensor(f"{name}_pE", [EP, 4, 4, 128], F32))
            s_dve = sem("dve_chain")
            onehots_ready = sem("onehots_ready")
            transposed, counted, moved = sem("transposed"), sem("counted"), sem("moved")
            compared, ranked = sem("compared"), sem("ranked")
            block = c1.enter_context(nc.Block())

            @block.vector
            def _(v):
                link = chain(v, s_dve)
                link(nc.vector.tensor_copy(ki[:, :], key))
                link(nc.vector.tensor_single_scalar(ti[:, :], ki[:, :], 5, ALU.logical_shift_right))
                link(nc.vector.tensor_copy(hif[:, :], ti[:, :]))
                link(nc.vector.tensor_single_scalar(ti[:, :], ki[:, :], 31, ALU.bitwise_and))
                link(nc.vector.tensor_copy(lof[:, :], ti[:, :]))
                for f, iota, a, n in ((hif, "iota_hi", 0, HI), (lof, "iota_lo", HI, LO)):
                    nc.vector.tensor_tensor(
                        onehot[:, :, a:a + n],
                        C.f(iota, EP).unsqueeze(1).to_broadcast([EP, T, n]),
                        f[:, :].unsqueeze(2).to_broadcast([EP, T, n]), ALU.is_equal,
                    ).then_inc(onehots_ready, 1)
                def step(g):
                    for u in range(GT):
                        if u % 4 == 0:
                            v.wait_ge(compared, g * 4 + (u // 4 + 1))
                        wait(v, ranked, g * GT + (u - 3))
                        nc.vector.scalar_tensor_tensor(
                            eqtmp[:, u % 4, :], pe_[:, u // 4, u % 4, 0:EP], 2.0,
                            C.f("earlier", EP)[:, 0:EP], ALU.is_equal, ALU.mult,
                            accum_out=rankin[:, bass.ds(g * GT + u, 1)]).then_inc(ranked, 1)
                peeled(v, T // GT, step)

            @block.tensor
            def _(pe):
                pe.wait_ge(onehots_ready, 2)
                def step(g):
                    wait(pe, moved, g * 3)
                    for u in range(GT):
                        ins = nc.tensor.transpose(
                            pt[:, u // 8, u % 8, 0:EP],
                            onehot[:, bass.ds(g * GT + u, 1), :].rearrange("p a n -> p (a n)"),
                            identb[0:EP, 0:EP])
                        if u % 8 == 7:
                            ins.then_inc(transposed, 1)
                    for u in range(GT):
                        oh = onehot[:, bass.ds(g * GT + u, 1), :].rearrange("p a n -> p (a n)")
                        ins = nc.tensor.matmul(pc[:, u, :], oh[:, 0:HI], oh[:, HI:KO],
                                               start=True, stop=True)
                    ins.then_inc(counted, 1)
                    pe.wait_ge(moved, g * 3 + 2)
                    wait(pe, ranked, g * GT)
                    for u in range(GT):
                        oh = onehotT[:, bass.ds(g * GT + u, 1), :].rearrange("p a n -> p (a n)")
                        ins = nc.tensor.matmul(pe_[:, u // 4, u % 4, 0:EP], oh, oh, start=True, stop=True)
                        if u % 4 == 3:
                            ins.then_inc(compared, 1)
                peeled(pe, T // GT, step)

            @block.scalar
            def _(act):
                with act.Fori(0, T // GT) as g:
                    for w in range(2):
                        act.wait_ge(transposed, g * 2 + (w + 1))
                        nc.scalar.copy(
                            onehotT[:, bass.ds(g * GT + w * 8, 8), :], pt[:, w, :, 0:EP]).then_inc(moved, 1)
                    act.wait_ge(counted, g + 1)
                    nc.scalar.copy(cnt[:, :, bass.ds(g * GT, GT)].rearrange("p l t -> p t l"),
                                   pc[:, :, :]).then_inc(moved, 1)

        with ExitStack() as c1:
            sem = stage_semaphores(nc, c1, name)
            ps = c1.enter_context(nc.psum_tensor(f"{name}_pS", [HI, 4], F32))
            pp = c1.enter_context(nc.psum_tensor(f"{name}_pP", [1, PAIRS], F32))
            pg = c1.enter_context(nc.psum_tensor(f"{name}_pG", [EP, 2, GT, LO], F32))
            s_dve, summed = sem("dve_chain"), sem("summed")
            tot_ready, pads_ready, prefix_ready, pairs_ready = (
                sem("tot_ready"), sem("pads_ready"), sem("prefix_ready"), sem("pairs_ready"))
            gathered, taken, s_red = sem("gathered"), sem("taken"), sem("reduced")
            block = c1.enter_context(nc.Block())

            @block.vector
            def _(v):
                link = chain(v, s_dve)
                flat = lambda a: a[:, :, :].rearrange("p l t -> p (l t)")
                link(nc.vector.memset(small[:, 1:2], 0.0))
                nc.vector.tensor_tensor_scan(flat(inc), flat(cnt),
                                             small[:, 1:2].to_broadcast([HI, LO * T]), 0.0,
                                             ALU.add, ALU.add).then_inc(tot_ready, 1)
                v.wait_ge(summed, 1)
                link(nc.vector.tensor_scalar(smalli[:, 0:1], ps[:, 0:1], 255.0, None, ALU.add))
                link(nc.vector.tensor_scalar(smalli[:, 1:2], smalli[:, 0:1], 8, 8,
                                             ALU.logical_shift_right, ALU.logical_shift_left))
                nc.vector.tensor_copy(small[:, 2:3], smalli[:, 1:2]).then_inc(pads_ready, 1)
                v.wait_ge(summed, 2)
                link(nc.vector.tensor_copy(small[:, 4:6], ps[:, 1:3]))
                link(nc.vector.tensor_tensor(small[:, 3:4], small[:, 4:5], small[:, 5:6], ALU.add))
                nc.vector.tensor_scalar(atleast[:, :], C.f("pair_start", HI), small[:, 5:6], None,
                                        ALU.is_ge).then_inc(pairs_ready, 1)
                link(nc.vector.scalar_tensor_tensor(flat(inc), flat(inc), small[:, 3:4], flat(cnt),
                                                    ALU.add, ALU.subtract))
                link(nc.vector.tensor_copy(flat(prea), flat(inc)))
                nc.vector.tensor_tensor(flat(preb), flat(inc), flat(prea),
                                        ALU.subtract).then_inc(prefix_ready, 1)
                v.wait_ge(summed, 3)
                nc.vector.tensor_copy(pair_block, pp[:, :])
                with v.Fori(0, T // GT // 2) as g:
                    for w in range(2):
                        v.wait_ge(gathered, g * 2 + (w + 1))
                        nc.vector.tensor_tensor(tmp[:, :, :], pg[:, w, :, :],
                                                onehot[:, bass.ds(g * 2 * GT + w * GT, GT), HI:KO],
                                                ALU.mult).then_inc(taken, 1)
                        v.wait_ge(taken, g * 2 + (w + 1))
                        nc.vector.tensor_reduce(rankto[:, bass.ds(g * 2 * GT + w * GT, GT)], tmp[:, :, :],
                                                AX.X, ALU.add).then_inc(s_red, 1)
                        v.wait_ge(s_red, g * 2 + (w + 1))
                link(nc.vector.tensor_tensor(ki[:, :], rankto[:, :], rankin[:, :], ALU.add))
                if row_major:
                    link(nc.vector.tensor_single_scalar(ti[:, :], ki[:, :], 127, ALU.bitwise_and))
                    link(nc.vector.tensor_copy(hif[:, :], ti[:, :]))
                    link(nc.vector.tensor_single_scalar(ti[:, :], ki[:, :], 7, ALU.logical_shift_right))
                    link(nc.vector.tensor_copy(lof[:, :], ti[:, :]))
                    link(nc.vector.scalar_tensor_tensor(ki[:, :], hif[:, :], float(SLOTS), lof[:, :],
                                                        ALU.mult, ALU.add))
                link(nc.vector.tensor_copy(rec[:, :, ROW:ROW + 1].bitcast(I32).rearrange("p t a -> p (t a)"),
                                           ki[:, :]))
                link(nc.vector.tensor_copy(ki[:, :], key))
                link(nc.vector.tensor_single_scalar(ti[:, :], ki[:, :], 127, ALU.bitwise_and))
                link(nc.vector.tensor_copy(rec[:, :, LOC], ti[:, :]))
                for col, f in fields:
                    link(nc.vector.tensor_copy(rec[:, :, col], f))

            @block.tensor
            def _(pe):
                pe.wait_ge(tot_ready, 1)
                total = inc[:, LO - 1, T - 1:T]
                nc.tensor.matmul(ps[:, 0:1], C.f("same_block", HI), total, start=True, stop=True
                                 ).then_inc(summed, 1)
                pe.wait_ge(pads_ready, 1)
                nc.tensor.matmul(ps[:, 1:2], C.f("lower_in_block", HI), total, start=True, stop=True)
                nc.tensor.matmul(ps[:, 2:3], C.f("first_of_lower_block", HI), small[:, 2:3],
                                 start=True, stop=True).then_inc(summed, 1)
                pe.wait_ge(pairs_ready, 1)
                nc.tensor.matmul(pp[:, :], C.f("block_head", HI), atleast[:, :], start=True, stop=True
                                 ).then_inc(summed, 1)
                pe.wait_ge(prefix_ready, 1)
                def step(g):
                    for w in range(2):
                        wait(pe, taken, g * 2 + (w - 1))
                        for u in range(GT):
                            t = g * 2 * GT + (w * GT + u)
                            oh = onehotT[0:HI, bass.ds(t, 1), :].rearrange("p a n -> p (a n)")
                            nc.tensor.matmul(pg[:, w, u, :], oh, prea[:, :, bass.ds(t, 1)].rearrange("p l a -> p (l a)"),
                                             start=True, stop=False)
                            ins = nc.tensor.matmul(pg[:, w, u, :], oh, preb[:, :, bass.ds(t, 1)].rearrange("p l a -> p (l a)"),
                                                   start=False, stop=True)
                        ins.then_inc(gathered, 1)
                peeled(pe, T // GT // 2, step)


def write_records(nc, name, rec, table, fill):
    RING = 8
    with ExitStack() as ctx:
        sem = stage_semaphores(nc, ctx, name)
        ring = ctx.enter_context(nc.sbuf_tensor(f"{name}_rec_ring", [EP, RING, RC], F32))
        filled, copied = sem("table_filled"), sem("rec_copied")
        checked = sem("checked")
        written = [sem(f"rec_written{k}") for k in range(RING)]
        block = ctx.enter_context(nc.Block())

        @block.sync
        def _(sp):
            sp.dma_start(table.rearrange("(p s) c -> p (s c)", p=P),
                         fill[:, :].rearrange("p (s c) -> p s c", c=RC).rearrange("p s c -> p (s c)")).then_inc(filled, 16)
            sp.wait_ge(filled, 16)

        @block.gpsimd
        def _(pool):
            pool.wait_ge(filled, 16)

            def step(i):
                for k in range(RING):
                    wait(pool, written[k], i * 16)
                    nc.gpsimd.tensor_copy(ring[:, k, :],
                                          rec[:, bass.ds(i * RING + k, 1), :].rearrange("p a c -> p (a c)")
                                          ).then_inc(copied, 1)
                    pool.wait_ge(copied, i * RING + (k + 1))
                    pool.sem_inc(checked, 1)
                    pool.indirect_dma_start(table, bass.IndirectOffsetOnAxis(ring[:, k, ROW:ROW + 1].bitcast(I32), 0),
                                            ring[:, k, :], None).then_inc(written[k], 16)
            peeled(pool, T // RING, step)
            for k in range(RING):
                pool.wait_ge(written[k], T // RING * 16)


def flat(ap):
    return ap.rearrange("p a n -> p (a n)")


RINGP = 4
BODYP = 8
NSTEP = PAIRS // BODYP


def edge_pass(nc, name, C, tables, idx, loc, pair_block, acc, kind, weight=None, side=None):
    nt = len(tables)
    ns = {"weighted": H, "counted": 1}.get(kind, 0)
    with ExitStack() as ctx:
        sb = lambda n, s, d: ctx.enter_context(nc.sbuf_tensor(f"{name}_{n}", s, d))
        sem = stage_semaphores(nc, ctx, name)
        rows = sb("rows", [P, RINGP, 2, nt, D], F32)
        idxr = sb("idx_ring", [P, nt, 2, 8], I32)
        ohr = sb("onehot_ring", [P, 2, 2, P], F32)
        ps = ctx.enter_context(nc.psum_tensor(f"{name}_ps", [P, 2, D], F32))
        psn = ctx.enter_context(nc.psum_tensor(f"{name}_psn", [P, 2, D], F32)) if ns else None
        ones = sb("ones", [P, 1], F32) if kind == "counted" else None
        idx_copied, sent = sem("idx_copied"), sem("sent")
        got = [sem(f"got{q}") for q in range(RINGP)]
        zeroed, oh_ready, msg_ready, relu_done = sem("zeroed"), sem("oh_ready"), sem("msg_ready"), sem("relu_done")
        summed, added, nadded = sem("summed"), sem("added"), sem("nadded")
        block = ctx.enter_context(nc.Block())

        @block.gpsimd
        def _(pool):
            def step(i):
                for half in range(2):
                    for q in range(RINGP):
                        wait(pool, got[q], (i * 2 + (half - 1)) * (32 * nt))
                    for t in range(nt):
                        ins = nc.gpsimd.tensor_copy(idxr[:, t, half, :],
                                                    idx[t][:, bass.ds(i * 16 + half * 8, 8)])
                    ins.then_inc(idx_copied, 1)
                    pool.wait_ge(idx_copied, i * 2 + (half + 1))
                    for q in range(RINGP):
                        wait(pool, summed, i * BODYP + (half * 4 + q - 3))
                        pool.sem_inc(sent, 1)
                        for s in range(2):
                            for t in range(nt):
                                pool.indirect_dma_start(
                                    rows[:, q, s, t, :], None, tables[t],
                                    bass.IndirectOffsetOnAxis(idxr[:, t, half, q * 2 + s:q * 2 + s + 1], 0),
                                ).then_inc(got[q], 16)
            peeled(pool, NSTEP, step)

        @block.vector
        def _(v):
            nc.vector.memset(acc[:, :, :], 0.0).then_inc(zeroed, 1)
            if ns:
                nc.vector.memset(side[:, :, :], 0.0).then_inc(zeroed, 1)
            if kind == "counted":
                nc.vector.memset(ones[:, :], 1.0).then_inc(zeroed, 1)
            v.wait_ge(zeroed, 1 + (ns > 0) + (kind == "counted"))

            def accumulate(i, m):
                j1 = i * BODYP + (m + 1)
                b = v.value_load(pair_block[0:1, bass.ds(i * BODYP + m, 1)], min_val=0, max_val=NB - 1)
                v.wait_ge(summed, j1)
                wait(v, added, i * BODYP + m)
                a = flat(acc[:, bass.ds(b, 1), :])
                nc.vector.tensor_tensor(a, ps[:, m % 2, :], a, ALU.add).then_inc(added, 1)
                if ns:
                    wait(v, nadded, i * BODYP + m)
                    a = flat(side[:, bass.ds(b, 1), :])
                    nc.vector.tensor_tensor(a, psn[:, m % 2, 0:ns], a, ALU.add).then_inc(nadded, 1)

            def step(i):
                for m in range(BODYP):
                    wait(v, summed, i * BODYP + (m - 1))
                    nc.vector.tensor_tensor(
                        ohr[:, m % 2, :, :],
                        C.f("iota_p").unsqueeze(1).to_broadcast([P, 2, P]),
                        loc[:, bass.ds(i * 16 + m * 2, 2)].unsqueeze(2).to_broadcast([P, 2, P]),
                        ALU.is_equal).then_inc(oh_ready, 1)
                    q = m % RINGP
                    if kind == "relu_sum":
                        v.wait_ge(got[q], (i * 2 + (m // 4 + 1)) * (32 * nt))
                        nc.vector.tensor_tensor(rows[:, q, :, 0, :], rows[:, q, :, 0, :],
                                                rows[:, q, :, 1, :], ALU.add).then_inc(msg_ready, 1)
                    if kind == "weighted":
                        v.wait_ge(got[q], (i * 2 + (m // 4 + 1)) * (32 * nt))
                        r = rows[:, q, :, 0, :].rearrange("p s (h d) -> p (s h) d", h=H)
                        nc.vector.tensor_tensor(
                            r, r, flat(weight[:, bass.ds(i * 16 + m * 2, 2), :]).unsqueeze(2).to_broadcast([P, 2 * H, DH]),
                            ALU.mult).then_inc(msg_ready, 1)
                    if m:
                        accumulate(i, m - 1)
                    elif not isinstance(i, int):
                        accumulate(i - 1, BODYP - 1)
            peeled(v, NSTEP, step)
            accumulate(NSTEP - 1, BODYP - 1)

        if kind == "relu_sum":
            @block.scalar
            def _(act):
                def step(i):
                    for m in range(BODYP):
                        act.wait_ge(msg_ready, i * BODYP + (m + 1))
                        r = rows[:, m % RINGP, :, 0, :]
                        nc.scalar.activation(r, r, ACT.Relu).then_inc(relu_done, 1)
                peeled(act, NSTEP, step)

        @block.tensor
        def _(pe):
            pe.wait_ge(zeroed, 1 + (ns > 0) + (kind == "counted"))

            def step(i):
                for m in range(BODYP):
                    j1 = i * BODYP + (m + 1)
                    q = m % RINGP
                    pe.wait_ge(oh_ready, j1)
                    if kind == "relu_sum":
                        pe.wait_ge(relu_done, j1)
                    elif kind == "weighted":
                        pe.wait_ge(msg_ready, j1)
                    else:
                        pe.wait_ge(got[q], (i * 2 + (m // 4 + 1)) * (32 * nt))
                    wait(pe, added, i * BODYP + (m - 1))
                    if ns:
                        wait(pe, nadded, i * BODYP + (m - 1))
                    for s in range(2):
                        ins = nc.tensor.matmul(ps[:, m % 2, :], ohr[:, m % 2, s, :], rows[:, q, s, 0, :],
                                               start=s == 0, stop=s == 1)
                        if ns:
                            n = (weight[:, bass.ds(i * 16 + (m * 2 + s), 1), :].rearrange("p a h -> p (a h)")
                                 if kind == "weighted" else ones[:, :])
                            ins = nc.tensor.matmul(psn[:, m % 2, 0:ns], ohr[:, m % 2, s, :], n,
                                                   start=s == 0, stop=s == 1)
                    ins.then_inc(summed, 1)
            peeled(pe, NSTEP, step)


def layer_stats(link, nc, v, act_sem, dve_sem, src, S, n):
    for b in range(NB):
        link(nc.vector.bn_stats(S["bn"][:, b, :], src[:, b, :]))
        link(nc.vector.bn_aggr(S["mv"][:, b, :], S["bn"][:, b, :]))
    nc.vector.tensor_scalar(S["var"][:, :], S["mv"][:, :, 1], 1e-5, None, ALU.add).then_inc(dve_sem, 1)
    v.wait_ge(act_sem, n)
    link(nc.vector.reciprocal(S["rstd"][:, :], S["sd"][:, :]))


def node_stage(nc, name, C, X, acc, S, pre, n_stats, weights, norm_src, save, gate=None):
    nw = len(weights)
    with ExitStack() as ctx:
        sb = lambda n, s, d: ctx.enter_context(nc.sbuf_tensor(f"{name}_{n}", s, d))
        sem = stage_semaphores(nc, ctx, name)
        xn = sb("x_block", [P, 2, D], F32)
        xt = sb("xT_block", [P, 2, 4, P], F32)
        yr = sb("y_ring", [P, 2, nw, D], F32)
        tmp = sb("tmp", [P, D], F32)
        gates = sb("gates", [P, 2, 2], F32)
        pt = ctx.enter_context(nc.psum_tensor(f"{name}_pT", [P, 4, P], F32))
        py = ctx.enter_context(nc.psum_tensor(f"{name}_pY", [P, 2, nw, D], F32))
        pgate = ctx.enter_context(nc.psum_tensor(f"{name}_pGate", [P, 2, 2], F32)) if gate is not None else None
        s_dve, s_var, s_sd, pre_done = sem("dve_chain"), sem("var_ready"), sem("sd_ready"), sem("pre_done")
        normed, saved, transposed, xcopied = sem("normed"), sem("saved"), sem("transposed"), sem("xcopied")
        multiplied, dve_out, act_out, s_tmp = sem("multiplied"), sem("dve_out"), sem("act_out"), sem("s_tmp")
        gated = sem("gated")
        stored = [sem(f"stored{k}") for k in range(2)]
        on_dve = [w for w, (_, kind, _) in enumerate(weights) if kind in ("bias_table", "bias_keep")]
        on_act = [w for w, (_, kind, _) in enumerate(weights) if kind in ("table", "gated", "attend")]
        tabled = [w for w, (_, kind, _) in enumerate(weights) if kind != "bias_keep"]
        attend = [w for w, (_, kind, _) in enumerate(weights) if kind == "attend"]
        n_dve = len(on_dve) + len(attend)
        block = ctx.enter_context(nc.Block())

        @block.vector
        def _(v):
            link = chain(v, s_dve)
            if pre:
                pre(link, v, s_var, s_sd)

            def norm(b, k):
                wait(v, transposed, b - 1)
                wait(v, saved, b - 1)
                if norm_src is not None:
                    nc.vector.tensor_scalar(xn[:, k, :], flat(norm_src[:, bass.ds(b, 1), :]),
                                            S["mv"][:, bass.ds(b, 1), 0], S["rstd"][:, bass.ds(b, 1)],
                                            ALU.subtract, ALU.mult).then_inc(normed, 1)
                else:
                    nc.vector.tensor_copy(xn[:, k, :], flat(X[:, bass.ds(b, 1), :])).then_inc(normed, 1)
                v.wait_ge(normed, b + 1)
                if save:
                    nc.vector.tensor_copy(flat(X[:, bass.ds(b, 1), :]), xn[:, k, :]).then_inc(saved, 1)
                else:
                    v.sem_inc(saved, 1)

            def finish(b, k, rounds):
                v.wait_ge(multiplied, b + 1)
                if set(on_dve) & set(tabled):
                    wait(v, stored[k], rounds * (16 * len(tabled)))
                for w in on_dve:
                    _, kind, (bias, keep) = weights[w]
                    o = yr[:, k, w, :] if kind == "bias_table" else flat(keep[:, bass.ds(b, 1), :])
                    ins = nc.vector.tensor_tensor(o, py[:, k, w, :], bias, ALU.add)
                if on_dve:
                    ins.then_inc(dve_out, 1)
                for w in attend:
                    v.wait_ge(act_out, b + 1)
                    for n, (vec, est) in enumerate(weights[w][2]):
                        wait(v, s_tmp, b * 4 + 2 * n)
                        nc.vector.tensor_tensor(tmp[:, :], yr[:, k, w, :], vec, ALU.mult).then_inc(s_tmp, 1)
                        v.wait_ge(s_tmp, b * 4 + (2 * n + 1))
                        nc.vector.tensor_reduce(flat(est[:, bass.ds(b, 1), :]),
                                                tmp[:, :].rearrange("p (h d) -> p h d", h=H),
                                                AX.X, ALU.add).then_inc(s_tmp, 1)
                    v.wait_ge(s_tmp, b * 4 + 4)
                    v.sem_inc(dve_out, 1)

            def step(i):
                for k in range(2):
                    norm(i * 2 + k, k)
                    if k or not isinstance(i, int):
                        finish(i * 2 + (k - 1), 1 - k, i if k else i - 1)
            peeled(v, NB // 2, step)
            finish(NB - 1, 1, NB // 2 - 1)

        @block.tensor
        def _(pe):
            def turn(b, k):
                pe.wait_ge(normed, b + 1)
                wait(pe, xcopied, b)
                for c in range(4):
                    ins = nc.tensor.transpose(pt[:, c, :], xn[:, k, c * P:(c + 1) * P], C.f("ident"))
                ins.then_inc(transposed, 1)

            def multiply(b, k):
                pe.wait_ge(xcopied, b + 1)
                if n_dve:
                    wait(pe, dve_out, b - 1)
                wait(pe, act_out, b - 1)
                for w in range(nw):
                    for c in range(4):
                        ins = nc.tensor.matmul(py[:, k, w, :], xt[:, k, c, :], weights[w][0][:, c, :],
                                               start=c == 0, stop=c == 3)
                if gate is not None:
                    wait(pe, gated, b)
                    for c in range(4):
                        ins = nc.tensor.matmul(pgate[:, k, :], xt[:, k, c, :], gate[:, c, :],
                                               start=c == 0, stop=c == 3)
                ins.then_inc(multiplied, 1)

            def step(i):
                for k in range(2):
                    turn(i * 2 + k, k)
                    if k or not isinstance(i, int):
                        multiply(i * 2 + (k - 1), 1 - k)
            peeled(pe, NB // 2, step)
            multiply(NB - 1, 1)

        @block.scalar
        def _(act):
            for n in range(n_stats):
                act.wait_ge(s_var, n + 1)
                nc.scalar.activation(S["sd"][:, :], S["var"][:, :], ACT.Sqrt).then_inc(s_sd, 1)

            def copy_x(b, k):
                act.wait_ge(transposed, b + 1)
                wait(act, multiplied, b - 1)
                nc.scalar.copy(xt[:, k, :, :], pt[:, :, :]).then_inc(xcopied, 1)

            def finish(b, k, rounds):
                act.wait_ge(multiplied, b + 1)
                if gate is not None:
                    nc.scalar.activation(gates[:, k, :], pgate[:, k, :], ACT.Sigmoid).then_inc(gated, 1)
                    act.wait_ge(gated, b + 1)
                if on_act:
                    wait(act, stored[k], rounds * (16 * len(tabled)))
                for w in on_act:
                    _, kind, extra = weights[w]
                    scale = gates[:, k, extra:extra + 1] if kind == "gated" else 1.0
                    ins = nc.scalar.activation(yr[:, k, w, :], py[:, k, w, :], ACT.Copy, scale=scale)
                ins.then_inc(act_out, 1)

            def step(i):
                for k in range(2):
                    copy_x(i * 2 + k, k)
                    if k or not isinstance(i, int):
                        finish(i * 2 + (k - 1), 1 - k, i if k else i - 1)
            peeled(act, NB // 2, step)
            finish(NB - 1, 1, NB // 2 - 1)

        @block.sync
        def _(sp):
            with sp.Fori(0, NB // 2) as i:
                for k in range(2):
                    b = i * 2 + k
                    rows = sp.snap(b * P)
                    if n_dve:
                        sp.wait_ge(dve_out, b + 1)
                    sp.wait_ge(act_out, b + 1)
                    for w in tabled:
                        sp.dma_start(S["targets"][w][bass.ds(rows, P), :], yr[:, k, w, :]).then_inc(stored[k], 16)
            for k in range(2):
                sp.wait_ge(stored[k], NB // 2 * 16 * len(tabled))


def transpose_weights(nc, name, C, pairs):
    n = len(pairs)
    with ExitStack() as ctx:
        sem = stage_semaphores(nc, ctx, name)
        raw = ctx.enter_context(nc.sbuf_tensor(f"{name}_raw", [P, 2, 4, D], F32))
        pt = ctx.enter_context(nc.psum_tensor(f"{name}_pT", [P, 2, 4, P], F32))
        loaded = [sem(f"loaded{k}") for k in range(2)]
        turned, copied = sem("turned"), sem("copied")
        block = ctx.enter_context(nc.Block())

        @block.sync
        def _(sp):
            for m, (w, _) in enumerate(pairs):
                wait(sp, turned, (m - 1) * 4)
                sp.dma_start(raw[:, m % 2, :, :], w.rearrange("(c p) i -> p c i", p=P)).then_inc(loaded[m % 2], 16)
            for k in range(min(n, 2)):
                sp.wait_ge(loaded[k], (n + 1 - k) // 2 * 16)

        @block.tensor
        def _(pe):
            for m in range(n):
                pe.wait_ge(loaded[m % 2], (m // 2 + 1) * 16)
                for ic in range(4):
                    g = m * 4 + ic
                    wait(pe, copied, g - 1)
                    for oc in range(4):
                        ins = nc.tensor.transpose(pt[:, g % 2, oc, :], raw[:, m % 2, oc, ic * P:(ic + 1) * P],
                                                  C.f("ident"))
                    ins.then_inc(turned, 1)

        @block.scalar
        def _(act):
            for m, (_, out) in enumerate(pairs):
                for ic in range(4):
                    g = m * 4 + ic
                    act.wait_ge(turned, g + 1)
                    nc.scalar.copy(out[:, ic, :], pt[:, g % 2, :, :].rearrange("p o n -> p (o n)")).then_inc(copied, 1)


BASES, REL = 30, 2
BCH = 4
BW = 4096
BN = D * D // BCH // BW


def contract_basis(nc, name, basis, att, wtab):
    K = BCH * BASES
    with ExitStack() as ctx:
        sb = lambda n, s, d: ctx.enter_context(nc.sbuf_tensor(f"{name}_{n}", s, d))
        sem = stage_semaphores(nc, ctx, name)
        mix = sb("mix", [K, 32], F32)
        piece = sb("piece", [K, 2, BW], F32)
        wout = sb("wout", [P, 2, 2, D], F32)
        ps = ctx.enter_context(nc.psum_tensor(f"{name}_ps", [P, 4, D], F32))
        zeroed, mixed = sem("zeroed"), sem("mixed")
        loaded = [sem(f"loaded{k}") for k in range(2)]
        stored = [sem(f"stored{k}") for k in range(2)]
        used, moved = sem("used"), sem("moved")
        src = basis.rearrange("b i o -> b (i o)").rearrange("b (c f) -> c b f", c=BCH)
        dst = wtab.rearrange("(r c) f -> (r c) f", c=BCH)
        block = ctx.enter_context(nc.Block())

        @block.sync
        def _(sp):
            sp.wait_ge(zeroed, 1)
            with nc.allow_non_contiguous_dma("60 attention weights, once"):
                for c in range(BCH):
                    for r in range(REL):
                        sp.dma_start(mix[c * BASES:(c + 1) * BASES, r * BCH + c:r * BCH + c + 1],
                                     att[r:r + 1, :].rearrange("r b -> b r")).then_inc(mixed, 16)

            def step(i):
                for k in range(2):
                    wait(sp, used, (i * 2 + (k - 1)) * 2)
                    for c in range(BCH):
                        sp.dma_start(piece[c * BASES:(c + 1) * BASES, k, :],
                                     src[c, :, bass.ds((i * 2 + k) * BW, BW)]).then_inc(loaded[k], 16)
            peeled(sp, BN // 2, step)

        @block.vector
        def _(v):
            nc.vector.memset(mix[:, :], 0.0).then_inc(zeroed, 1)

        @block.tensor
        def _(pe):
            pe.wait_ge(mixed, 16 * BCH * REL)

            def step(i):
                for k in range(2):
                    pe.wait_ge(loaded[k], (i + 1) * (16 * BCH))
                    for s in range(2):
                        n = i * 4 + (k * 2 + s)
                        wait(pe, moved, n - 3)
                        for q in range(4):
                            f = (s * 4 + q) * D
                            ins = nc.tensor.matmul(ps[32 * q:32 * q + 32, k * 2 + s, :], mix[:, :],
                                                   piece[:, k, f:f + D], start=True, stop=True,
                                                   skip_group_check=True)
                        ins.then_inc(used, 1)
            peeled(pe, BN // 2, step)

        @block.scalar
        def _(act):
            def step(i):
                for k in range(2):
                    wait(act, stored[k], i * 64)
                    for s in range(2):
                        act.wait_ge(used, i * 4 + (k * 2 + s + 1))
                        nc.scalar.copy(wout[:, k, s, :], ps[:, k * 2 + s, :]).then_inc(moved, 1)
                    act.wait_ge(moved, i * 4 + (k * 2 + 2))
                    for q in range(4):
                        act.dma_start(
                            dst[:, bass.ds((i * 2 + k) * BW, BW)].rearrange("r (s f) -> r s f", s=2)[:, :, q * D:(q + 1) * D],
                            wout[32 * q:32 * q + REL * BCH, k, :, :]).then_inc(stored[k], 16)
            peeled(act, BN // 2, step)
            for k in range(2):
                act.wait_ge(stored[k], BN // 2 * 64)


def attention_weights(nc, name, C, table, es_t, ed_t, emb, exd):
    with ExitStack() as ctx:
        sb = lambda n, s, d: ctx.enter_context(nc.sbuf_tensor(f"{name}_{n}", s, d))
        recs = sb("recs", [P, SLOTS, RC], F32)
        before = sb("before", [P, RC], F32)
        es, ed = sb("es", [P, SLOTS, H], F32), sb("ed", [P, SLOTS, H], F32)
        idx = sb("idx", [P, 2, SLOTS], I32)
        embv = sb("emb", [P, 8, H], F32)
        fac = sb("factor", [P, H, SLOTS], F32)
        e = sb("e", [P, H, SLOTS], F32)
        t1, t2 = sb("t1", [P, H, SLOTS], F32), sb("t2", [P, H, SLOTS], F32)
        same = sb("same", [P, H, SLOTS], F32)
        same_n = sb("same_next", [P, H, SLOTS], F32)
        key = sb("key", [P, SLOTS], F32)
        mask = sb("mask", [P, SLOTS], F32)
        cols = sb("cols", [P, 4, H], F32)
        row = sb("row", [H, 4, P + 2], F32)
        outr = sb("outr", [H, 2, P + 2], F32)
        carry = sb("carry", [H, 2, P], F32)
        pr = ctx.enter_context(nc.psum_tensor(f"{name}_pr", [H, 4, P], F32))
        pc = ctx.enter_context(nc.psum_tensor(f"{name}_pc", [P, 2, H], F32))
        sem = stage_semaphores(nc, ctx, name)
        idxr = sb("idx_ring", [P, 2, 2, 8], I32)
        gr = sb("gather_ring", [P, 2, 2, 8, H], F32)
        loaded, set_before, s_dve, idx_ready = sem("loaded"), sem("set_before"), sem("dve_chain"), sem("idx_ready")
        idx_copied, landed, out_copied = sem("idx_copied"), [sem(f"landed{k}") for k in range(2)], sem("out_copied")
        sent = sem("sent")
        turned, exd_ready, s_out, exp_in, exp_out, cols_ready = (
            sem("turned"), sem("exd_ready"), sem("s_out"), sem("exp_in"), sem("exp_out"), sem("cols_ready"))
        block = ctx.enter_context(nc.Block())

        @block.sync
        def _(sp):
            sp.dma_start(flat(recs[:, :, :]), table.rearrange("(p s) c -> p (s c)", p=P)).then_inc(loaded, 16)
            sp.dma_start(flat(embv[:, :, :]), emb.rearrange("t h -> (t h)").partition_broadcast(P)).then_inc(loaded, 16)
            sp.wait_ge(set_before, 1)
            sp.dma_start(before[1:P, :], table.rearrange("(p s) c -> p s c", p=P)[0:P - 1, SLOTS - 1, :]
                         ).then_inc(loaded, 16)
            sp.wait_ge(loaded, 48)
            sp.wait_ge(exd_ready, 1)
            sp.dma_start(exd.rearrange("(p s) h -> p (s h)", p=P), flat(es[:, :, :])).then_inc(s_out, 16)
            sp.wait_ge(s_out, 16)

        @block.gpsimd
        def _(pool):
            pool.wait_ge(idx_ready, 1)

            def step(i):
                for half in range(2):
                    wait(pool, landed[half], i * (16 * 16))
                    nc.gpsimd.tensor_copy(idxr[:, half, :, :], idx[:, :, bass.ds(i * 16 + half * 8, 8)]
                                          ).then_inc(idx_copied, 1)
                    wait(pool, out_copied, i * 4 + (half * 2))
                    pool.wait_ge(idx_copied, i * 2 + (half + 1))
                    pool.sem_inc(sent, 1)
                    for s in range(8):
                        for t, tab in enumerate((es_t, ed_t)):
                            pool.indirect_dma_start(
                                gr[:, half, t, s, :], None, tab,
                                bass.IndirectOffsetOnAxis(idxr[:, half, t, s:s + 1], 0)).then_inc(landed[half], 16)
            peeled(pool, SLOTS // 16, step)

        @block.scalar
        def _(act):
            def step(i):
                for half in range(2):
                    act.wait_ge(landed[half], (i + 1) * 256)
                    for t, o in enumerate((es, ed)):
                        nc.scalar.copy(o[:, bass.ds(i * 16 + half * 8, 8), :], gr[:, half, t, :, :]).then_inc(out_copied, 1)
            peeled(act, SLOTS // 16, step)
            act.wait_ge(exp_in, 1)
            nc.scalar.activation(es[:, :, :].rearrange("p s h -> p h s"), e[:, :, :], ACT.Exp).then_inc(exd_ready, 1)

        @block.vector
        def _(v):
            link = chain(v, s_dve)
            nc.vector.memset(before[:, :], -2.0).then_inc(set_before, 1)
            v.wait_ge(loaded, 48)
            link(nc.vector.tensor_copy(idx[:, 0, :], recs[:, :, COL1]))
            nc.vector.tensor_copy(idx[:, 1, :], recs[:, :, COL2]).then_inc(idx_ready, 1)
            link(nc.vector.tensor_scalar(flat(embv[:, :, :]), flat(embv[:, :, :]), 1.0, None, ALU.add))
            link(nc.vector.memset(flat(fac[:, :, :]), 0.0))
            for t in range(8):
                link(nc.vector.tensor_scalar(mask[:, :], recs[:, :, COL3], float(t), None, ALU.is_equal))
                link(nc.vector.tensor_tensor(t1[:, :, :], mask[:, :].unsqueeze(1).to_broadcast([P, H, SLOTS]),
                                             embv[:, t, :].unsqueeze(2).to_broadcast([P, H, SLOTS]), ALU.mult))
                link(nc.vector.tensor_tensor(fac[:, :, :], fac[:, :, :], t1[:, :, :], ALU.add))
            link(nc.vector.scalar_tensor_tensor(key[:, :], recs[:, :, COL2], 256.0, recs[:, :, LOC], ALU.mult, ALU.add))
            link(nc.vector.scalar_tensor_tensor(before[:, 0:1], before[:, COL2:COL2 + 1], 256.0, before[:, LOC:LOC + 1],
                                                ALU.mult, ALU.add))
            link(nc.vector.memset(mask[:, 0:1], 0.0))
            link(nc.vector.tensor_tensor(mask[:, 1:SLOTS], key[:, 1:SLOTS], key[:, 0:SLOTS - 1], ALU.is_equal))
            link(nc.vector.tensor_copy(same[:, :, :], mask[:, :].unsqueeze(1).to_broadcast([P, H, SLOTS])))
            link(nc.vector.memset(same_n[:, :, SLOTS - 1:SLOTS], 0.0))
            link(nc.vector.tensor_copy(same_n[:, :, 0:SLOTS - 1], same[:, :, 1:SLOTS]))
            link(nc.vector.tensor_tensor(before[:, 1:2], key[:, 0:1], before[:, 0:1], ALU.is_equal))
            link(nc.vector.tensor_reduce(before[:, 2:3], mask[:, 1:SLOTS], AX.X, ALU.min))
            link(nc.vector.tensor_copy(cols[:, 2, :], before[:, 2:3].to_broadcast([P, H])))
            link(nc.vector.tensor_copy(cols[:, 3, :], before[:, 1:2].to_broadcast([P, H])))
            link(nc.vector.memset(row[:, :, :], 0.0))
            link(nc.vector.memset(outr[:, :, :], 0.0))
            v.wait_ge(out_copied, SLOTS // 4)
            hs = lambda a: a[:, :, :].rearrange("p s h -> p h s")
            link(nc.vector.tensor_tensor(t1[:, :, :], hs(es), hs(ed), ALU.add))
            link(nc.vector.scalar_tensor_tensor(t2[:, :, :], t1[:, :, :], 0.2, t1[:, :, :], ALU.mult, ALU.max))
            link(nc.vector.tensor_tensor(t2[:, :, :], t2[:, :, :], fac[:, :, :], ALU.mult))
            link(nc.vector.tensor_tensor(e[:, :, :], t2[:, :, :],
                                         recs[:, :, COL4].unsqueeze(1).to_broadcast([P, H, SLOTS]), ALU.mult))
            def forward(src, out):
                link(nc.vector.tensor_tensor_scan(flat(out[:, :, :]), flat(same[:, :, :]), flat(src[:, :, :]), 0.0,
                                                  ALU.mult, ALU.max))

            def backward(src, out):
                link(nc.vector.tensor_tensor_scan(flat(out[:, :, :])[:, ::-1], flat(same_n[:, :, :])[:, ::-1],
                                                  flat(src[:, :, :])[:, ::-1], 0.0, ALU.mult, ALU.max))

            forward(e, t1)
            backward(e, t2)
            link(nc.vector.tensor_copy(cols[:, 0, :], t1[:, :, SLOTS - 1]))
            nc.vector.tensor_copy(cols[:, 1, :], t2[:, :, 0]).then_inc(cols_ready, 1)
            v.wait_ge(turned, 1)
            link(nc.vector.tensor_copy(row[:, :, 1:P + 1], pr[:, :, :]))
            tail, head, one, cont = (row[:, n, :] for n in range(4))
            link(nc.vector.tensor_tensor(carry[:, 0, :], one[:, 1:P + 1], cont[:, 1:P + 1], ALU.mult))
            link(nc.vector.tensor_tensor(carry[:, 1, :], one[:, 1:P + 1], cont[:, 2:P + 2], ALU.mult))
            link(nc.vector.tensor_tensor_scan(outr[:, 0, 1:P + 1], carry[:, 0, :], tail[:, 1:P + 1], 0.0,
                                              ALU.mult, ALU.max))
            link(nc.vector.tensor_tensor_scan(outr[:, 1, 1:P + 1][:, ::-1], carry[:, 1, :][:, ::-1],
                                              head[:, 1:P + 1][:, ::-1], 0.0, ALU.mult, ALU.max))
            link(nc.vector.tensor_tensor(carry[:, 0, :], cont[:, 1:P + 1], outr[:, 0, 0:P], ALU.mult))
            nc.vector.tensor_tensor(carry[:, 1, :], cont[:, 2:P + 2], outr[:, 1, 2:P + 2], ALU.mult
                                    ).then_inc(cols_ready, 1)
            link(nc.vector.tensor_copy(fac[:, :, :], e[:, :, :]))
            v.wait_ge(turned, 2)
            link(nc.vector.tensor_tensor(fac[:, :, 0], fac[:, :, 0], pc[:, 0, :], ALU.max))
            link(nc.vector.tensor_tensor(fac[:, :, SLOTS - 1], fac[:, :, SLOTS - 1], pc[:, 1, :], ALU.max))
            forward(fac, t1)
            backward(t1, t2)
            nc.vector.tensor_tensor(e[:, :, :], e[:, :, :], t2[:, :, :], ALU.subtract).then_inc(exp_in, 1)

        @block.tensor
        def _(pe):
            pe.wait_ge(cols_ready, 1)
            for n in range(4):
                ins = nc.tensor.transpose(pr[:, n, :], cols[:, n, :], C.f("ident"))
            ins.then_inc(turned, 1)
            pe.wait_ge(cols_ready, 2)
            for n in range(2):
                ins = nc.tensor.transpose(pc[:, n, :], carry[:, n, :], C.f("ident", H)[:, 0:H])
            ins.then_inc(turned, 1)


def gnn(nc, ins, consts, out):
    dram = lambda n, s: nc.dram_tensor(n, s, F32, kind="Internal").ap()
    tab = {n: dram(f"tab_{n}", s) for n, s in {
        "src": [ROWS, RC], "dst": [ROWS, RC], "p": [NP, D], "q": [NP, D], "h": [NP, D],
        "es": [NP, H], "ed": [NP, H], "ex": [ROWS, H], "n": [NP, D], "y": [REL * NP, D],
        "w1": [REL * BCH, D * D // BCH], "w2": [REL * BCH, D * D // BCH]}.items()}
    VECS = ["L0_gnn_b", "L1_gnn_ln_gamma", "L1_gnn_ln_beta", "L2_gnn_bias", "L2_gnn_gamma", "L2_gnn_beta",
            "L3_gnn_bias1", "L3_gnn_bias2", "L1_gnn_a_src", "L1_gnn_a_dst"]
    with ExitStack() as top:
        keep = lambda n, s, d: top.enter_context(nc.sbuf_tensor(n, s, d))
        C = Const(keep("const_table", [P, CONSTS.shape[1]], F32), None)
        identb = keep("identb", [P, P], BF16)
        pairs = {k: keep(f"pair_block_{k}", [1, PAIRS], I32) for k in ("src", "dst")}
        loc = {k: keep(f"loc_{k}", [P, SLOTS], F32) for k in ("src", "dst")}
        idx = {k: keep(f"idx_{k}", [P, SLOTS], I32) for k in ("p", "q", "rel", "h")}

        with ExitStack() as ctx:
            sb = lambda n, s, d: ctx.enter_context(nc.sbuf_tensor(n, s, d))
            raw = sb("edge_ints", [EP, 4, T], I32)
            fld = sb("edge_fields", [EP, 6, T], F32)
            rec = {k: sb(f"rec_{k}", [EP, T, RC], F32) for k in ("src", "dst")}
            fill = sb("fill", [P, SLOTS * RC], F32)
            SRC, DST, T2, T8, WT, RELROW = range(6)
            with ExitStack() as c1:
                sem = stage_semaphores(nc, c1, "load")
                const_in, edges_in, s_dve = sem("const_in"), sem("edges_in"), sem("load_chain")
                block = c1.enter_context(nc.Block())

                @block.sync
                def _(sp):
                    for n, k in enumerate(("src", "dst", "edge_type_2", "edge_type_8")):
                        sp.dma_start(raw[:, n, :], ins[k].rearrange("(p t) -> p t", t=T)).then_inc(edges_in, 16)
                    sp.dma_start(fld[:, WT, :], ins["edge_weight"].rearrange("(p t) -> p t", t=T)).then_inc(edges_in, 16)
                    sp.dma_start(C.t[:, :], consts).then_inc(const_in, 16)
                    sp.wait_ge(edges_in, 80)
                    sp.wait_ge(const_in, 16)

                @block.vector
                def _(v):
                    link = chain(v, s_dve)
                    link(nc.vector.memset(fill[:, :], 0.0))
                    link(nc.vector.memset(fill[:, :].rearrange("p (s c) -> p s c", c=RC)[:, :, LOC], -1.0))
                    for k in rec:
                        link(nc.vector.memset(rec[k][:, :, :], 0.0))
                    v.wait_ge(edges_in, 80)
                    link(nc.vector.tensor_copy(fld[:, 0:4, :], raw[:, :, :]))
                    link(nc.vector.tensor_scalar(fld[:, RELROW, :], fld[:, T2, :], 0.0, float(NP),
                                                 ALU.not_equal, ALU.mult))
                    link(nc.vector.tensor_tensor(fld[:, RELROW, :], fld[:, RELROW, :], fld[:, DST, :], ALU.add))
                    v.wait_ge(const_in, 16)
                    link(nc.vector.tensor_copy(identb[:, :], C.f("ident")))
            f = lambda n: fld[:, n, :]
            rank_edges(nc, "src", C, identb, f(SRC), [(COL1, f(SRC)), (COL2, f(DST)), (COL3, f(RELROW))],
                       rec["src"], pairs["src"][:, :], True)
            write_records(nc, "src", rec["src"], tab["src"], fill)
            rank_edges(nc, "dst", C, identb, f(DST), [(COL1, f(SRC)), (COL2, f(DST)), (COL3, f(T8)), (COL4, f(WT))],
                       rec["dst"], pairs["dst"][:, :], False)
            write_records(nc, "dst", rec["dst"], tab["dst"], fill)

        X, acc, held = (keep(n, [P, NB, D], F32) for n in ("x", "acc", "held"))
        vec = keep("vectors", [P, len(VECS), D], F32)
        V = {n: vec[:, k, :] for k, n in enumerate(VECS)}
        W = [keep(f"weights{n}", [P, 4, D], F32) for n in range(3)]
        gate_w = keep("gate_w", [P, 2, 4, REL], F32)
        S = {"bn": keep("bn", [P, NB, 6], F32), "mv": keep("mv", [P, NB, 2], F32), "var": keep("var", [P, NB], F32),
             "sd": keep("sd", [P, NB], F32), "rstd": keep("rstd", [P, NB], F32)}
        side = keep("side", [P, NB, H], F32)
        count = keep("count", [P, NB, 1], F32)
        est, edt = keep("e_src", [P, NB, H], F32), keep("e_dst", [P, NB, H], F32)
        wt = keep("edge_weights", [P, SLOTS, H], F32)

        with ExitStack() as ctx:
            sem = stage_semaphores(nc, ctx, "load")
            recs = ctx.enter_context(nc.sbuf_tensor("recs_in", [P, 2, SLOTS, RC], F32))
            recs_in, vecs_in, x_in, x_zero, s_dve = sem("recs_in"), sem("vecs_in"), sem("x_in"), sem("x_zero"), sem("in_chain")
            block = ctx.enter_context(nc.Block())

            @block.sync
            def _(sp):
                sp.dma_start(flat(recs[:, 0, :, :]), tab["src"].rearrange("(p s) c -> p (s c)", p=P)).then_inc(recs_in, 16)
                with nc.allow_non_contiguous_dma("records of 32 bytes"):
                    sp.dma_start(recs[:, 1, :, :], tab["dst"].rearrange("(s p) c -> p s c", p=P)).then_inc(recs_in, 16)
                for k, n in enumerate(VECS):
                    a = ins[n]
                    if len(a.shape) == 2:
                        a = a.rearrange("a b -> (a b)")
                    sp.dma_start(vec[:, k, :], a.partition_broadcast(P)).then_inc(vecs_in, 16)
                with nc.allow_non_contiguous_dma("gate weights, once"):
                    for l in range(2):
                        for r in range(REL):
                            sp.dma_start(gate_w[:, l, :, r],
                                         ins[f"L3_gnn_gate_w{l + 1}"][r, :, :].rearrange("(c p) a -> p (c a)", p=P)
                                         ).then_inc(vecs_in, 16)
                full = N // P
                sp.dma_start(X[:, 0:full, :], ins["x"][0:full * P, :].rearrange("(b p) d -> p b d", p=P)).then_inc(x_in, 16)
                sp.wait_ge(x_zero, 1)
                sp.dma_start(X[0:N - full * P, full, :], ins["x"][full * P:N, :]).then_inc(x_in, 16)
                sp.wait_ge(x_in, 32)
                sp.wait_ge(vecs_in, 16 * (len(VECS) + 4))

            @block.vector
            def _(v):
                link = chain(v, s_dve)
                nc.vector.memset(X[:, NB - 1, :], 0.0).then_inc(x_zero, 1)
                v.wait_ge(recs_in, 32)
                for m, k in enumerate(("src", "dst")):
                    link(nc.vector.tensor_copy(loc[k][:, :], recs[:, m, :, LOC]))
                for k, m, col in (("p", 0, COL1), ("q", 0, COL2), ("rel", 0, COL3), ("h", 1, COL1)):
                    link(nc.vector.tensor_copy(idx[k][:, :], recs[:, m, :, col]))

        W0 = ins["L0_gnn_W"]
        transpose_weights(nc, "w0", C, [(W0[:, 0:D], W[0]), (W0[:, D:2 * D], W[1])])
        S["targets"] = [tab["p"], tab["q"]]
        node_stage(nc, "n0", C, X, acc, S, None, 0,
                   [(W[0], "bias_table", (V["L0_gnn_b"], None)), (W[1], "table", None)], None, False)
        edge_pass(nc, "e0", C, [tab["p"], tab["q"]], [idx["p"], idx["q"]], loc["src"], pairs["src"], acc, "relu_sum")

        def pre1(link, v, s_var, s_sd):
            link(nc.vector.tensor_tensor(acc[:, :, :], acc[:, :, :], X[:, :, :], ALU.add))
            layer_stats(link, nc, v, s_sd, s_var, acc, S, 1)

        transpose_weights(nc, "w1", C, [(ins["L1_gnn_W"], W[0])])
        S["targets"] = [tab["h"]]
        node_stage(nc, "n1", C, X, acc, S, pre1, 1,
                   [(W[0], "attend", ((V["L1_gnn_a_src"], est), (V["L1_gnn_a_dst"], edt)))], acc, True)
        with ExitStack() as ctx:
            s_e = stage_semaphores(nc, ctx, "move")("scores_out")
            block = ctx.enter_context(nc.Block())

            @block.sync
            def _(sp):
                with nc.allow_non_contiguous_dma("scores of 32 bytes"):
                    sp.dma_start(tab["es"].rearrange("(b p) h -> p b h", p=P), est[:, :, :]).then_inc(s_e, 16)
                    sp.dma_start(tab["ed"].rearrange("(b p) h -> p b h", p=P), edt[:, :, :]).then_inc(s_e, 16)
                sp.wait_ge(s_e, 32)
        attention_weights(nc, "att", C, tab["dst"], tab["es"], tab["ed"], ins["L1_gnn_et_emb"], tab["ex"])
        with ExitStack() as ctx:
            s_w = stage_semaphores(nc, ctx, "move")("weights_in")
            block = ctx.enter_context(nc.Block())

            @block.sync
            def _(sp):
                with nc.allow_non_contiguous_dma("edge weights of 32 bytes"):
                    sp.dma_start(wt[:, :, :], tab["ex"].rearrange("(s p) h -> p s h", p=P)).then_inc(s_w, 16)
                sp.wait_ge(s_w, 16)
        edge_pass(nc, "e1", C, [tab["h"]], [idx["h"]], loc["dst"], pairs["dst"], acc, "weighted", wt, side)

        def bc(a):
            return a.unsqueeze(1).to_broadcast([P, NB, D])

        def affine_add(link, gamma, beta):
            for b in range(NB):
                link(nc.vector.tensor_scalar(acc[:, b, :], acc[:, b, :], S["mv"][:, b, 0:1], S["rstd"][:, b:b + 1],
                                             ALU.subtract, ALU.mult))
            link(nc.vector.tensor_tensor(acc[:, :, :], acc[:, :, :], bc(gamma), ALU.mult))
            link(nc.vector.tensor_tensor(acc[:, :, :], acc[:, :, :], bc(beta), ALU.add))
            link(nc.vector.tensor_tensor(acc[:, :, :], acc[:, :, :], X[:, :, :], ALU.add))

        def pre2(link, v, s_var, s_sd):
            link(nc.vector.tensor_scalar(side[:, :, :], side[:, :, :], 1e-10, None, ALU.add))
            link(nc.vector.reciprocal(side[:, :, :], side[:, :, :]))
            ah = acc[:, :, :].rearrange("p b (h d) -> p (b h) d", h=H)
            link(nc.vector.tensor_tensor(ah, ah, flat(side[:, :, :]).unsqueeze(2).to_broadcast([P, NB * H, DH]), ALU.mult))
            link(nc.vector.tensor_tensor(acc[:, :, :], acc[:, :, :], X[:, :, :], ALU.add))
            layer_stats(link, nc, v, s_sd, s_var, acc, S, 1)
            affine_add(link, V["L1_gnn_ln_gamma"], V["L1_gnn_ln_beta"])
            layer_stats(link, nc, v, s_sd, s_var, acc, S, 2)

        transpose_weights(nc, "w2", C, [(ins["L2_gnn_W_neigh"], W[0]), (ins["L2_gnn_W_self"], W[1])])
        S["targets"] = [tab["n"], None]
        node_stage(nc, "n2", C, X, acc, S, pre2, 2,
                   [(W[0], "table", None), (W[1], "bias_keep", (V["L2_gnn_bias"], held))], acc, True)
        edge_pass(nc, "e2", C, [tab["n"]], [idx["h"]], loc["dst"], pairs["dst"], acc, "counted", None, count)

        def pre3(link, v, s_var, s_sd):
            link(nc.vector.tensor_scalar(count[:, :, :], count[:, :, :], 1.0, None, ALU.max))
            link(nc.vector.reciprocal(count[:, :, :], count[:, :, :]))
            link(nc.vector.tensor_tensor(acc[:, :, :], acc[:, :, :], count[:, :, :].to_broadcast([P, NB, D]), ALU.mult))
            link(nc.vector.tensor_tensor(acc[:, :, :], acc[:, :, :], held[:, :, :], ALU.add))
            layer_stats(link, nc, v, s_sd, s_var, acc, S, 1)
            affine_add(link, V["L2_gnn_gamma"], V["L2_gnn_beta"])
            layer_stats(link, nc, v, s_sd, s_var, acc, S, 2)

        def pre4(link, v, s_var, s_sd):
            link(nc.vector.tensor_tensor(acc[:, :, :], acc[:, :, :], held[:, :, :], ALU.add))
            link(nc.vector.tensor_scalar(acc[:, :, :], acc[:, :, :], 0.0, None, ALU.max))

        for l in range(2):
            wt_dram = tab[f"w{l + 1}"]
            contract_basis(nc, f"basis{l}", ins[f"L3_gnn_basis{l + 1}"], ins[f"L3_gnn_att{l + 1}"], wt_dram)
            with ExitStack() as ctx:
                s_w = stage_semaphores(nc, ctx, "move")(f"rel_weights_in{l}")
                block = ctx.enter_context(nc.Block())

                @block.sync
                def _(sp):
                    for r in range(REL):
                        sp.dma_start(W[r][:, :, :], wt_dram[r * BCH:(r + 1) * BCH, :].rearrange(
                            "c (p o) -> p c o", o=D)).then_inc(s_w, 16)
                    sp.dma_start(W[2][:, :, :], ins[f"L3_gnn_root{l + 1}"].rearrange("(c p) o -> p c o", p=P)
                                 ).then_inc(s_w, 16)
                    sp.wait_ge(s_w, 48)
            S["targets"] = [tab["y"][0:NP, :], tab["y"][NP:REL * NP, :], None]
            node_stage(nc, f"n{3 + l}", C, X if l == 0 else acc, acc, S, pre4 if l else pre3, 0 if l else 2,
                       [(W[0], "gated", 0), (W[1], "gated", 1), (W[2], "bias_keep", (V[f"L3_gnn_bias{l + 1}"], held))],
                       None if l else acc, l == 0, gate=gate_w[:, l, :, :])
            edge_pass(nc, f"e{3 + l}", C, [tab["y"]], [idx["rel"]], loc["src"], pairs["src"], acc, "plain")

        with ExitStack() as ctx:
            sem = stage_semaphores(nc, ctx, "load")
            s_dve, s_var, s_sd, final, s_out = (sem(f"last_{n}") for n in ("chain", "var", "sd", "final", "out"))
            block = ctx.enter_context(nc.Block())

            @block.vector
            def _(v):
                link = chain(v, s_dve)
                link(nc.vector.tensor_tensor(acc[:, :, :], acc[:, :, :], held[:, :, :], ALU.add))
                link(nc.vector.tensor_tensor(acc[:, :, :], acc[:, :, :], X[:, :, :], ALU.add))
                layer_stats(link, nc, v, s_sd, s_var, acc, S, 1)
                for b in range(NB):
                    nc.vector.tensor_scalar(acc[:, b, :], acc[:, b, :], S["mv"][:, b, 0:1], S["rstd"][:, b:b + 1],
                                            ALU.subtract, ALU.mult).then_inc(final, 1)

            @block.scalar
            def _(act):
                act.wait_ge(s_var, 1)
                nc.scalar.activation(S["sd"][:, :], S["var"][:, :], ACT.Sqrt).then_inc(s_sd, 1)

            @block.sync
            def _(sp):
                full = N // P
                sp.wait_ge(final, NB)
                sp.dma_start(out[0:full * P, :].rearrange("(b p) d -> p b d", p=P), acc[:, 0:full, :]).then_inc(s_out, 16)
                sp.dma_start(out[full * P:N, :], acc[0:N - full * P, full, :]).then_inc(s_out, 16)
                sp.wait_ge(s_out, 32)


_INS = ["x", "src", "dst", "edge_type_2", "edge_type_8", "edge_weight", "L0_gnn_W", "L0_gnn_b", "L1_gnn_W",
        "L1_gnn_a_src", "L1_gnn_a_dst", "L1_gnn_et_emb", "L1_gnn_ln_gamma", "L1_gnn_ln_beta", "L2_gnn_W_self",
        "L2_gnn_W_neigh", "L2_gnn_bias", "L2_gnn_gamma", "L2_gnn_beta", "L3_gnn_basis1", "L3_gnn_att1",
        "L3_gnn_gate_w1", "L3_gnn_root1", "L3_gnn_bias1", "L3_gnn_basis2", "L3_gnn_att2", "L3_gnn_gate_w2",
        "L3_gnn_root2", "L3_gnn_bias2"]


def kernel(**inputs):
    import numpy as _np
    import concourse.bacc as _bacc
    from concourse import mybir as _mybir
    from concourse.bass_utils import run_bass_kernel_spmd as _run

    nc = _bacc.Bacc("TRN2", target_bir_lowering=False, num_devices=1)
    arrays, aps = {"constants": CONSTS}, {}
    consts = nc.dram_tensor("constants", CONSTS.shape, _mybir.dt.float32, kind="ExternalInput").ap()
    for name in _INS:
        a = _np.ascontiguousarray(inputs[name])
        arrays[f"in_{name}"] = a
        aps[name] = nc.dram_tensor(f"in_{name}", a.shape, _mybir.dt.from_np(a.dtype), kind="ExternalInput").ap()
    out = nc.dram_tensor("out", (N, D), _mybir.dt.float32, kind="ExternalOutput").ap()
    gnn(nc, aps, consts, out)
    r = _run(nc, [arrays], core_ids=[0])
    return r.results[0]["out"]
```

```python
import concourse.bass as bass
from concourse import mybir
from contextlib import ExitStack
import numpy as np

F32, BF16, I32 = mybir.dt.float32, mybir.dt.bfloat16, mybir.dt.int32
ALU, ACT, AX = mybir.AluOpType, mybir.ActivationFunctionType, mybir.AxisListType

P = 128
N, E, D = 1250, 20000, 512
NB = -(-N // P)
NP = NB * P
EP, T = 125, 160
GT = 16
LB = 4
HI, LO = NP >> LB, 1 << LB
KO = HI + LO
PAIRS = E // 256 + NB
SLOTS = 2 * PAIRS
ROWS = SLOTS * P
H, DH = 8, 64


def stage_semaphores(nc, ctx, name):
    taken = []

    def give_back():
        nc.clear_and_free_semaphores(taken)
        nc.all_engine_barrier(sem_only=True)

    ctx.callback(give_back)

    def sem(what):
        taken.append(nc.alloc_semaphore(name=f"{name}_{what}_{nc.next_id()}"))
        return taken[-1]

    return sem


def chain(eng, sem):
    count = [0]

    def link(ins):
        count[0] += 1
        ins.then_inc(sem, 1)
        eng.wait_ge(sem, count[0])

    return link


def wait(eng, sem, value):
    if isinstance(value, int) and value <= 0:
        return
    eng.wait_ge(sem, value)


def peeled(eng, n, body, first=1, last=0):
    for i in range(first):
        body(i)
    with eng.Fori(first, n - last) as i:
        body(i)
    for i in range(n - last, n):
        body(i)


def is_first(i):
    return isinstance(i, int) and i == 0


def lagged(eng, steps, width, works, last=0):
    most = max(lag for lag, _ in works)

    def step(i):
        for u in range(width):
            for lag, work in works:
                back = -((u - lag) // width)
                if not (isinstance(i, int) and i < back):
                    work(i - back, u - lag + back * width)

    peeled(eng, steps, step, first=1 + most // width, last=last)
    for n in range(most):
        for lag, work in works:
            if n < lag:
                at = steps * width + n - lag
                work(at // width, at % width)


def constants():
    m = np.arange(HI)
    hb = P // LO
    c = {}
    c["ident"] = np.eye(P)
    e = np.arange(P)
    c["earlier"] = (e[None, :] < e[:, None]) * 1.0
    c["iota_hi"] = np.tile(np.arange(HI), (P, 1))
    c["iota_lo"] = np.tile(np.arange(LO), (P, 1))
    c["iota_p"] = np.tile(np.arange(P), (P, 1))
    c["pair_start"] = np.tile(np.arange(PAIRS) * 256, (P, 1))
    c["iota_slot"] = np.tile(np.arange(SLOTS), (P, 1))

    def on_his(a):
        return np.concatenate([a, np.zeros((P - HI, a.shape[1]))])

    same = m[:, None] // hb == m[None, :] // hb
    c["same_block"] = on_his(same * 1.0)
    c["lower_in_block"] = on_his((same & (m[:, None] < m[None, :])) * 1.0)
    c["first_of_lower_block"] = on_his(((m[:, None] % hb == 0) & (m[:, None] // hb < m[None, :] // hb)) * 1.0)
    c["block_head"] = on_his(np.tile(((m % hb == 0) & (m > 0))[:, None] * 1.0, (1, P)))
    cols, at = [], {}
    n = 0
    for k, v in c.items():
        at[k] = (n, n + v.shape[1])
        n += v.shape[1]
        cols.append(v)
    return np.concatenate(cols, 1).astype(np.float32), at


CONSTS, CAT = constants()


class Const:
    def __init__(self, tile, tileb):
        self.t, self.b = tile, tileb

    def f(self, name, parts=P):
        a, b = CAT[name]
        return self.t[0:parts, a:b]


BASES, REL = 30, 2
BCH = 4
BW = 4096


class Basis:
    PIECES = D * D // BCH // BW
    STEPS = PIECES // 2

    def __init__(self, nc, name, basis, att, wtab):
        self.nc, self.name, self.att = nc, name, att
        self.src = basis.rearrange("b i o -> b (i o)").rearrange("b (c f) -> c b f", c=BCH)
        self.dst = wtab

    def begin(self, ctx, sem):
        nc, K = self.nc, BCH * BASES
        sb = lambda n, s, d: ctx.enter_context(nc.sbuf_tensor(f"{self.name}_{n}", s, d))
        self.mix = sb("mix", [K, 32], F32)
        self.piece = sb("piece", [K, 2, BW], F32)
        self.wout = sb("wout", [P, 2, 2, D], F32)
        self.ps = ctx.enter_context(nc.psum_tensor(f"{self.name}_ps", [P, 4, D], F32))
        self.zeroed, self.mixed = sem("mix_zeroed"), sem("mix_in")
        self.loaded = [sem(f"basis_loaded{k}") for k in range(2)]
        self.stored = [sem(f"basis_stored{k}") for k in range(2)]
        self.used, self.moved = sem("piece_used"), sem("basis_moved")

    def clear_mix(self):
        self.nc.vector.memset(self.mix[:, :], 0.0).then_inc(self.zeroed, 1)

    def load(self, eng):
        eng.wait_ge(self.zeroed, 1)
        with self.nc.allow_non_contiguous_dma("60 attention weights, once"):
            for c in range(BCH):
                for r in range(REL):
                    eng.dma_start(self.mix[c * BASES:(c + 1) * BASES, r * BCH + c:r * BCH + c + 1],
                                  self.att[r:r + 1, :].rearrange("r b -> b r")).then_inc(self.mixed, 16)

        def step(i):
            for k in range(2):
                wait(eng, self.used, (i * 2 + (k - 1)) * 2)
                for c in range(BCH):
                    eng.dma_start(self.piece[c * BASES:(c + 1) * BASES, k, :],
                                  self.src[c, :, bass.ds((i * 2 + k) * BW, BW)]).then_inc(self.loaded[k], 16)
        peeled(eng, self.STEPS, step)

    def start_multiply(self, pe):
        pe.wait_ge(self.mixed, 16 * BCH * REL)

    def multiply(self, pe, i, k):
        pe.wait_ge(self.loaded[k], (i + 1) * (16 * BCH))
        for s in range(2):
            wait(pe, self.moved, i * 4 + (k * 2 + s - 3))
            for q in range(4):
                f = (s * 4 + q) * D
                ins = self.nc.tensor.matmul(self.ps[32 * q:32 * q + 32, k * 2 + s, :], self.mix[:, :],
                                            self.piece[:, k, f:f + D], start=True, stop=True,
                                            skip_group_check=True)
            ins.then_inc(self.used, 1)

    def store(self, act):
        def step(i):
            for k in range(2):
                wait(act, self.stored[k], i * 64)
                for s in range(2):
                    act.wait_ge(self.used, i * 4 + (k * 2 + s + 1))
                    self.nc.scalar.copy(self.wout[:, k, s, :], self.ps[:, k * 2 + s, :]).then_inc(self.moved, 1)
                act.wait_ge(self.moved, i * 4 + (k * 2 + 2))
                for q in range(4):
                    act.dma_start(
                        self.dst[:, bass.ds((i * 2 + k) * BW, BW)].rearrange("r (s f) -> r s f", s=2)[:, :, q * D:(q + 1) * D],
                        self.wout[32 * q:32 * q + REL * BCH, k, :, :]).then_inc(self.stored[k], 16)
        peeled(act, self.STEPS, step)
        for k in range(2):
            act.wait_ge(self.stored[k], self.STEPS * 64)


def sort_edges(nc, name, C, identb, key, packed, extra, pair_block, block_f, sorted_out, basis=None):
    values = [0] if extra is None else [0, 1]
    with ExitStack() as ctx:
        sb = lambda n, s, d: ctx.enter_context(nc.sbuf_tensor(f"{name}_{n}", s, d))
        ki = sb("key_int", [EP, T], I32)
        ti = sb("int_tmp", [EP, T], I32)
        hif = sb("hi_f", [EP, T], F32)
        lof = sb("lo_f", [EP, T], F32)
        onehot = sb("onehot", [EP, T, KO], BF16)
        onehotT = sb("onehotT", [KO, T, EP], BF16)
        cnt = sb("cnt", [HI, LO, T], F32)
        inc = sb("inc", [HI, LO, T], F32)
        pre = sb("prefix_parts", [HI, 2, LO, T], BF16)
        rankin = sb("rank_in_tile", [EP, T], F32)
        rankto = sb("rank_to_tile", [EP, T], F32)
        tmp = sb("gather_tmp", [EP, GT, 2, LO], F32)
        small = sb("small", [HI, 8], F32)
        smalli = sb("small_i", [HI, 2], I32)
        atleast = sb("pair_at_least", [HI, PAIRS], F32)
        eqtmp = sb("eq_tmp", [EP, 4, EP], F32)
        pos_p, pos_s = sb("pos_partition", [EP, T], F32), sb("pos_slot", [EP, T], F32)
        value = sb("packed_value", [EP, T], F32)
        tot = small[:, 0:1]

        with ExitStack() as c1:
            sem = stage_semaphores(nc, c1, name)
            pt = c1.enter_context(nc.psum_tensor(f"{name}_pT", [KO, 2, 8, 128], BF16))
            pc = c1.enter_context(nc.psum_tensor(f"{name}_pC", [HI, GT, LO], F32))
            pe_ = c1.enter_context(nc.psum_tensor(f"{name}_pE", [EP, 4, 4, 128], F32))
            s_dve = sem("dve_chain")
            onehots_ready = sem("onehots_ready")
            transposed, counted, moved = sem("transposed"), sem("counted"), sem("moved")
            compared, ranked = sem("compared"), sem("ranked")
            block = c1.enter_context(nc.Block())

            G = T // GT

            @block.vector
            def _(v):
                link = chain(v, s_dve)
                link(nc.vector.tensor_copy(ki[:, :], key))
                link(nc.vector.tensor_single_scalar(ti[:, :], ki[:, :], LB, ALU.logical_shift_right))
                link(nc.vector.tensor_copy(hif[:, :], ti[:, :]))
                link(nc.vector.tensor_single_scalar(ti[:, :], ki[:, :], LO - 1, ALU.bitwise_and))
                link(nc.vector.tensor_copy(lof[:, :], ti[:, :]))

                def build(g, _):
                    for f, iota, a, n in ((hif, "iota_hi", 0, HI), (lof, "iota_lo", HI, LO)):
                        nc.vector.tensor_tensor(
                            onehot[:, bass.ds(g * GT, GT), a:a + n],
                            C.f(iota, EP).unsqueeze(1).to_broadcast([EP, GT, n]),
                            f[:, bass.ds(g * GT, GT)].unsqueeze(2).to_broadcast([EP, GT, n]), ALU.is_equal,
                        ).then_inc(onehots_ready, 1)

                def rank(g, _):
                    for u in range(GT):
                        if u % 4 == 0:
                            v.wait_ge(compared, g * 4 + (u // 4 + 1))
                        wait(v, ranked, g * GT + (u - 3))
                        nc.vector.scalar_tensor_tensor(
                            eqtmp[:, u % 4, :], pe_[:, u // 4, u % 4, 0:EP], 2.0,
                            C.f("earlier", EP)[:, 0:EP], ALU.is_equal, ALU.mult,
                            accum_out=rankin[:, bass.ds(g * GT + u, 1)]).then_inc(ranked, 1)

                lagged(v, G, 1, [(0, build), (2, rank)])

            @block.tensor
            def _(pe):
                def turn(g, _):
                    pe.wait_ge(onehots_ready, g * 2 + 2)
                    wait(pe, moved, g * 3)
                    for u in range(GT):
                        ins = nc.tensor.transpose(
                            pt[:, u // 8, u % 8, 0:EP],
                            onehot[:, bass.ds(g * GT + u, 1), :].rearrange("p a n -> p (a n)"),
                            identb[0:EP, 0:EP])
                        if u % 8 == 7:
                            ins.then_inc(transposed, 1)
                    for u in range(GT):
                        oh = onehot[:, bass.ds(g * GT + u, 1), :].rearrange("p a n -> p (a n)")
                        ins = nc.tensor.matmul(pc[:, u, :], oh[:, 0:HI], oh[:, HI:KO],
                                               start=True, stop=True)
                    ins.then_inc(counted, 1)

                def compare(g, _):
                    pe.wait_ge(moved, g * 3 + 2)
                    for u in range(GT):
                        if u % 4 == 0:
                            wait(pe, ranked, g * GT + (u + 4 - GT))
                        oh = onehotT[:, bass.ds(g * GT + u, 1), :].rearrange("p a n -> p (a n)")
                        ins = nc.tensor.matmul(pe_[:, u // 4, u % 4, 0:EP], oh, oh, start=True, stop=True)
                        if u % 4 == 3:
                            ins.then_inc(compared, 1)

                lagged(pe, G, 1, [(0, turn), (1, compare)])

            @block.scalar
            def _(act):
                with act.Fori(0, G) as g:
                    for w in range(2):
                        act.wait_ge(transposed, g * 2 + (w + 1))
                        nc.scalar.copy(
                            onehotT[:, bass.ds(g * GT + w * 8, 8), :], pt[:, w, :, 0:EP]).then_inc(moved, 1)
                    act.wait_ge(counted, g + 1)
                    nc.scalar.copy(cnt[:, :, bass.ds(g * GT, GT)].rearrange("p l t -> p t l"),
                                   pc[:, :, :]).then_inc(moved, 1)

        with ExitStack() as c1:
            sem = stage_semaphores(nc, c1, name)
            ps = c1.enter_context(nc.psum_tensor(f"{name}_pS", [HI, 4], F32))
            pp = c1.enter_context(nc.psum_tensor(f"{name}_pP", [P, PAIRS], F32))
            pg = c1.enter_context(nc.psum_tensor(f"{name}_pG", [EP, 2, GT, 2, LO], F32))
            s_dve, summed = sem("dve_chain"), sem("summed")
            tot_ready, pads_ready, prefix_ready, pairs_ready = (
                sem("tot_ready"), sem("pads_ready"), sem("prefix_ready"), sem("pairs_ready"))
            gathered, taken, s_red = sem("gathered"), sem("taken"), sem("reduced")
            block = c1.enter_context(nc.Block())

            @block.vector
            def _(v):
                link = chain(v, s_dve)
                flat = lambda a: a[:, :, :].rearrange("p l t -> p (l t)")
                link(nc.vector.memset(small[:, 1:2], 0.0))
                nc.vector.tensor_tensor_scan(flat(inc), flat(cnt),
                                             small[:, 1:2].to_broadcast([HI, LO * T]), 0.0,
                                             ALU.add, ALU.add).then_inc(tot_ready, 1)
                v.wait_ge(summed, 1)
                link(nc.vector.tensor_scalar(smalli[:, 0:1], ps[:, 0:1], 255.0, None, ALU.add))
                link(nc.vector.tensor_scalar(smalli[:, 1:2], smalli[:, 0:1], 8, 8,
                                             ALU.logical_shift_right, ALU.logical_shift_left))
                nc.vector.tensor_copy(small[:, 2:3], smalli[:, 1:2]).then_inc(pads_ready, 1)
                v.wait_ge(summed, 2)
                link(nc.vector.tensor_copy(small[:, 4:6], ps[:, 1:3]))
                link(nc.vector.tensor_tensor(small[:, 3:4], small[:, 4:5], small[:, 5:6], ALU.add))
                nc.vector.tensor_scalar(atleast[:, :], C.f("pair_start", HI), small[:, 5:6], None,
                                        ALU.is_ge).then_inc(pairs_ready, 1)
                link(nc.vector.scalar_tensor_tensor(flat(inc), flat(inc), small[:, 3:4], flat(cnt),
                                                    ALU.add, ALU.subtract))
                parts = [pre[:, n, :, :].rearrange("p l t -> p (l t)") for n in range(2)]
                link(nc.vector.tensor_copy(parts[0], flat(inc)))
                nc.vector.tensor_tensor(parts[1], flat(inc), parts[0],
                                        ALU.subtract).then_inc(prefix_ready, 1)
                v.wait_ge(summed, 3)
                nc.vector.tensor_copy(pair_block, pp[0:1, :])
                nc.vector.tensor_copy(block_f, pp[:, :])
                with v.Fori(0, T // GT // 2) as g:
                    for w in range(2):
                        v.wait_ge(gathered, g * 2 + (w + 1))
                        nc.vector.tensor_tensor(
                            tmp[:, :, :, :], pg[:, w, :, :, :],
                            onehot[:, bass.ds(g * 2 * GT + w * GT, GT), HI:KO].unsqueeze(2).to_broadcast([EP, GT, 2, LO]),
                            ALU.mult).then_inc(taken, 1)
                        v.wait_ge(taken, g * 2 + (w + 1))
                        nc.vector.tensor_reduce(rankto[:, bass.ds(g * 2 * GT + w * GT, GT)], tmp[:, :, :, :].rearrange("p t n l -> p t (n l)"),
                                                AX.X, ALU.add).then_inc(s_red, 1)
                        v.wait_ge(s_red, g * 2 + (w + 1))
                link(nc.vector.tensor_tensor(ki[:, :], rankto[:, :], rankin[:, :], ALU.add))
                link(nc.vector.tensor_single_scalar(ti[:, :], ki[:, :], P - 1, ALU.bitwise_and))
                link(nc.vector.tensor_copy(pos_p[:, :], ti[:, :]))
                link(nc.vector.tensor_single_scalar(ti[:, :], ki[:, :], 7, ALU.logical_shift_right))
                link(nc.vector.tensor_copy(pos_s[:, :], ti[:, :]))
                link(nc.vector.tensor_copy(ki[:, :], key))
                link(nc.vector.tensor_single_scalar(ti[:, :], ki[:, :], P - 1, ALU.bitwise_and))
                link(nc.vector.tensor_scalar(value[:, :], ti[:, :], 1.0, None, ALU.add))
                for f, factor in packed:
                    link(nc.vector.scalar_tensor_tensor(value[:, :], f, float(factor), value[:, :],
                                                        ALU.mult, ALU.add))

            @block.tensor
            def _(pe):
                pe.wait_ge(tot_ready, 1)
                total = inc[:, LO - 1, T - 1:T]
                nc.tensor.matmul(ps[:, 0:1], C.f("same_block", HI), total, start=True, stop=True
                                 ).then_inc(summed, 1)
                pe.wait_ge(pads_ready, 1)
                nc.tensor.matmul(ps[:, 1:2], C.f("lower_in_block", HI), total, start=True, stop=True)
                nc.tensor.matmul(ps[:, 2:3], C.f("first_of_lower_block", HI), small[:, 2:3],
                                 start=True, stop=True).then_inc(summed, 1)
                pe.wait_ge(pairs_ready, 1)
                nc.tensor.matmul(pp[:, :], C.f("block_head", HI), atleast[:, :], start=True, stop=True
                                 ).then_inc(summed, 1)
                pe.wait_ge(prefix_ready, 1)
                def step(g):
                    for w in range(2):
                        wait(pe, taken, g * 2 + (w - 1))
                        for u in range(GT):
                            t = g * 2 * GT + (w * GT + u)
                            oh = onehotT[0:HI, bass.ds(t, 1), :].rearrange("p a n -> p (a n)")
                            ins = nc.tensor.matmul(
                                pg[:, w, u, :, :].rearrange("p n l -> p (n l)"), oh,
                                pre[:, :, :, bass.ds(t, 1)].rearrange("p n l a -> p (n l a)"), start=True, stop=True)
                        ins.then_inc(gathered, 1)
                peeled(pe, T // GT // 2, step)

        RING, STEP = 4, 8 if basis is None else T // Basis.STEPS
        with ExitStack() as c1:
            sem = stage_semaphores(nc, c1, name)
            onp = c1.enter_context(nc.sbuf_tensor(f"{name}_onehot_p", [EP, RING, P], F32))
            ons = c1.enter_context(nc.sbuf_tensor(f"{name}_onehot_s", [EP, RING, 2, SLOTS], F32))
            po = c1.enter_context(nc.psum_tensor(f"{name}_pO", [P, 2, D], F32))
            built, placed = sem("built"), sem("placed")
            if basis:
                basis.begin(c1, sem)
            block = c1.enter_context(nc.Block())

            if basis:
                @block.sync
                def _(sp):
                    basis.load(sp)

                @block.scalar
                def _(act):
                    basis.store(act)

            @block.vector
            def _(v):
                if basis:
                    basis.clear_mix()
                def step(i):
                    for u in range(STEP):
                        k = u % RING
                        t = i * STEP + u
                        wait(v, placed, i * STEP + (u + 1 - RING))
                        nc.vector.tensor_scalar(onp[:, k, :], C.f("iota_p", EP), pos_p[:, bass.ds(t, 1)], None,
                                                ALU.is_equal)
                        if extra is not None:
                            nc.vector.tensor_scalar(ons[:, k, 1, :], C.f("iota_slot", EP), pos_s[:, bass.ds(t, 1)],
                                                    extra[:, bass.ds(t, 1)], ALU.is_equal, ALU.mult)
                        nc.vector.tensor_scalar(ons[:, k, 0, :], C.f("iota_slot", EP), pos_s[:, bass.ds(t, 1)],
                                                value[:, bass.ds(t, 1)], ALU.is_equal, ALU.mult).then_inc(built, 1)
                peeled(v, T // STEP, step)
                v.wait_ge(placed, T)
                for n in values:
                    nc.vector.tensor_copy(sorted_out[n], po[:, n, 0:SLOTS])

            @block.tensor
            def _(pe):
                def step(i, first=False, last=False):
                    for u in range(STEP):
                        pe.wait_ge(built, i * STEP + (u + 1))
                        for n in values:
                            ins = nc.tensor.matmul(po[:, n, 0:SLOTS], onp[:, u % RING, :], ons[:, u % RING, n, :],
                                                   start=first and u == 0, stop=last and u == STEP - 1)
                        ins.then_inc(placed, 1)
                        if basis and u % (STEP // 2) == STEP // 2 - 1:
                            if first and u < STEP // 2:
                                basis.start_multiply(pe)
                            basis.multiply(pe, i, u // (STEP // 2))
                step(0, first=True)
                with pe.Fori(1, T // STEP - 1) as i:
                    step(i)
                step(T // STEP - 1, last=True)


def flat(ap):
    return ap.rearrange("p a n -> p (a n)")


BODYP = 8
NSTEP = PAIRS // BODYP


def edge_pass(nc, name, C, table, idx, loc, pair_block, acc, weight=None, side=None, own=None, fetch=()):
    ns = H + 1 if weight is not None else 0
    assert NB <= NSTEP - 1
    with ExitStack() as ctx:
        sb = lambda n, s, d: ctx.enter_context(nc.sbuf_tensor(f"{name}_{n}", s, d))
        ps = lambda n, s, d: ctx.enter_context(nc.psum_tensor(f"{name}_{n}", s, d))
        sem = stage_semaphores(nc, ctx, name)
        rows = sb("rows", [P, BODYP, 2, D], F32)
        idxr = sb("idx_ring", [P, 2, 8], I32)
        ohr = sb("onehot_ring", [P, 4, 2, P], F32)
        pS = ps("pS", [P, 2, D], F32)
        pN = ps("pN", [P, 2, D], F32) if ns else None
        pR = ps("pR", [P, D], F32)
        xs = sb("xT_block", [P, 4, P], F32)
        idx_copied, sent = sem("idx_copied"), sem("sent")
        got = [sem(f"got{q}") for q in range(BODYP)]
        zeroed, built, weighted = sem("zeroed"), sem("onehot_built"), sem("weighted")
        summed, added, nadded = sem("summed"), sem("added"), sem("nadded")
        x_copied, multiplied, kept, fetched = sem("x_copied"), sem("own_multiplied"), sem("own_kept"), sem("fetched")
        block = ctx.enter_context(nc.Block())

        def has_block(i):
            return own and not (isinstance(i, int) and i == NSTEP - 1)

        @block.sync
        def _(sp):
            for tile, source in fetch:
                sp.dma_start(tile, source).then_inc(fetched, 16)
            if fetch:
                sp.wait_ge(fetched, 16 * len(fetch))

        @block.gpsimd
        def _(pool):
            def step(i):
                for half in range(2):
                    for q in range(half * 4, half * 4 + 4):
                        wait(pool, got[q], i * 32)
                    nc.gpsimd.tensor_copy(idxr[:, half, :],
                                          idx[:, bass.ds(i * 16 + half * 8, 8)]).then_inc(idx_copied, 1)
                    pool.wait_ge(idx_copied, i * 2 + (half + 1))
                    for q in range(half * 4, half * 4 + 4):
                        wait(pool, summed, i * BODYP + (q + 1 - BODYP))
                        pool.sem_inc(sent, 1)
                        for s in range(2):
                            n = (q % 4) * 2 + s
                            pool.indirect_dma_start(rows[:, q, s, :], None, table,
                                                    bass.IndirectOffsetOnAxis(idxr[:, half, n:n + 1], 0)
                                                    ).then_inc(got[q], 16)
            peeled(pool, NSTEP, step)

        @block.vector
        def _(v):
            nc.vector.memset(acc[:, :, :], 0.0).then_inc(zeroed, 1)
            if ns:
                nc.vector.memset(side[:, :, :], 0.0).then_inc(zeroed, 1)
            v.wait_ge(zeroed, 1 + (ns > 0))

            def build(i, u):
                wait(v, summed, i * BODYP + (u - 3))
                nc.vector.tensor_tensor(
                    ohr[:, u % 4, :, :], C.f("iota_p").unsqueeze(1).to_broadcast([P, 2, P]),
                    loc[:, bass.ds(i * 16 + u * 2, 2)].unsqueeze(2).to_broadcast([P, 2, P]),
                    ALU.is_equal).then_inc(built, 1)

            def multiply(i, u):
                v.wait_ge(got[u], (i + 1) * 32)
                r = rows[:, u, :, :].rearrange("p s (h d) -> p s h d", h=H)
                nc.vector.tensor_tensor(
                    r, r, weight[:, bass.ds(i * 16 + u * 2, 2), 0:H].unsqueeze(3).to_broadcast([P, 2, H, DH]),
                    ALU.mult).then_inc(weighted, 1)

            def accumulate(i, u):
                j = i * BODYP + u
                b = v.value_load(pair_block[0:1, bass.ds(j, 1)], min_val=0, max_val=NB - 1)
                v.wait_ge(summed, j + 1)
                wait(v, added, j)
                a = flat(acc[:, bass.ds(b, 1), :])
                nc.vector.tensor_tensor(a, pS[:, u % 2, :], a, ALU.add).then_inc(added, 1)
                if ns:
                    wait(v, nadded, j)
                    a = flat(side[:, bass.ds(b, 1), :])
                    nc.vector.tensor_tensor(a, pN[:, u % 2, 0:ns], a, ALU.add).then_inc(nadded, 1)

            def keep_own(i, u):
                if u == BODYP - 1 and has_block(i):
                    v.wait_ge(multiplied, i + 1)
                    nc.vector.tensor_tensor(flat(own[3][:, bass.ds(i, 1), :]), pR[:, :], own[2],
                                            ALU.add).then_inc(kept, 1)

            lagged(v, NSTEP, BODYP, [(0, build)] + ([(0, multiply)] if ns else []) + [(1, accumulate), (0, keep_own)],
                   last=1)

        if own:
            @block.scalar
            def _(act):
                def step(i):
                    wait(act, multiplied, i)
                    nc.scalar.copy(xs[:, :, :], own[0][:, bass.ds(i, 1), :, :].rearrange("p a c n -> p (a c) n")
                                   ).then_inc(x_copied, 1)
                peeled(act, NB, step)

        @block.tensor
        def _(pe):
            pe.wait_ge(zeroed, 1 + (ns > 0))

            def scatter(i, u):
                j = i * BODYP + u
                pe.wait_ge(built, j + 1)
                if ns:
                    pe.wait_ge(weighted, j + 1)
                    wait(pe, nadded, j - 1)
                else:
                    pe.wait_ge(got[u], (i + 1) * 32)
                wait(pe, added, j - 1)
                for s in range(2):
                    ins = nc.tensor.matmul(pS[:, u % 2, :], ohr[:, u % 4, s, :], rows[:, u, s, :],
                                           start=s == 0, stop=s == 1)
                    if ns:
                        ins = nc.tensor.matmul(
                            pN[:, u % 2, 0:ns], ohr[:, u % 4, s, :],
                            weight[:, bass.ds(i * 16 + (u * 2 + s), 1), :].rearrange("p a h -> p (a h)"),
                            start=s == 0, stop=s == 1)
                ins.then_inc(summed, 1)

            def multiply_own(i, u):
                if u == BODYP // 2 and has_block(i):
                    pe.wait_ge(x_copied, i + 1)
                    wait(pe, kept, i)
                    for c in range(4):
                        ins = nc.tensor.matmul(pR[:, :], xs[:, c, :], own[1][:, c, :], start=c == 0, stop=c == 3)
                    ins.then_inc(multiplied, 1)

            lagged(pe, NSTEP, BODYP, [(0, multiply_own), (0, scatter)], last=1)


def edge_convolution(nc, name, C, identb, p_parts, q_table, idx, loc, pair_block, acc):
    RING, FR = BODYP, mybir.dt.float32r
    with ExitStack() as ctx:
        sb = lambda n, s, d: ctx.enter_context(nc.sbuf_tensor(f"{name}_{n}", s, d))
        ps = lambda n, s, d: ctx.enter_context(nc.psum_tensor(f"{name}_{n}", s, d))
        sem = stage_semaphores(nc, ctx, name)
        rows = sb("rows", [P, RING, 2, D], F32)
        idxr = sb("idx_ring", [P, 2, 8], I32)
        ohb = sb("onehot_bf16", [P, 4, 2, P], BF16)
        ohf = sb("onehot_f32", [P, RING, 2, P], F32)
        ohT = sb("onehotT", [P, 2, 2, P], FR)
        pT = ps("pT", [P, 2, 8, P], BF16)
        pP = ps("pP", [P, 2, 2, D], F32)
        pS = ps("pS", [P, 2, D], F32)
        idx_copied, sent = sem("idx_copied"), sem("sent")
        got = [sem(f"got{q}") for q in range(RING)]
        zeroed, built, turned, turned_out, widened = (
            sem("zeroed"), sem("onehot_built"), sem("turned"), sem("turned_out"), sem("onehot_widened"))
        looked, summand, relued, summed, added = sem("looked"), sem("summand"), sem("relued"), sem("summed"), sem("added")
        block = ctx.enter_context(nc.Block())

        @block.gpsimd
        def _(pool):
            def step(i):
                for half in range(2):
                    for q in range(half * 4, half * 4 + 4):
                        wait(pool, got[q], i * 32)
                    nc.gpsimd.tensor_copy(idxr[:, half, :],
                                          idx[:, bass.ds(i * 16 + half * 8, 8)]).then_inc(idx_copied, 1)
                    pool.wait_ge(idx_copied, i * 2 + (half + 1))
                    for q in range(half * 4, half * 4 + 4):
                        wait(pool, summed, i * RING + (q + 1 - RING))
                        pool.sem_inc(sent, 1)
                        for s in range(2):
                            n = (q % 4) * 2 + s
                            pool.indirect_dma_start(rows[:, q, s, :], None, q_table,
                                                    bass.IndirectOffsetOnAxis(idxr[:, half, n:n + 1], 0)
                                                    ).then_inc(got[q], 16)
            peeled(pool, NSTEP, step)

        @block.vector
        def _(v):
            nc.vector.memset(acc[:, :, :], 0.0).then_inc(zeroed, 1)
            v.wait_ge(zeroed, 1)

            def build(i, u):
                j = i * BODYP + u
                wait(v, turned, j - 3)
                wait(v, widened, j - 3)
                nc.vector.tensor_tensor(
                    ohb[:, u % 4, :, :], C.f("iota_p").unsqueeze(1).to_broadcast([P, 2, P]),
                    loc[:, bass.ds(i * 16 + u * 2, 2)].unsqueeze(2).to_broadcast([P, 2, P]),
                    ALU.is_equal).then_inc(built, 1)

            def add(i, u):
                v.wait_ge(got[u], (i + 1) * 32)
                v.wait_ge(looked, i * BODYP + (u + 1))
                nc.vector.tensor_tensor(rows[:, u, :, :], rows[:, u, :, :], pP[:, u % 2, :, :],
                                        ALU.add).then_inc(summand, 1)

            def accumulate(i, u):
                j = i * BODYP + u
                b = v.value_load(pair_block[0:1, bass.ds(j, 1)], min_val=0, max_val=NB - 1)
                v.wait_ge(summed, j + 1)
                wait(v, added, j)
                a = flat(acc[:, bass.ds(b, 1), :])
                nc.vector.tensor_tensor(a, pS[:, u % 2, :], a, ALU.add).then_inc(added, 1)

            lagged(v, NSTEP, BODYP, [(0, build), (2, add), (4, accumulate)])

        @block.scalar
        def _(act):
            def evacuate(i, u):
                j = i * BODYP + u
                act.wait_ge(turned, j + 1)
                wait(act, looked, j - 1)
                nc.scalar.copy(ohT[:, u % 2, :, :], pT[:, u % 2, 0:2, :]).then_inc(turned_out, 1)
                wait(act, summed, j + (1 - RING))
                nc.scalar.copy(ohf[:, u, :, :], ohb[:, u % 4, :, :]).then_inc(widened, 1)

            def relu(i, u):
                act.wait_ge(summand, i * BODYP + (u + 1))
                nc.scalar.activation(rows[:, u, :, :], rows[:, u, :, :], ACT.Relu).then_inc(relued, 1)

            lagged(act, NSTEP, BODYP, [(0, evacuate), (2, relu)])

        @block.tensor
        def _(pe):
            def turn(i, u):
                j = i * BODYP + u
                pe.wait_ge(built, j + 1)
                wait(pe, turned_out, j - 1)
                for s in range(2):
                    ins = nc.tensor.transpose(pT[:, u % 2, s, :], ohb[:, u % 4, s, :], identb[:, :])
                ins.then_inc(turned, 1)

            def look(i, u):
                j = i * BODYP + u
                b = pe.value_load(pair_block[0:1, bass.ds(j, 1)], min_val=0, max_val=NB - 1)
                pe.wait_ge(turned_out, j + 1)
                wait(pe, summand, j - 1)
                for s in range(2):
                    for n in range(2):
                        ins = nc.tensor.matmul(pP[:, u % 2, s, :], ohT[:, u % 2, s, :],
                                               flat(p_parts[n][:, bass.ds(b, 1), :]), start=n == 0, stop=n == 1)
                ins.then_inc(looked, 1)

            def scatter(i, u):
                j = i * BODYP + u
                pe.wait_ge(widened, j + 1)
                pe.wait_ge(relued, j + 1)
                wait(pe, added, j - 1)
                for s in range(2):
                    ins = nc.tensor.matmul(pS[:, u % 2, :], ohf[:, u, s, :], rows[:, u, s, :],
                                           start=s == 0, stop=s == 1)
                ins.then_inc(summed, 1)

            lagged(pe, NSTEP, BODYP, [(0, turn), (1, look), (3, scatter)])


class BlockChain:

    def __init__(self, eng, sem, waited):
        self.eng, self.sem, self.waited, self.length = eng, sem, waited, None

    def begin(self, b):
        self.base, self.count = (0 if self.length is None else b * self.length), 0

    def end(self):
        if self.length is None:
            self.length = self.count
        assert self.length == self.count

    def __call__(self, ins):
        self.count += 1
        ins.then_inc(self.sem, 1)
        self.eng.wait_ge(self.sem, self.base + self.count)

    def take_wait(self):
        self.eng.sem_inc(self.waited, 1)


class Normal:

    def __init__(self, nc, ctx, sem, name, per_block):
        sb = lambda n, w: ctx.enter_context(nc.sbuf_tensor(f"{name}_{n}", [P, w], F32))
        self.nc, self.per_block = nc, per_block
        self.bn, self.mv, self.var, self.sd, self.rstd = sb("bn", 6), sb("mv", 2), sb("var", 1), sb("sd", 1), sb("rstd", 1)
        self.var_ready, self.sd_ready = sem("var_ready"), sem("sd_ready")

    def stats(self, link, v, b, n, src):
        nc = self.nc
        link.take_wait()
        link(nc.vector.bn_stats(self.bn[:, :], src))
        link.take_wait()
        link(nc.vector.bn_aggr(self.mv[:, :], self.bn[:, :]))
        nc.vector.tensor_scalar(self.var[:, :], self.mv[:, 1:2], 1e-5, None, ALU.add).then_inc(self.var_ready, 1)
        v.wait_ge(self.sd_ready, b * self.per_block + (n + 1))
        link(nc.vector.reciprocal(self.rstd[:, :], self.sd[:, :]))

    def apply(self, out, src):
        return self.nc.vector.tensor_scalar(out, src, self.mv[:, 0:1], self.rstd[:, 0:1], ALU.subtract, ALU.mult)

    def roots(self, act, b):
        for n in range(self.per_block):
            act.wait_ge(self.var_ready, b * self.per_block + (n + 1))
            self.nc.scalar.activation(self.sd[:, :], self.var[:, :], ACT.Sqrt).then_inc(self.sd_ready, 1)


def node_stage(nc, name, X, acc, ident, prepare, n_stats, weights, save, targets, gate=None,
               keep_xT=None):
    nw = len(weights)
    with ExitStack() as ctx:
        sb = lambda n, s, d: ctx.enter_context(nc.sbuf_tensor(f"{name}_{n}", s, d))
        sem = stage_semaphores(nc, ctx, name)
        xn = sb("x_block", [P, 2, D], F32)
        xt = sb("xT_block", [P, 2, 4, P], F32)
        yr = sb("y_ring", [P, 2, nw, D], F32)
        tmp = sb("tmp", [P, D], F32)
        gates = sb("gates", [P, 2, 2], F32)
        pt = ctx.enter_context(nc.psum_tensor(f"{name}_pT", [P, 4, P], F32))
        py = ctx.enter_context(nc.psum_tensor(f"{name}_pY", [P, 2, nw, D], F32))
        pgate = ctx.enter_context(nc.psum_tensor(f"{name}_pGate", [P, 2, 2], F32)) if gate is not None else None
        normal = Normal(nc, ctx, sem, name, n_stats)
        s_dve, waited = sem("dve_chain"), sem("waited")
        normed, saved, transposed, xcopied = sem("normed"), sem("saved"), sem("transposed"), sem("xcopied")
        multiplied, dve_out, act_out, s_tmp = sem("multiplied"), sem("dve_out"), sem("act_out"), sem("s_tmp")
        gated = sem("gated")
        stored = [sem(f"stored{k}") for k in range(2)]
        on_dve = [w for w, (_, kind, _) in enumerate(weights) if kind == "bias_split"]
        on_act = [w for w, (_, kind, _) in enumerate(weights) if kind in ("table", "gated", "attend")]
        tabled = [w for w, (_, kind, _) in enumerate(weights) if not kind.startswith("bias")]
        attend = [w for w, (_, kind, _) in enumerate(weights) if kind == "attend"]
        n_dve = len(on_dve) + len(attend)
        block = ctx.enter_context(nc.Block())

        def two_behind(eng, first, second):
            def step(i):
                for k in range(2):
                    first(i * 2 + k, k)
                    if not is_first(i):
                        second(i * 2 + (k - 2), k, i - 1)
            peeled(eng, NB // 2, step, 2)
            for k in range(2):
                second(NB - 2 + k, k, NB // 2 - 1)

        @block.vector
        def _(v):
            link = BlockChain(v, s_dve, waited)

            def norm(b, k):
                wait(v, transposed, b - 1)
                wait(v, saved, b - 1)
                link.begin(b)
                prepare(link, v, normal, b, xn[:, k, :]).then_inc(normed, 1)
                link.end()
                if save:
                    v.wait_ge(normed, b + 1)
                    link.take_wait()
                    nc.vector.tensor_copy(flat(X[:, bass.ds(b, 1), :]), xn[:, k, :]).then_inc(saved, 1)
                else:
                    v.sem_inc(saved, 1)

            def finish(b, k, rounds):
                v.wait_ge(multiplied, b + 1)
                for w in on_dve:
                    bias, parts = weights[w][2]
                    high, low = (flat(part[:, bass.ds(b, 1), :]) for part in parts)
                    wait(v, dve_out, b)
                    nc.vector.tensor_tensor(tmp[:, :], py[:, k, w, :], bias, ALU.add).then_inc(s_tmp, 1)
                    v.wait_ge(s_tmp, b * 2 + 1)
                    nc.vector.tensor_scalar(high, tmp[:, :], 1.0, None, ALU.mult).then_inc(s_tmp, 1)
                    v.wait_ge(s_tmp, b * 2 + 2)
                    nc.vector.tensor_tensor(low, tmp[:, :], high.bitcast(F32), ALU.subtract).then_inc(dve_out, 1)
                for w in attend:
                    v.wait_ge(act_out, b + 1)
                    for n, (vec, est) in enumerate(weights[w][2]):
                        wait(v, s_tmp, b * 4 + 2 * n)
                        nc.vector.tensor_tensor(tmp[:, :], yr[:, k, w, :], vec, ALU.mult).then_inc(s_tmp, 1)
                        v.wait_ge(s_tmp, b * 4 + (2 * n + 1))
                        nc.vector.tensor_reduce(flat(est[:, bass.ds(b, 1), :]),
                                                tmp[:, :].rearrange("p (h d) -> p h d", h=H),
                                                AX.X, ALU.add).then_inc(s_tmp, 1)
                    v.wait_ge(s_tmp, b * 4 + 4)
                    v.sem_inc(dve_out, 1)

            two_behind(v, norm, finish)

        @block.tensor
        def _(pe):
            def turn(b, k):
                pe.wait_ge(normed, b + 1)
                wait(pe, xcopied, b)
                for c in range(4):
                    ins = nc.tensor.transpose(pt[:, c, :], xn[:, k, c * P:(c + 1) * P], ident)
                ins.then_inc(transposed, 1)

            def multiply(b, k):
                pe.wait_ge(xcopied, b + 1)
                if n_dve:
                    wait(pe, dve_out, b - 1)
                wait(pe, act_out, b - 1)
                for w in range(nw):
                    for c in range(4):
                        ins = nc.tensor.matmul(py[:, k, w, :], xt[:, k, c, :], weights[w][0][:, c, :],
                                               start=c == 0, stop=c == 3)
                if gate is not None:
                    wait(pe, gated, b)
                    for c in range(4):
                        ins = nc.tensor.matmul(pgate[:, k, :], xt[:, k, c, :], gate[:, c, :],
                                               start=c == 0, stop=c == 3)
                ins.then_inc(multiplied, 1)

            def step(i):
                for k in range(2):
                    turn(i * 2 + k, k)
                    if k or not is_first(i):
                        multiply(i * 2 + (k - 1), 1 - k)
            peeled(pe, NB // 2, step, 2)
            multiply(NB - 1, 1)

        @block.scalar
        def _(act):
            def copy_x(b, k):
                act.wait_ge(transposed, b + 1)
                wait(act, multiplied, b - 1)
                if keep_xT is not None:
                    nc.scalar.copy(keep_xT[:, bass.ds(b, 1), :, :].rearrange("p a c n -> p (a c) n"), pt[:, :, :])
                nc.scalar.copy(xt[:, k, :, :], pt[:, :, :]).then_inc(xcopied, 1)

            def finish(b, k, rounds):
                act.wait_ge(multiplied, b + 1)
                if gate is not None:
                    nc.scalar.activation(gates[:, k, :], pgate[:, k, :], ACT.Sigmoid).then_inc(gated, 1)
                    act.wait_ge(gated, b + 1)
                if on_act:
                    wait(act, stored[k], rounds * (16 * len(tabled)))
                for w in on_act:
                    _, kind, extra = weights[w]
                    scale = gates[:, k, extra:extra + 1] if kind == "gated" else 1.0
                    ins = nc.scalar.activation(yr[:, k, w, :], py[:, k, w, :], ACT.Copy, scale=scale)
                ins.then_inc(act_out, 1)

            def step(i):
                for k in range(2):
                    normal.roots(act, i * 2 + k)
                    if not is_first(i):
                        finish(i * 2 + (k - 2), k, i - 1)
                    copy_x(i * 2 + k, k)
            peeled(act, NB // 2, step, 2)
            for k in range(2):
                finish(NB - 2 + k, k, NB // 2 - 1)

        @block.sync
        def _(sp):
            with sp.Fori(0, NB // 2) as i:
                for k in range(2):
                    b = i * 2 + k
                    rows = sp.snap(b * P)
                    if n_dve:
                        sp.wait_ge(dve_out, b + 1)
                    sp.wait_ge(act_out, b + 1)
                    for w in tabled:
                        sp.dma_start(targets[w][bass.ds(rows, P), :], yr[:, k, w, :]).then_inc(stored[k], 16)
            for k in range(2):
                sp.wait_ge(stored[k], NB // 2 * 16 * len(tabled))


def last_norm(nc, name, prepare, out):
    with ExitStack() as ctx:
        sem = stage_semaphores(nc, ctx, name)
        rows = ctx.enter_context(nc.sbuf_tensor(f"{name}_rows", [P, NB, D], F32))
        normal = Normal(nc, ctx, sem, name, 1)
        s_dve, waited = sem("dve_chain"), sem("waited")
        final, stored = sem("final"), sem("stored")
        block = ctx.enter_context(nc.Block())

        @block.vector
        def _(v):
            link = BlockChain(v, s_dve, waited)

            def step(b):
                link.begin(b)
                prepare(link, v, normal, b, flat(rows[:, bass.ds(b, 1), :])).then_inc(final, 1)
                link.end()
            peeled(v, NB, step)

        @block.scalar
        def _(act):
            with act.Fori(0, NB) as b:
                normal.roots(act, b)

        @block.sync
        def _(sp):
            with sp.Fori(0, NB - 1) as b:
                at, n = sp.snap(b * P), sp.snap(b)
                sp.wait_ge(final, b + 1)
                sp.dma_start(out[bass.ds(at, P), :], flat(rows[:, bass.ds(n, 1), :])).then_inc(stored, 16)
            sp.wait_ge(final, NB)
            at = (NB - 1) * P
            sp.dma_start(out[at:N, :], rows[0:N - at, NB - 1, :]).then_inc(stored, 16)
            sp.wait_ge(stored, 16 * NB)


def transpose_weights(nc, name, C, pairs):
    n = len(pairs)
    with ExitStack() as ctx:
        sem = stage_semaphores(nc, ctx, name)
        raw = ctx.enter_context(nc.sbuf_tensor(f"{name}_raw", [P, 2, 4, D], F32))
        pt = ctx.enter_context(nc.psum_tensor(f"{name}_pT", [P, 2, 4, P], F32))
        loaded = [sem(f"loaded{k}") for k in range(2)]
        turned, copied = sem("turned"), sem("copied")
        block = ctx.enter_context(nc.Block())

        @block.sync
        def _(sp):
            for m, (w, _) in enumerate(pairs):
                wait(sp, turned, (m - 1) * 4)
                sp.dma_start(raw[:, m % 2, :, :], w.rearrange("(c p) i -> p c i", p=P)).then_inc(loaded[m % 2], 16)
            for k in range(min(n, 2)):
                sp.wait_ge(loaded[k], (n + 1 - k) // 2 * 16)

        @block.tensor
        def _(pe):
            for m in range(n):
                pe.wait_ge(loaded[m % 2], (m // 2 + 1) * 16)
                for ic in range(4):
                    g = m * 4 + ic
                    wait(pe, copied, g - 1)
                    for oc in range(4):
                        ins = nc.tensor.transpose(pt[:, g % 2, oc, :], raw[:, m % 2, oc, ic * P:(ic + 1) * P],
                                                  C.f("ident"))
                    ins.then_inc(turned, 1)

        @block.scalar
        def _(act):
            for m, (_, out) in enumerate(pairs):
                for ic in range(4):
                    g = m * 4 + ic
                    act.wait_ge(turned, g + 1)
                    nc.scalar.copy(out[:, ic, :], pt[:, g % 2, :, :].rearrange("p o n -> p (o n)")).then_inc(copied, 1)


GS = 4


def split3(link, nc, out, src, rest):
    link(nc.vector.tensor_copy(out[0], src))
    link(nc.vector.tensor_tensor(rest, src, out[0], ALU.subtract))
    link(nc.vector.tensor_copy(out[1], rest))
    link(nc.vector.tensor_tensor(rest, rest, out[1], ALU.subtract))
    link(nc.vector.tensor_copy(out[2], rest))


def edge_scores(nc, name, C, identb, est, edt, src_lo, src_block, loc, pair_block, es_out, ed_out):
    U = 4
    STEPS = SLOTS // GS // U
    with ExitStack() as ctx:
        sb = lambda n, s, d: ctx.enter_context(nc.sbuf_tensor(f"{name}_{n}", s, d))
        ps = lambda n, s, d: ctx.enter_context(nc.psum_tensor(f"{name}_{n}", s, d))
        sem = stage_semaphores(nc, ctx, name)
        s3, d3 = sb("source3", [P, 3, NB, H], BF16), sb("target3", [P, 3, NB, H], BF16)
        rest = sb("rest", [P, NB, H], F32)
        oh = sb("onehots", [P, 2, 2, GS, P], BF16)
        ohT = sb("onehotsT", [P, 2, 2, GS, P], BF16)
        ohb = sb("onehot_block", [P, U, GS, NB], F32)
        mine = sb("of_own_block", [P, 2, GS, H, NB], F32)
        pT = ps("pT", [P, 2, 2, GS, P], BF16)
        pl = ps("pLook", [P, 2, D], F32)
        ES, ED = GS * NB * H, GS * H
        s_dve, tables = sem("dve_chain"), sem("tables_ready")
        built, turned, copied, looked = sem("built"), sem("turned"), sem("copied"), sem("looked")
        masked, taken = sem("masked"), sem("taken")
        block = ctx.enter_context(nc.Block())

        @block.vector
        def _(v):
            link = chain(v, s_dve)
            split3(link, nc, [s3[:, n, :, :] for n in range(3)], est[:, :, :], rest[:, :, :])
            split3(link, nc, [d3[:, n, :, :] for n in range(3)], edt[:, :, :], rest[:, :, :])
            v.sem_inc(tables, 1)

            def build(i, u):
                wait(v, turned, i * U + (u - 1))
                s = bass.ds((i * U + u) * GS, GS)
                for n, col in ((0, src_lo), (1, loc)):
                    nc.vector.tensor_tensor(oh[:, u % 2, n, :, :],
                                            C.f("iota_p").unsqueeze(1).to_broadcast([P, GS, P]),
                                            col[:, s].unsqueeze(2).to_broadcast([P, GS, P]),
                                            ALU.is_equal).then_inc(built, 1)
                wait(v, masked, i * U + (u - U + 1))
                nc.vector.tensor_tensor(ohb[:, u, :, :],
                                        C.f("iota_p")[:, 0:NB].unsqueeze(1).to_broadcast([P, GS, NB]),
                                        src_block[:, s].unsqueeze(2).to_broadcast([P, GS, NB]),
                                        ALU.is_equal).then_inc(built, 1)

            def mask(i, u):
                g = i * U + u
                v.wait_ge(built, g * 3 + 3)
                v.wait_ge(looked, g + 1)
                wait(v, taken, g - 1)
                nc.vector.tensor_copy(ed_out[:, bass.ds(g * GS, GS), :],
                                      pl[:, u % 2, ES:ES + ED].rearrange("p (s h) -> p s h", h=H))
                nc.vector.tensor_tensor(
                    mine[:, u % 2, :, :, :],
                    pl[:, u % 2, 0:ES].rearrange("p (s b h) -> p s h b", h=H, b=NB),
                    ohb[:, u, :, :].unsqueeze(2).to_broadcast([P, GS, H, NB]), ALU.mult).then_inc(masked, 1)

            def take(i, u):
                g = i * U + u
                v.wait_ge(masked, g + 1)
                nc.vector.tensor_reduce(es_out[:, bass.ds(g * GS, GS), :], mine[:, u % 2, :, :, :],
                                        AX.X, ALU.add).then_inc(taken, 1)

            def step(i):
                for u in range(U):
                    build(i, u)
                    for lag, work in ((2, mask), (3, take)):
                        if u >= lag:
                            work(i, u - lag)
                        elif not isinstance(i, int):
                            work(i - 1, U + u - lag)
            peeled(v, STEPS, step)
            mask(STEPS - 1, U - 2)
            take(STEPS - 1, U - 3)
            mask(STEPS - 1, U - 1)
            take(STEPS - 1, U - 2)
            take(STEPS - 1, U - 1)

        @block.scalar
        def _(act):
            def step(i):
                for u in range(U):
                    g = i * U + u
                    act.wait_ge(turned, g + 1)
                    wait(act, looked, g - 1)
                    nc.scalar.copy(ohT[:, u % 2, :, :, :], pT[:, u % 2, :, :, :]).then_inc(copied, 1)
            peeled(act, STEPS, step)

        @block.tensor
        def _(pe):
            pe.wait_ge(tables, 1)

            def turn(i, u):
                g = i * U + u
                pe.wait_ge(built, g * 3 + 2)
                wait(pe, copied, g - 1)
                for n in range(2):
                    for s in range(GS):
                        ins = nc.tensor.transpose(pT[:, u % 2, n, s, :], oh[:, u % 2, n, s, :], identb[:, :])
                ins.then_inc(turned, 1)

            def look(i, u):
                g = i * U + u
                blocks = [pe.value_load(pair_block[0:1, bass.ds(g * (GS // 2) + q, 1)], min_val=0,
                                        max_val=NB - 1) for q in range(GS // 2)]
                pe.wait_ge(copied, g + 1)
                wait(pe, masked, g - 1)
                for s in range(GS):
                    for n in range(3):
                        nc.tensor.matmul(pl[:, u % 2, s * NB * H:(s + 1) * NB * H], ohT[:, u % 2, 0, s, :],
                                         flat(s3[:, n, :, :]), start=n == 0, stop=n == 2)
                    for n in range(3):
                        ins = nc.tensor.matmul(pl[:, u % 2, ES + s * H:ES + (s + 1) * H], ohT[:, u % 2, 1, s, :],
                                               flat(d3[:, n, bass.ds(blocks[s // 2], 1), :]),
                                               start=n == 0, stop=n == 2)
                ins.then_inc(looked, 1)

            def step(i):
                for u in range(U):
                    turn(i, u)
                    if u:
                        look(i, u - 1)
                    elif not isinstance(i, int):
                        look(i - 1, U - 1)
            peeled(pe, STEPS, step)
            look(STEPS - 1, U - 1)


EC = H + 1


def attention_weights(nc, name, C, es, ed, types, weight, loc, block_f, emb, edram, exd, wt):
    with ExitStack() as ctx:
        sb = lambda n, s, d: ctx.enter_context(nc.sbuf_tensor(f"{name}_{n}", s, d))
        before = sb("before", [P, EC], F32)
        embv = sb("emb", [P, 8, H], F32)
        fac = sb("factor", [P, H, SLOTS], F32)
        scored = sb("scored", [P, SLOTS, EC], F32)
        neigh = sb("neighbours", [P, SLOTS, EC], F32)
        e = neigh[:, :, 0:H].rearrange("p s h -> p h s")
        key = neigh[:, :, H]
        t1, t2 = sb("t1", [P, H, SLOTS], F32), sb("t2", [P, H, SLOTS], F32)
        same = sb("same", [P, H, SLOTS], F32)
        same_n = sb("same_next", [P, H, SLOTS], F32)
        ex = sb("ex", [P, SLOTS, H], F32)
        mask = sb("mask", [P, SLOTS], F32)
        flags = sb("flags", [P, 2], F32)
        cols = sb("cols", [P, 4, H], F32)
        row = sb("row", [H, 4, P + 2], F32)
        outr = sb("outr", [H, 2, P + 2], F32)
        carry = sb("carry", [H, 2, P], F32)
        pr = ctx.enter_context(nc.psum_tensor(f"{name}_pr", [H, 4, P], F32))
        pc = ctx.enter_context(nc.psum_tensor(f"{name}_pc", [P, 2, H], F32))
        sem = stage_semaphores(nc, ctx, name)
        emb_in, set_before, s_dve = sem("emb_in"), sem("set_before"), sem("dve_chain")
        scored_ready, e_out, e_in = sem("scored_ready"), sem("e_out"), sem("e_in")
        turned, ex_ready, s_out, s_back, exp_in, cols_ready = (
            sem("turned"), sem("ex_ready"), sem("ex_out"), sem("ex_back"), sem("exp_in"), sem("cols_ready"))
        block = ctx.enter_context(nc.Block())

        @block.sync
        def _(sp):
            sp.dma_start(flat(embv[:, :, :]), emb.rearrange("t h -> (t h)").partition_broadcast(P)).then_inc(emb_in, 16)
            with nc.allow_non_contiguous_dma("scores of 36 bytes"):
                sp.wait_ge(scored_ready, 1)
                sp.dma_start(edram.rearrange("(s p) c -> p s c", p=P), scored[:, :, :]).then_inc(e_out, 16)
                sp.wait_ge(e_out, 16)
                sp.dma_start(flat(neigh[:, :, :]), edram.rearrange("(p s) c -> p (s c)", p=P)).then_inc(e_in, 16)
                sp.wait_ge(set_before, 1)
                sp.dma_start(before[1:P, :], edram.rearrange("(p s) c -> p s c", p=P)[0:P - 1, SLOTS - 1, :]
                             ).then_inc(e_in, 16)
                sp.wait_ge(e_in, 32)
                sp.wait_ge(ex_ready, 1)
                sp.dma_start(exd.rearrange("(p s) h -> p (s h)", p=P), flat(ex[:, :, :])).then_inc(s_out, 16)
                sp.wait_ge(s_out, 16)
                sp.dma_start(wt[:, :, 0:H], exd.rearrange("(s p) h -> p s h", p=P)).then_inc(s_back, 16)
                sp.wait_ge(s_back, 16)

        @block.scalar
        def _(act):
            act.wait_ge(exp_in, 1)
            nc.scalar.activation(ex[:, :, :], t1[:, :, :].rearrange("p h s -> p s h"), ACT.Exp).then_inc(ex_ready, 1)

        @block.vector
        def _(v):
            link = chain(v, s_dve)
            nc.vector.memset(before[:, :], -2.0).then_inc(set_before, 1)
            v.wait_ge(emb_in, 16)
            link(nc.vector.tensor_scalar(flat(embv[:, :, :]), flat(embv[:, :, :]), 1.0, None, ALU.add))
            link(nc.vector.memset(flat(fac[:, :, :]), 0.0))
            for t in range(8):
                link(nc.vector.tensor_scalar(mask[:, :], types, float(t), None, ALU.is_equal))
                link(nc.vector.tensor_tensor(t1[:, :, :], mask[:, :].unsqueeze(1).to_broadcast([P, H, SLOTS]),
                                             embv[:, t, :].unsqueeze(2).to_broadcast([P, H, SLOTS]), ALU.mult))
                link(nc.vector.tensor_tensor(fac[:, :, :], fac[:, :, :], t1[:, :, :], ALU.add))
            link(nc.vector.tensor_tensor(es[:, :, :], es[:, :, :], ed[:, :, :], ALU.add))
            link(nc.vector.scalar_tensor_tensor(flat(es[:, :, :]), flat(es[:, :, :]), 0.2, flat(es[:, :, :]),
                                                ALU.mult, ALU.max))
            link(nc.vector.tensor_tensor(es[:, :, :], es[:, :, :], fac[:, :, :].rearrange("p h s -> p s h"), ALU.mult))
            link(nc.vector.tensor_tensor(scored[:, :, 0:H], es[:, :, :],
                                         weight.unsqueeze(2).to_broadcast([P, SLOTS, H]), ALU.mult))
            link(nc.vector.tensor_scalar(mask[:, :], loc, 0.0, float(P), ALU.is_ge, ALU.mult))
            link(nc.vector.tensor_tensor(
                mask[:, :].rearrange("p (j s) -> p j s", s=2), mask[:, :].rearrange("p (j s) -> p j s", s=2),
                block_f.unsqueeze(2).to_broadcast([P, PAIRS, 2]), ALU.mult))
            nc.vector.tensor_tensor(scored[:, :, H], mask[:, :], loc, ALU.add).then_inc(scored_ready, 1)
            v.wait_ge(scored_ready, 1)
            v.wait_ge(e_in, 32)
            link(nc.vector.memset(mask[:, 0:1], 0.0))
            link(nc.vector.tensor_tensor(mask[:, 1:SLOTS], key[:, 1:SLOTS], key[:, 0:SLOTS - 1], ALU.is_equal))
            link(nc.vector.tensor_copy(same[:, :, :], mask[:, :].unsqueeze(1).to_broadcast([P, H, SLOTS])))
            link(nc.vector.memset(same_n[:, :, SLOTS - 1:SLOTS], 0.0))
            link(nc.vector.tensor_copy(same_n[:, :, 0:SLOTS - 1], same[:, :, 1:SLOTS]))
            link(nc.vector.tensor_tensor(flags[:, 0:1], key[:, 0:1], before[:, H:EC], ALU.is_equal))
            link(nc.vector.tensor_reduce(flags[:, 1:2], mask[:, 1:SLOTS], AX.X, ALU.min))
            link(nc.vector.tensor_copy(cols[:, 2, :], flags[:, 1:2].to_broadcast([P, H])))
            link(nc.vector.tensor_copy(cols[:, 3, :], flags[:, 0:1].to_broadcast([P, H])))
            link(nc.vector.memset(row[:, :, :], 0.0))
            link(nc.vector.memset(outr[:, :, :], 0.0))
            def forward(src, out):
                link(nc.vector.tensor_tensor_scan(flat(out[:, :, :]), flat(same[:, :, :]), flat(src[:, :, :]), 0.0,
                                                  ALU.mult, ALU.max))

            def backward(src, out):
                link(nc.vector.tensor_tensor_scan(flat(out[:, :, :])[:, ::-1], flat(same_n[:, :, :])[:, ::-1],
                                                  flat(src[:, :, :])[:, ::-1], 0.0, ALU.mult, ALU.max))

            link(nc.vector.tensor_copy(fac[:, :, :], e))
            forward(fac, t1)
            backward(fac, t2)
            link(nc.vector.tensor_copy(cols[:, 0, :], t1[:, :, SLOTS - 1]))
            nc.vector.tensor_copy(cols[:, 1, :], t2[:, :, 0]).then_inc(cols_ready, 1)
            v.wait_ge(turned, 1)
            link(nc.vector.tensor_copy(row[:, :, 1:P + 1], pr[:, :, :]))
            tail, head, one, cont = (row[:, n, :] for n in range(4))
            link(nc.vector.tensor_tensor(carry[:, 0, :], one[:, 1:P + 1], cont[:, 1:P + 1], ALU.mult))
            link(nc.vector.tensor_tensor(carry[:, 1, :], one[:, 1:P + 1], cont[:, 2:P + 2], ALU.mult))
            link(nc.vector.tensor_tensor_scan(outr[:, 0, 1:P + 1], carry[:, 0, :], tail[:, 1:P + 1], 0.0,
                                              ALU.mult, ALU.max))
            link(nc.vector.tensor_tensor_scan(outr[:, 1, 1:P + 1][:, ::-1], carry[:, 1, :][:, ::-1],
                                              head[:, 1:P + 1][:, ::-1], 0.0, ALU.mult, ALU.max))
            link(nc.vector.tensor_tensor(carry[:, 0, :], cont[:, 1:P + 1], outr[:, 0, 0:P], ALU.mult))
            nc.vector.tensor_tensor(carry[:, 1, :], cont[:, 2:P + 2], outr[:, 1, 2:P + 2], ALU.mult
                                    ).then_inc(cols_ready, 1)
            v.wait_ge(turned, 2)
            link(nc.vector.tensor_tensor(fac[:, :, 0], fac[:, :, 0], pc[:, 0, :], ALU.max))
            link(nc.vector.tensor_tensor(fac[:, :, SLOTS - 1], fac[:, :, SLOTS - 1], pc[:, 1, :], ALU.max))
            forward(fac, t1)
            backward(t1, t2)
            nc.vector.tensor_tensor(t1[:, :, :], e, t2[:, :, :], ALU.subtract).then_inc(exp_in, 1)

        @block.tensor
        def _(pe):
            pe.wait_ge(cols_ready, 1)
            for n in range(4):
                ins = nc.tensor.transpose(pr[:, n, :], cols[:, n, :], C.f("ident"))
            ins.then_inc(turned, 1)
            pe.wait_ge(cols_ready, 2)
            for n in range(2):
                ins = nc.tensor.transpose(pc[:, n, :], carry[:, n, :], C.f("ident", H)[:, 0:H])
            ins.then_inc(turned, 1)


def unpack(link, nc, packed, itmp, loc, outs):
    v = itmp[:, 0, :]
    link(nc.vector.tensor_copy(v, packed))
    link(nc.vector.tensor_single_scalar(itmp[:, 1, :], v, 255, ALU.bitwise_and))
    link(nc.vector.tensor_scalar(loc[:, :], itmp[:, 1, :], 1.0, None, ALU.subtract))
    for out, shift, mask in outs:
        link(nc.vector.tensor_scalar(itmp[:, 1, :], v, shift, mask, ALU.logical_shift_right, ALU.bitwise_and))
        link(nc.vector.tensor_copy(out, itmp[:, 1, :]))


def gnn(nc, ins, consts, out):
    dram = lambda n, s: nc.dram_tensor(n, s, F32, kind="Internal").ap()
    tab = {n: dram(f"tab_{n}", s) for n, s in {
        "q": [NP, D], "h": [NP, D],
        "e": [ROWS, EC], "ex": [ROWS, H], "n": [NP, D], "y": [REL * NP, D],
        "w1": [REL * BCH, D * D // BCH], "w2": [REL * BCH, D * D // BCH]}.items()}
    VECS = ["L0_gnn_b", "L1_gnn_ln_gamma", "L1_gnn_ln_beta", "L2_gnn_bias", "L2_gnn_gamma", "L2_gnn_beta",
            "L3_gnn_bias1", "L3_gnn_bias2", "L1_gnn_a_src", "L1_gnn_a_dst"]
    with ExitStack() as top:
        keep = lambda n, s, d: top.enter_context(nc.sbuf_tensor(n, s, d))
        C = Const(keep("const_table", [P, CONSTS.shape[1]], F32), None)
        identb = keep("identb", [P, P], BF16)
        ends = ("src", "dst")
        pairs = {k: keep(f"pair_block_{k}", [1, PAIRS], I32) for k in ends}
        blocks = {k: keep(f"block_of_pair_{k}", [P, PAIRS], F32) for k in ends}
        loc = {k: keep(f"loc_{k}", [P, SLOTS], F32) for k in ends}
        idx = {k: keep(f"idx_{k}", [P, SLOTS], I32) for k in ("q", "rel", "h")}
        packed = {k: keep(f"packed_{k}", [P, SLOTS], F32) for k in ends}
        src_block, src_lo, types, weight = (keep(n, [P, SLOTS], F32) for n in ("src_block", "src_lo", "types", "weight"))

        basis = [Basis(nc, f"basis{l}", ins[f"L3_gnn_basis{l + 1}"], ins[f"L3_gnn_att{l + 1}"], tab[f"w{l + 1}"])
                 for l in range(2)]

        with ExitStack() as ctx:
            sb = lambda n, s, d: ctx.enter_context(nc.sbuf_tensor(n, s, d))
            raw = sb("edge_ints", [EP, 4, T], I32)
            fld = sb("edge_fields", [EP, 6, T], F32)
            SRC, DST, T2, T8, WT, REL1 = range(6)
            with ExitStack() as c1:
                sem = stage_semaphores(nc, c1, "load")
                const_in, edges_in, s_dve = sem("const_in"), sem("edges_in"), sem("load_chain")
                block = c1.enter_context(nc.Block())

                @block.sync
                def _(sp):
                    for n, k in enumerate(("src", "dst", "edge_type_2", "edge_type_8")):
                        sp.dma_start(raw[:, n, :], ins[k].rearrange("(p t) -> p t", t=T)).then_inc(edges_in, 16)
                    sp.dma_start(fld[:, WT, :], ins["edge_weight"].rearrange("(p t) -> p t", t=T)).then_inc(edges_in, 16)
                    sp.dma_start(C.t[:, :], consts).then_inc(const_in, 16)
                    sp.wait_ge(edges_in, 80)
                    sp.wait_ge(const_in, 16)

                @block.vector
                def _(v):
                    link = chain(v, s_dve)
                    v.wait_ge(edges_in, 80)
                    link(nc.vector.tensor_copy(fld[:, 0:4, :], raw[:, :, :]))
                    link(nc.vector.tensor_scalar(fld[:, REL1, :], fld[:, T2, :], 0.0, None, ALU.not_equal))
                    v.wait_ge(const_in, 16)
                    link(nc.vector.tensor_copy(identb[:, :], C.f("ident")))
            f = lambda n: fld[:, n, :]
            SH1, SH2 = 8, 19
            sort_edges(nc, "src", C, identb, f(SRC), [(f(DST), 1 << SH1), (f(REL1), 1 << SH2)], None,
                       pairs["src"][:, :], blocks["src"][:, :], [packed["src"][:, :]], basis[1])
            sort_edges(nc, "dst", C, identb, f(DST), [(f(SRC), 1 << SH1), (f(T8), 1 << SH2)], f(WT),
                       pairs["dst"][:, :], blocks["dst"][:, :], [packed["dst"][:, :], weight[:, :]], basis[0])

        X, acc = (keep(n, [P, NB, D], F32) for n in ("x", "acc"))
        vec = keep("vectors", [P, len(VECS), D], F32)
        V = {n: vec[:, k, :] for k, n in enumerate(VECS)}
        W = [keep(f"weights{n}", [P, 4, D], F32) for n in range(3)]
        gate_w = keep("gate_w", [P, 2, 4, REL], F32)
        side = keep("side", [P, NB, H + 1], F32)
        est, edt = keep("e_src", [P, NB, H], F32), keep("e_dst", [P, NB, H], F32)
        wt = keep("edge_weights", [P, SLOTS, H + 1], F32)

        with ExitStack() as ctx:
            sem = stage_semaphores(nc, ctx, "load")
            itmp = ctx.enter_context(nc.sbuf_tensor("unpack_tmp", [P, 2, SLOTS], I32))
            vecs_in, x_in, x_zero, s_dve = sem("vecs_in"), sem("x_in"), sem("x_zero"), sem("in_chain")
            block = ctx.enter_context(nc.Block())

            @block.sync
            def _(sp):
                for k, n in enumerate(VECS):
                    a = ins[n]
                    if len(a.shape) == 2:
                        a = a.rearrange("a b -> (a b)")
                    sp.dma_start(vec[:, k, :], a.partition_broadcast(P)).then_inc(vecs_in, 16)
                with nc.allow_non_contiguous_dma("gate weights, once"):
                    for l in range(2):
                        for r in range(REL):
                            sp.dma_start(gate_w[:, l, :, r],
                                         ins[f"L3_gnn_gate_w{l + 1}"][r, :, :].rearrange("(c p) a -> p (c a)", p=P)
                                         ).then_inc(vecs_in, 16)
                full = N // P
                sp.dma_start(X[:, 0:full, :], ins["x"][0:full * P, :].rearrange("(b p) d -> p b d", p=P)).then_inc(x_in, 16)
                sp.wait_ge(x_zero, 1)
                sp.dma_start(X[0:N - full * P, full, :], ins["x"][full * P:N, :]).then_inc(x_in, 16)
                sp.wait_ge(x_in, 32)
                sp.wait_ge(vecs_in, 16 * (len(VECS) + 4))

            @block.vector
            def _(v):
                link = chain(v, s_dve)
                nc.vector.memset(X[:, NB - 1, :], 0.0).then_inc(x_zero, 1)
                link(nc.vector.memset(wt[:, :, H:H + 1], 1.0))
                unpack(link, nc, packed["src"][:, :], itmp, loc["src"],
                       [(idx["q"][:, :], SH1, 2047), (idx["rel"][:, :], SH2, 1)])
                link(nc.vector.scalar_tensor_tensor(idx["rel"][:, :], idx["rel"][:, :], float(NP), idx["q"][:, :],
                                                    ALU.mult, ALU.add))
                unpack(link, nc, packed["dst"][:, :], itmp, loc["dst"],
                       [(idx["h"][:, :], SH1, 2047), (src_block[:, :], SH1 + 7, 15), (src_lo[:, :], SH1, P - 1),
                        (types[:, :], SH2, 7)])

        W0 = ins["L0_gnn_W"]
        transpose_weights(nc, "w0", C, [(W0[:, 0:D], W[0]), (W0[:, D:2 * D], W[1])])
        def rows_of(tile, b):
            return flat(tile[:, bass.ds(b, 1), :])

        def take_x(link, v, normal, b, x):
            link.take_wait()
            return nc.vector.tensor_copy(x, rows_of(X, b))

        with ExitStack() as ctx:
            p_parts = [ctx.enter_context(nc.sbuf_tensor(f"p_{n}", [P, NB, D], mybir.dt.float32r))
                       for n in ("high", "low")]
            node_stage(nc, "n0", X, acc, C.f("ident"), take_x, 0,
                       [(W[0], "bias_split", (V["L0_gnn_b"], p_parts)), (W[1], "table", None)], False,
                       [None, tab["q"]])
            edge_convolution(nc, "e0", C, identb, p_parts, tab["q"], idx["q"], loc["src"], pairs["src"], acc)

        def norm_of_sum(link, v, normal, b, x):
            a = rows_of(acc, b)
            link(nc.vector.tensor_tensor(a, a, rows_of(X, b), ALU.add))
            normal.stats(link, v, b, 0, a)
            return normal.apply(x, a)

        transpose_weights(nc, "w1", C, [(ins["L1_gnn_W"], W[0])])
        node_stage(nc, "n1", X, acc, C.f("ident"), norm_of_sum, 1,
                   [(W[0], "attend", ((V["L1_gnn_a_src"], est), (V["L1_gnn_a_dst"], edt)))], True, [tab["h"]])
        with ExitStack() as ctx:
            es, ed = (ctx.enter_context(nc.sbuf_tensor(n, [P, SLOTS, H], F32)) for n in ("edge_e_src", "edge_e_dst"))
            edge_scores(nc, "scores", C, identb, est, edt, src_lo, src_block, loc["dst"], pairs["dst"], es, ed)
            attention_weights(nc, "att", C, es, ed, types[:, :], weight[:, :], loc["dst"][:, :], blocks["dst"][:, :],
                              ins["L1_gnn_et_emb"], tab["e"], tab["ex"], wt)
        edge_pass(nc, "e1", C, tab["h"], idx["h"], loc["dst"], pairs["dst"], acc, wt, side)

        held = keep("held", [P, NB, D], F32)
        xT = keep("xT", [P, NB, 4, P], F32)
        affine = keep("affine_tmp", [P, D], F32)

        extra = [keep(f"more_weights{n}", [P, 4, D], F32) for n in range(2)]

        def rel_tiles(l):
            return (W[0], W[2], extra[0]) if l == 0 else (W[1], extra[1], W[2])

        def rel_weights(l):
            w0, w1, root = rel_tiles(l)
            return [(w[:, :, :], tab[f"w{l + 1}"][r * BCH:(r + 1) * BCH, :].rearrange("c (p o) -> p c o", o=D))
                    for r, w in enumerate((w0, w1))] + [
                        (root[:, :, :], ins[f"L3_gnn_root{l + 1}"].rearrange("(c p) o -> p c o", p=P))]

        def norm_affine_norm(link, v, normal, b, x, a, gamma, beta):
            normal.stats(link, v, b, 0, a)
            link(nc.vector.tensor_tensor(affine[:, :], rows_of(X, b), beta, ALU.add))
            link(nc.vector.scalar_tensor_tensor(a, a, normal.mv[:, 0:1], gamma, ALU.subtract, ALU.mult))
            link(nc.vector.scalar_tensor_tensor(a, a, normal.rstd[:, 0:1], affine[:, :], ALU.mult, ALU.add))
            normal.stats(link, v, b, 1, a)
            return normal.apply(x, a)

        def after_attention(link, v, normal, b, x):
            a, w = rows_of(acc, b), flat(side[:, bass.ds(b, 1), 0:H])
            ah = a.rearrange("p (h d) -> p h d", h=H)
            link(nc.vector.tensor_scalar(w, w, 1e-10, None, ALU.add))
            link.take_wait()
            link(nc.vector.reciprocal(w, w))
            link(nc.vector.tensor_tensor(ah, ah, w.unsqueeze(2).to_broadcast([P, H, DH]), ALU.mult))
            link(nc.vector.tensor_tensor(a, a, rows_of(X, b), ALU.add))
            return norm_affine_norm(link, v, normal, b, x, a, V["L1_gnn_ln_gamma"], V["L1_gnn_ln_beta"])

        transpose_weights(nc, "w2", C, [(ins["L2_gnn_W_neigh"], W[0]), (ins["L2_gnn_W_self"], W[1])])
        node_stage(nc, "n2", X, acc, C.f("ident"), after_attention, 2,
                   [(W[0], "table", None)], True, [tab["n"]], keep_xT=xT)
        edge_pass(nc, "e2", C, tab["n"], idx["h"], loc["dst"], pairs["dst"], acc,
                  own=(xT, W[1], V["L2_gnn_bias"], held), fetch=rel_weights(0))

        def after_mean(link, v, normal, b, x):
            a, n = rows_of(acc, b), flat(side[:, bass.ds(b, 1), H:H + 1])
            link(nc.vector.tensor_scalar(n, n, 1.0, None, ALU.max))
            link.take_wait()
            link(nc.vector.reciprocal(n, n))
            link(nc.vector.scalar_tensor_tensor(a, a, n, rows_of(held, b), ALU.mult, ALU.add))
            return norm_affine_norm(link, v, normal, b, x, a, V["L2_gnn_gamma"], V["L2_gnn_beta"])

        def relu_of_sum(link, v, normal, b, x):
            a = rows_of(acc, b)
            link(nc.vector.tensor_tensor(a, a, rows_of(held, b), ALU.add))
            return nc.vector.tensor_scalar(x, a, 0.0, None, ALU.max)

        for l in range(2):
            w0, w1, root = rel_tiles(l)
            node_stage(nc, f"n{3 + l}", X, acc, C.f("ident"), relu_of_sum if l else after_mean, 0 if l else 2,
                       [(w0, "gated", 0), (w1, "gated", 1)], l == 0,
                       [tab["y"][0:NP, :], tab["y"][NP:REL * NP, :]], gate=gate_w[:, l, :, :], keep_xT=xT)
            edge_pass(nc, f"e{3 + l}", C, tab["y"], idx["rel"], loc["src"], pairs["src"], acc,
                      own=(xT, root, V[f"L3_gnn_bias{l + 1}"], held), fetch=() if l else rel_weights(1))

        def all_summed(link, v, normal, b, x):
            a = rows_of(acc, b)
            link(nc.vector.tensor_tensor(a, a, rows_of(held, b), ALU.add))
            return norm_of_sum(link, v, normal, b, x)

        last_norm(nc, "last", all_summed, out)


_INS = ["x", "src", "dst", "edge_type_2", "edge_type_8", "edge_weight", "L0_gnn_W", "L0_gnn_b", "L1_gnn_W",
        "L1_gnn_a_src", "L1_gnn_a_dst", "L1_gnn_et_emb", "L1_gnn_ln_gamma", "L1_gnn_ln_beta", "L2_gnn_W_self",
        "L2_gnn_W_neigh", "L2_gnn_bias", "L2_gnn_gamma", "L2_gnn_beta", "L3_gnn_basis1", "L3_gnn_att1",
        "L3_gnn_gate_w1", "L3_gnn_root1", "L3_gnn_bias1", "L3_gnn_basis2", "L3_gnn_att2", "L3_gnn_gate_w2",
        "L3_gnn_root2", "L3_gnn_bias2"]


def kernel(**inputs):
    import numpy as _np
    import concourse.bacc as _bacc
    from concourse import mybir as _mybir
    from concourse.bass_utils import run_bass_kernel_spmd as _run

    nc = _bacc.Bacc("TRN2", target_bir_lowering=False, num_devices=1)
    arrays, aps = {"constants": CONSTS}, {}
    consts = nc.dram_tensor("constants", CONSTS.shape, _mybir.dt.float32, kind="ExternalInput").ap()
    for name in _INS:
        a = _np.ascontiguousarray(inputs[name])
        arrays[f"in_{name}"] = a
        aps[name] = nc.dram_tensor(f"in_{name}", a.shape, _mybir.dt.from_np(a.dtype), kind="ExternalInput").ap()
    out = nc.dram_tensor("out", (N, D), _mybir.dt.float32, kind="ExternalOutput").ap()
    gnn(nc, aps, consts, out)
    r = _run(nc, [arrays], core_ids=[0])
    return r.results[0]["out"]
```

```python
import concourse.bass as bass
from concourse import mybir
from contextlib import ExitStack
import numpy as np

F32, BF16, I32 = mybir.dt.float32, mybir.dt.bfloat16, mybir.dt.int32
ALU, ACT, AX = mybir.AluOpType, mybir.ActivationFunctionType, mybir.AxisListType

P = 128
N, E, D = 1250, 20000, 512
NB = -(-N // P)
NP = NB * P
EP, T = 125, 160
GT = 16
LB = 4
HI, LO = NP >> LB, 1 << LB
KO = HI + LO
PAIRS = E // 256 + NB
SLOTS = 2 * PAIRS
H, DH = 8, 64


def stage_semaphores(nc, ctx, name):
    taken = []

    def give_back():
        nc.clear_and_free_semaphores(taken)
        nc.all_engine_barrier(sem_only=True)

    ctx.callback(give_back)

    def sem(what):
        taken.append(nc.alloc_semaphore(name=f"{name}_{what}_{nc.next_id()}"))
        return taken[-1]

    return sem


def chain(eng, sem):
    count = [0]

    def link(ins):
        count[0] += 1
        ins.then_inc(sem, 1)
        eng.wait_ge(sem, count[0])

    return link


def wait(eng, sem, value):
    if isinstance(value, int) and value <= 0:
        return
    eng.wait_ge(sem, value)


def peeled(eng, n, body, first=1, last=0):
    for i in range(first):
        body(i)
    with eng.Fori(first, n - last) as i:
        body(i)
    for i in range(n - last, n):
        body(i)


def is_first(i):
    return isinstance(i, int) and i == 0


def lagged(eng, steps, width, works, last=0):
    most = max(lag for lag, _ in works)

    def step(i):
        for u in range(width):
            for lag, work in works:
                back = -((u - lag) // width)
                if not (isinstance(i, int) and i < back):
                    work(i - back, u - lag + back * width)

    peeled(eng, steps, step, first=1 + most // width, last=last)
    for n in range(most):
        for lag, work in works:
            if n < lag:
                at = steps * width + n - lag
                work(at // width, at % width)


def constants():
    m = np.arange(HI)
    hb = P // LO
    c = {}
    c["ident"] = np.eye(P)
    e = np.arange(P)
    c["earlier"] = (e[None, :] < e[:, None]) * 1.0
    c["iota_hi"] = np.tile(np.arange(HI), (P, 1))
    c["iota_lo"] = np.tile(np.arange(LO), (P, 1))
    c["iota_p"] = np.tile(np.arange(P), (P, 1))
    c["pair_start"] = np.tile(np.arange(PAIRS) * 256, (P, 1))
    c["iota_slot"] = np.tile(np.arange(SLOTS), (P, 1))

    feature = np.arange(D // P)[None, :, None] * P + e[:, None, None]
    c["head_of_feature"] = (feature // DH == np.arange(H)[None, None, :]).reshape(P, -1) * 1.0

    def on_his(a):
        return np.concatenate([a, np.zeros((P - HI, a.shape[1]))])

    same = m[:, None] // hb == m[None, :] // hb
    c["same_block"] = on_his(same * 1.0)
    c["lower_in_block"] = on_his((same & (m[:, None] < m[None, :])) * 1.0)
    c["first_of_lower_block"] = on_his(((m[:, None] % hb == 0) & (m[:, None] // hb < m[None, :] // hb)) * 1.0)
    c["block_head"] = on_his(np.tile(((m % hb == 0) & (m > 0))[:, None] * 1.0, (1, P)))
    cols, at = [], {}
    n = 0
    for k, v in c.items():
        at[k] = (n, n + v.shape[1])
        n += v.shape[1]
        cols.append(v)
    return np.concatenate(cols, 1).astype(np.float32), at


CONSTS, CAT = constants()


class Const:

    def __init__(self, tile):
        self.t = tile

    def f(self, name, parts=P):
        a, b = CAT[name]
        return self.t[0:parts, a:b]


BASES, REL = 30, 2
BCH = 4
BW = 4096


class Basis:
    PIECES = D * D // BCH // BW
    STEPS = PIECES // 2

    def __init__(self, nc, name, basis, att, wtab):
        self.nc, self.name, self.att = nc, name, att
        self.src = basis.rearrange("b i o -> b (i o)").rearrange("b (c f) -> c b f", c=BCH)
        self.dst = wtab

    def begin(self, ctx, sem):
        nc, K = self.nc, BCH * BASES
        sb = lambda n, s, d: ctx.enter_context(nc.sbuf_tensor(f"{self.name}_{n}", s, d))
        self.mix = sb("mix", [K, 32], F32)
        self.piece = sb("piece", [K, 2, BW], F32)
        self.wout = sb("wout", [P, 2, 2, D], F32)
        self.ps = ctx.enter_context(nc.psum_tensor(f"{self.name}_ps", [P, 4, D], F32))
        self.zeroed, self.mixed = sem("mix_zeroed"), sem("mix_in")
        self.loaded = [sem(f"basis_loaded{k}") for k in range(2)]
        self.stored = [sem(f"basis_stored{k}") for k in range(2)]
        self.used, self.moved = sem("piece_used"), sem("basis_moved")

    def clear_mix(self):
        self.nc.vector.memset(self.mix[:, :], 0.0).then_inc(self.zeroed, 1)

    def load(self, eng):
        eng.wait_ge(self.zeroed, 1)
        with self.nc.allow_non_contiguous_dma("60 attention weights, once"):
            for c in range(BCH):
                for r in range(REL):
                    eng.dma_start(self.mix[c * BASES:(c + 1) * BASES, r * BCH + c:r * BCH + c + 1],
                                  self.att[r:r + 1, :].rearrange("r b -> b r")).then_inc(self.mixed, 16)

        def step(i):
            for k in range(2):
                wait(eng, self.used, (i * 2 + (k - 1)) * 2)
                for c in range(BCH):
                    eng.dma_start(self.piece[c * BASES:(c + 1) * BASES, k, :],
                                  self.src[c, :, bass.ds((i * 2 + k) * BW, BW)]).then_inc(self.loaded[k], 16)
        peeled(eng, self.STEPS, step)

    def start_multiply(self, pe):
        pe.wait_ge(self.mixed, 16 * BCH * REL)

    def multiply(self, pe, i, k):
        pe.wait_ge(self.loaded[k], (i + 1) * (16 * BCH))
        for s in range(2):
            wait(pe, self.moved, i * 4 + (k * 2 + s - 3))
            for q in range(4):
                f = (s * 4 + q) * D
                ins = self.nc.tensor.matmul(self.ps[32 * q:32 * q + 32, k * 2 + s, :], self.mix[:, :],
                                            self.piece[:, k, f:f + D], start=True, stop=True,
                                            skip_group_check=True)
            ins.then_inc(self.used, 1)

    def store(self, act):
        def step(i):
            for k in range(2):
                wait(act, self.stored[k], i * 64)
                for s in range(2):
                    act.wait_ge(self.used, i * 4 + (k * 2 + s + 1))
                    self.nc.scalar.copy(self.wout[:, k, s, :], self.ps[:, k * 2 + s, :]).then_inc(self.moved, 1)
                act.wait_ge(self.moved, i * 4 + (k * 2 + 2))
                for q in range(4):
                    act.dma_start(
                        self.dst[:, bass.ds((i * 2 + k) * BW, BW)].rearrange("r (s f) -> r s f", s=2)[:, :, q * D:(q + 1) * D],
                        self.wout[32 * q:32 * q + REL * BCH, k, :, :]).then_inc(self.stored[k], 16)
        peeled(act, self.STEPS, step)
        for k in range(2):
            act.wait_ge(self.stored[k], self.STEPS * 64)


def sort_edges(nc, name, C, identb, key, packed, extra, pair_block, block_f, sorted_out, basis=None):
    values = [0] if extra is None else [0, 1]
    with ExitStack() as ctx:
        sb = lambda n, s, d: ctx.enter_context(nc.sbuf_tensor(f"{name}_{n}", s, d))
        ki = sb("key_int", [EP, T], I32)
        ti = sb("int_tmp", [EP, T], I32)
        hif = sb("hi_f", [EP, T], F32)
        lof = sb("lo_f", [EP, T], F32)
        onehot = sb("onehot", [EP, T, KO], BF16)
        onehotT = sb("onehotT", [KO, T, EP], BF16)
        cnt = sb("cnt", [HI, LO, T], F32)
        inc = sb("inc", [HI, LO, T], F32)
        pre = sb("prefix_parts", [HI, 2, LO, T], BF16)
        rankin = sb("rank_in_tile", [EP, T], F32)
        rankto = sb("rank_to_tile", [EP, T], F32)
        tmp = sb("gather_tmp", [EP, GT, 2, LO], F32)
        small = sb("small", [HI, 8], F32)
        smalli = sb("small_i", [HI, 2], I32)
        atleast = sb("pair_at_least", [HI, PAIRS], F32)
        eqtmp = sb("eq_tmp", [EP, 4, EP], F32)
        pos_p, pos_s = sb("pos_partition", [EP, T], F32), sb("pos_slot", [EP, T], F32)
        value = sb("packed_value", [EP, T], F32)

        with ExitStack() as c1:
            sem = stage_semaphores(nc, c1, name)
            pt = c1.enter_context(nc.psum_tensor(f"{name}_pT", [KO, 2, 8, 128], BF16))
            pc = c1.enter_context(nc.psum_tensor(f"{name}_pC", [HI, GT, LO], F32))
            pe_ = c1.enter_context(nc.psum_tensor(f"{name}_pE", [EP, 4, 4, 128], F32))
            s_dve = sem("dve_chain")
            onehots_ready = sem("onehots_ready")
            transposed, counted, moved = sem("transposed"), sem("counted"), sem("moved")
            compared, ranked = sem("compared"), sem("ranked")
            block = c1.enter_context(nc.Block())

            G = T // GT

            @block.vector
            def _(v):
                link = chain(v, s_dve)
                link(nc.vector.tensor_copy(ki[:, :], key))
                link(nc.vector.tensor_single_scalar(ti[:, :], ki[:, :], LB, ALU.logical_shift_right))
                link(nc.vector.tensor_copy(hif[:, :], ti[:, :]))
                link(nc.vector.tensor_single_scalar(ti[:, :], ki[:, :], LO - 1, ALU.bitwise_and))
                link(nc.vector.tensor_copy(lof[:, :], ti[:, :]))

                def build(g, _):
                    for f, iota, a, n in ((hif, "iota_hi", 0, HI), (lof, "iota_lo", HI, LO)):
                        nc.vector.tensor_tensor(
                            onehot[:, bass.ds(g * GT, GT), a:a + n],
                            C.f(iota, EP).unsqueeze(1).to_broadcast([EP, GT, n]),
                            f[:, bass.ds(g * GT, GT)].unsqueeze(2).to_broadcast([EP, GT, n]), ALU.is_equal,
                        ).then_inc(onehots_ready, 1)

                def rank(g, _):
                    for u in range(GT):
                        if u % 4 == 0:
                            v.wait_ge(compared, g * 4 + (u // 4 + 1))
                        wait(v, ranked, g * GT + (u - 3))
                        nc.vector.scalar_tensor_tensor(
                            eqtmp[:, u % 4, :], pe_[:, u // 4, u % 4, 0:EP], 2.0,
                            C.f("earlier", EP)[:, 0:EP], ALU.is_equal, ALU.mult,
                            accum_out=rankin[:, bass.ds(g * GT + u, 1)]).then_inc(ranked, 1)

                lagged(v, G, 1, [(0, build), (2, rank)])

            @block.tensor
            def _(pe):
                def turn(g, _):
                    pe.wait_ge(onehots_ready, g * 2 + 2)
                    wait(pe, moved, g * 3)
                    for u in range(GT):
                        ins = nc.tensor.transpose(
                            pt[:, u // 8, u % 8, 0:EP],
                            onehot[:, bass.ds(g * GT + u, 1), :].rearrange("p a n -> p (a n)"),
                            identb[0:EP, 0:EP])
                        if u % 8 == 7:
                            ins.then_inc(transposed, 1)
                    for u in range(GT):
                        oh = onehot[:, bass.ds(g * GT + u, 1), :].rearrange("p a n -> p (a n)")
                        ins = nc.tensor.matmul(pc[:, u, :], oh[:, 0:HI], oh[:, HI:KO],
                                               start=True, stop=True)
                    ins.then_inc(counted, 1)

                def compare(g, _):
                    pe.wait_ge(moved, g * 3 + 2)
                    for u in range(GT):
                        if u % 4 == 0:
                            wait(pe, ranked, g * GT + (u + 4 - GT))
                        oh = onehotT[:, bass.ds(g * GT + u, 1), :].rearrange("p a n -> p (a n)")
                        ins = nc.tensor.matmul(pe_[:, u // 4, u % 4, 0:EP], oh, oh, start=True, stop=True)
                        if u % 4 == 3:
                            ins.then_inc(compared, 1)

                lagged(pe, G, 1, [(0, turn), (1, compare)])

            @block.scalar
            def _(act):
                with act.Fori(0, G) as g:
                    for w in range(2):
                        act.wait_ge(transposed, g * 2 + (w + 1))
                        nc.scalar.copy(
                            onehotT[:, bass.ds(g * GT + w * 8, 8), :], pt[:, w, :, 0:EP]).then_inc(moved, 1)
                    act.wait_ge(counted, g + 1)
                    nc.scalar.copy(cnt[:, :, bass.ds(g * GT, GT)].rearrange("p l t -> p t l"),
                                   pc[:, :, :]).then_inc(moved, 1)

        with ExitStack() as c1:
            sem = stage_semaphores(nc, c1, name)
            ps = c1.enter_context(nc.psum_tensor(f"{name}_pS", [HI, 4], F32))
            pp = c1.enter_context(nc.psum_tensor(f"{name}_pP", [P, PAIRS], F32))
            pg = c1.enter_context(nc.psum_tensor(f"{name}_pG", [EP, 2, GT, 2, LO], F32))
            s_dve, summed = sem("dve_chain"), sem("summed")
            tot_ready, pads_ready, prefix_ready, pairs_ready = (
                sem("tot_ready"), sem("pads_ready"), sem("prefix_ready"), sem("pairs_ready"))
            gathered, taken, s_red = sem("gathered"), sem("taken"), sem("reduced")
            block = c1.enter_context(nc.Block())

            @block.vector
            def _(v):
                link = chain(v, s_dve)
                flat = lambda a: a[:, :, :].rearrange("p l t -> p (l t)")
                link(nc.vector.memset(small[:, 1:2], 0.0))
                nc.vector.tensor_tensor_scan(flat(inc), flat(cnt),
                                             small[:, 1:2].to_broadcast([HI, LO * T]), 0.0,
                                             ALU.add, ALU.add).then_inc(tot_ready, 1)
                v.wait_ge(summed, 1)
                link(nc.vector.tensor_scalar(smalli[:, 0:1], ps[:, 0:1], 255.0, None, ALU.add))
                link(nc.vector.tensor_scalar(smalli[:, 1:2], smalli[:, 0:1], 8, 8,
                                             ALU.logical_shift_right, ALU.logical_shift_left))
                nc.vector.tensor_copy(small[:, 2:3], smalli[:, 1:2]).then_inc(pads_ready, 1)
                v.wait_ge(summed, 2)
                link(nc.vector.tensor_copy(small[:, 4:6], ps[:, 1:3]))
                link(nc.vector.tensor_tensor(small[:, 3:4], small[:, 4:5], small[:, 5:6], ALU.add))
                nc.vector.tensor_scalar(atleast[:, :], C.f("pair_start", HI), small[:, 5:6], None,
                                        ALU.is_ge).then_inc(pairs_ready, 1)
                link(nc.vector.scalar_tensor_tensor(flat(inc), flat(inc), small[:, 3:4], flat(cnt),
                                                    ALU.add, ALU.subtract))
                parts = [pre[:, n, :, :].rearrange("p l t -> p (l t)") for n in range(2)]
                link(nc.vector.tensor_copy(parts[0], flat(inc)))
                nc.vector.tensor_tensor(parts[1], flat(inc), parts[0],
                                        ALU.subtract).then_inc(prefix_ready, 1)
                v.wait_ge(summed, 3)
                nc.vector.tensor_copy(pair_block, pp[0:1, :])
                nc.vector.tensor_copy(block_f, pp[:, :])
                with v.Fori(0, T // GT // 2) as g:
                    for w in range(2):
                        v.wait_ge(gathered, g * 2 + (w + 1))
                        nc.vector.tensor_tensor(
                            tmp[:, :, :, :], pg[:, w, :, :, :],
                            onehot[:, bass.ds(g * 2 * GT + w * GT, GT), HI:KO].unsqueeze(2).to_broadcast([EP, GT, 2, LO]),
                            ALU.mult).then_inc(taken, 1)
                        v.wait_ge(taken, g * 2 + (w + 1))
                        nc.vector.tensor_reduce(rankto[:, bass.ds(g * 2 * GT + w * GT, GT)],
                                                tmp[:, :, :, :].rearrange("p t n l -> p t (n l)"), AX.X, ALU.add).then_inc(s_red, 1)
                        v.wait_ge(s_red, g * 2 + (w + 1))
                link(nc.vector.tensor_tensor(ki[:, :], rankto[:, :], rankin[:, :], ALU.add))
                link(nc.vector.tensor_single_scalar(ti[:, :], ki[:, :], P - 1, ALU.bitwise_and))
                link(nc.vector.tensor_copy(pos_p[:, :], ti[:, :]))
                link(nc.vector.tensor_single_scalar(ti[:, :], ki[:, :], 7, ALU.logical_shift_right))
                link(nc.vector.tensor_copy(pos_s[:, :], ti[:, :]))
                link(nc.vector.tensor_copy(ki[:, :], key))
                link(nc.vector.tensor_single_scalar(ti[:, :], ki[:, :], P - 1, ALU.bitwise_and))
                link(nc.vector.tensor_scalar(value[:, :], ti[:, :], 1.0, None, ALU.add))
                for f, factor in packed:
                    link(nc.vector.scalar_tensor_tensor(value[:, :], f, float(factor), value[:, :],
                                                        ALU.mult, ALU.add))

            @block.tensor
            def _(pe):
                pe.wait_ge(tot_ready, 1)
                total = inc[:, LO - 1, T - 1:T]
                nc.tensor.matmul(ps[:, 0:1], C.f("same_block", HI), total, start=True, stop=True
                                 ).then_inc(summed, 1)
                pe.wait_ge(pads_ready, 1)
                nc.tensor.matmul(ps[:, 1:2], C.f("lower_in_block", HI), total, start=True, stop=True)
                nc.tensor.matmul(ps[:, 2:3], C.f("first_of_lower_block", HI), small[:, 2:3],
                                 start=True, stop=True).then_inc(summed, 1)
                pe.wait_ge(pairs_ready, 1)
                nc.tensor.matmul(pp[:, :], C.f("block_head", HI), atleast[:, :], start=True, stop=True
                                 ).then_inc(summed, 1)
                pe.wait_ge(prefix_ready, 1)

                def step(g):
                    for w in range(2):
                        wait(pe, taken, g * 2 + (w - 1))
                        for u in range(GT):
                            t = g * 2 * GT + (w * GT + u)
                            oh = onehotT[0:HI, bass.ds(t, 1), :].rearrange("p a n -> p (a n)")
                            ins = nc.tensor.matmul(
                                pg[:, w, u, :, :].rearrange("p n l -> p (n l)"), oh,
                                pre[:, :, :, bass.ds(t, 1)].rearrange("p n l a -> p (n l a)"), start=True, stop=True)
                        ins.then_inc(gathered, 1)
                peeled(pe, T // GT // 2, step)

        RING, STEP = 4, 8 if basis is None else T // Basis.STEPS
        with ExitStack() as c1:
            sem = stage_semaphores(nc, c1, name)
            onp = c1.enter_context(nc.sbuf_tensor(f"{name}_onehot_p", [EP, RING, P], F32))
            ons = c1.enter_context(nc.sbuf_tensor(f"{name}_onehot_s", [EP, RING, 2, SLOTS], F32))
            po = c1.enter_context(nc.psum_tensor(f"{name}_pO", [P, 2, D], F32))
            built, placed = sem("built"), sem("placed")
            if basis:
                basis.begin(c1, sem)
            block = c1.enter_context(nc.Block())

            if basis:
                @block.sync
                def _(sp):
                    basis.load(sp)

                @block.scalar
                def _(act):
                    basis.store(act)

            @block.vector
            def _(v):
                if basis:
                    basis.clear_mix()

                def step(i):
                    for u in range(STEP):
                        k = u % RING
                        t = i * STEP + u
                        wait(v, placed, i * STEP + (u + 1 - RING))
                        nc.vector.tensor_scalar(onp[:, k, :], C.f("iota_p", EP), pos_p[:, bass.ds(t, 1)], None,
                                                ALU.is_equal)
                        if extra is not None:
                            nc.vector.tensor_scalar(ons[:, k, 1, :], C.f("iota_slot", EP), pos_s[:, bass.ds(t, 1)],
                                                    extra[:, bass.ds(t, 1)], ALU.is_equal, ALU.mult)
                        nc.vector.tensor_scalar(ons[:, k, 0, :], C.f("iota_slot", EP), pos_s[:, bass.ds(t, 1)],
                                                value[:, bass.ds(t, 1)], ALU.is_equal, ALU.mult).then_inc(built, 1)
                peeled(v, T // STEP, step)
                v.wait_ge(placed, T)
                for n in values:
                    nc.vector.tensor_copy(sorted_out[n], po[:, n, 0:SLOTS])

            @block.tensor
            def _(pe):
                def step(i, first=False, last=False):
                    for u in range(STEP):
                        pe.wait_ge(built, i * STEP + (u + 1))
                        for n in values:
                            ins = nc.tensor.matmul(po[:, n, 0:SLOTS], onp[:, u % RING, :], ons[:, u % RING, n, :],
                                                   start=first and u == 0, stop=last and u == STEP - 1)
                        ins.then_inc(placed, 1)
                        if basis and u % (STEP // 2) == STEP // 2 - 1:
                            if first and u < STEP // 2:
                                basis.start_multiply(pe)
                            basis.multiply(pe, i, u // (STEP // 2))
                step(0, first=True)
                with pe.Fori(1, T // STEP - 1) as i:
                    step(i)
                step(T // STEP - 1, last=True)


def flat(ap):
    return ap.rearrange("p a n -> p (a n)")


BODYP = 8
NSTEP = PAIRS // BODYP


def edge_pass(nc, name, C, table, idx, loc, pair_block, acc, weight=None, side=None, own=None, fetch=(), shift=None):
    ns = H + 1 if weight is not None else 0
    assert NB <= NSTEP - 1
    with ExitStack() as ctx:
        sb = lambda n, s, d: ctx.enter_context(nc.sbuf_tensor(f"{name}_{n}", s, d))
        ps = lambda n, s, d: ctx.enter_context(nc.psum_tensor(f"{name}_{n}", s, d))
        sem = stage_semaphores(nc, ctx, name)
        rows = sb("rows", [P, BODYP, 2, D], F32)
        idxr = sb("idx_ring", [P, 2, 8], I32)
        ohr = sb("onehot_ring", [P, 4, 2, P], F32)
        pS = ps("pS", [P, 4, D], F32)
        pN = ps("pN", [P, 4, D], F32) if ns else None
        pR = ps("pR", [P, D], F32) if own else None
        xs = sb("xT_block", [P, 4, P], F32)
        idx_copied, sent = sem("idx_copied"), sem("sent")
        got = [sem(f"got{q}") for q in range(BODYP)]
        zeroed, built, weighted = sem("zeroed"), sem("onehot_built"), sem("weighted")
        summed, added, nadded = sem("summed"), sem("added"), sem("nadded")
        x_copied, multiplied, kept, fetched = sem("x_copied"), sem("own_multiplied"), sem("own_kept"), sem("fetched")
        shifted = sem("shifted")
        block = ctx.enter_context(nc.Block())

        def has_block(i):
            return own and not (isinstance(i, int) and i == NSTEP - 1)

        @block.sync
        def _(sp):
            for tile, source in fetch:
                sp.dma_start(tile, source).then_inc(fetched, 16)
            if fetch:
                sp.wait_ge(fetched, 16 * len(fetch))

        @block.gpsimd
        def _(pool):
            def step(i):
                for half in range(2):
                    pool.wait_ge(idx_copied, i * 2 + (half + 1))
                    for q in range(half * 4, half * 4 + 4):
                        wait(pool, summed, i * BODYP + (q + 1 - BODYP))
                        pool.sem_inc(sent, 1)
                        for s in range(2):
                            n = (q % 4) * 2 + s
                            pool.indirect_dma_start(rows[:, q, s, :], None, table,
                                                    bass.IndirectOffsetOnAxis(idxr[:, half, n:n + 1], 0)
                                                    ).then_inc(got[q], 16)
            peeled(pool, NSTEP, step)

        @block.vector
        def _(v):
            nc.vector.memset(acc[:, :, :], 0.0).then_inc(zeroed, 1)
            if ns:
                nc.vector.memset(side[:, :, :], 0.0).then_inc(zeroed, 1)
            v.wait_ge(zeroed, 1 + (ns > 0))

            def build(i, u):
                wait(v, summed, i * BODYP + (u - 3))
                nc.vector.tensor_tensor(
                    ohr[:, u % 4, :, :], C.f("iota_p").unsqueeze(1).to_broadcast([P, 2, P]),
                    loc[:, bass.ds(i * 16 + u * 2, 2)].unsqueeze(2).to_broadcast([P, 2, P]),
                    ALU.is_equal).then_inc(built, 1)

            def multiply(i, u):
                v.wait_ge(got[u], (i + 1) * 32)
                r = rows[:, u, :, :].rearrange("p s (h d) -> p s h d", h=H)
                nc.vector.tensor_tensor(
                    r, r, weight[:, bass.ds(i * 16 + u * 2, 2), 0:H].unsqueeze(3).to_broadcast([P, 2, H, DH]),
                    ALU.mult).then_inc(weighted, 1)

            def accumulate(i, u):
                j = i * BODYP + u
                b = v.value_load(pair_block[0:1, bass.ds(j, 1)], min_val=0, max_val=NB - 1)
                v.wait_ge(summed, j + 1)
                wait(v, added, j)
                a = flat(acc[:, bass.ds(b, 1), :])
                nc.vector.tensor_tensor(a, pS[:, u % 4, :], a, ALU.add).then_inc(added, 1)
                if ns:
                    wait(v, nadded, j)
                    a = flat(side[:, bass.ds(b, 1), :])
                    nc.vector.tensor_tensor(a, pN[:, u % 4, 0:ns], a, ALU.add).then_inc(nadded, 1)

            def keep_own(i, u):
                if u == BODYP - 1 and has_block(i):
                    v.wait_ge(multiplied, i + 1)
                    term = own[2]
                    if shift and term is shift[0]:
                        term = flat(term[:, bass.ds(i, 1), :])
                        v.wait_ge(shifted, i + 1)
                    nc.vector.tensor_tensor(flat(own[3][:, bass.ds(i, 1), :]), pR[:, :], term,
                                            ALU.add).then_inc(kept, 1)
                if u == 2 and shift and has_block(i):
                    x = flat(shift[0][:, bass.ds(i, 1), :])
                    nc.vector.tensor_tensor(x, x, shift[1], ALU.add).then_inc(shifted, 1)

            lagged(v, NSTEP, BODYP, [(0, build)] + ([(0, multiply)] if ns else []) + [(2, accumulate), (0, keep_own)],
                   last=1)

        @block.scalar
        def _(act):
            def step(i):
                for half in range(2):
                    for q in range(half * 4, half * 4 + 4):
                        wait(act, got[q], i * 32)
                    nc.scalar.copy(idxr[:, half, :],
                                   idx[:, bass.ds(i * 16 + half * 8, 8)]).then_inc(idx_copied, 1)
                if has_block(i):
                    wait(act, multiplied, i)
                    nc.scalar.copy(xs[:, :, :], own[0][:, bass.ds(i, 1), :, :].rearrange("p a c n -> p (a c) n")
                                   ).then_inc(x_copied, 1)
            peeled(act, NSTEP, step, last=1)

        @block.tensor
        def _(pe):
            def scatter(i, u):
                j = i * BODYP + u
                pe.wait_ge(built, j + 1)
                if ns:
                    pe.wait_ge(weighted, j + 1)
                    wait(pe, nadded, j - 3)
                else:
                    pe.wait_ge(got[u], (i + 1) * 32)
                wait(pe, added, j - 3)
                for s in range(2):
                    ins = nc.tensor.matmul(pS[:, u % 4, :], ohr[:, u % 4, s, :], rows[:, u, s, :],
                                           start=s == 0, stop=s == 1)
                    if ns:
                        ins = nc.tensor.matmul(
                            pN[:, u % 4, 0:ns], ohr[:, u % 4, s, :],
                            weight[:, bass.ds(i * 16 + (u * 2 + s), 1), :].rearrange("p a h -> p (a h)"),
                            start=s == 0, stop=s == 1)
                ins.then_inc(summed, 1)

            def multiply_own(i, u):
                if u == BODYP // 2 and has_block(i):
                    pe.wait_ge(x_copied, i + 1)
                    wait(pe, kept, i)
                    for c in range(4):
                        ins = nc.tensor.matmul(pR[:, :], xs[:, c, :], own[1][:, c, :], start=c == 0, stop=c == 3)
                    ins.then_inc(multiplied, 1)

            lagged(pe, NSTEP, BODYP, [(0, multiply_own), (0, scatter)], last=1)


def edge_convolution(nc, name, C, identb, p_parts, q_table, idx, loc, pair_block, acc):
    RING, FR = BODYP, mybir.dt.float32r
    with ExitStack() as ctx:
        sb = lambda n, s, d: ctx.enter_context(nc.sbuf_tensor(f"{name}_{n}", s, d))
        ps = lambda n, s, d: ctx.enter_context(nc.psum_tensor(f"{name}_{n}", s, d))
        sem = stage_semaphores(nc, ctx, name)
        rows = sb("rows", [P, RING, 2, D], F32)
        idxr = sb("idx_ring", [P, 2, 8], I32)
        ohb = sb("onehot_bf16", [P, 4, 2, P], BF16)
        ohf = sb("onehot_f32", [P, RING, 2, P], F32)
        ohT = sb("onehotT", [P, 2, 2, P], FR)
        pT = ps("pT", [P, 2, 8, P], BF16)
        pP = ps("pP", [P, 2, 2, D], F32)
        pS = ps("pS", [P, 2, D], F32)
        idx_copied, sent = sem("idx_copied"), sem("sent")
        got = [sem(f"got{q}") for q in range(RING)]
        built, turned, turned_out, widened = (
            sem("onehot_built"), sem("turned"), sem("turned_out"), sem("onehot_widened"))
        looked, summand, relued, summed, added = sem("looked"), sem("summand"), sem("relued"), sem("summed"), sem("added")
        block = ctx.enter_context(nc.Block())

        @block.gpsimd
        def _(pool):
            def step(i):
                for half in range(2):
                    for q in range(half * 4, half * 4 + 4):
                        wait(pool, got[q], i * 32)
                    nc.gpsimd.tensor_copy(idxr[:, half, :],
                                          idx[:, bass.ds(i * 16 + half * 8, 8)]).then_inc(idx_copied, 1)
                    pool.wait_ge(idx_copied, i * 2 + (half + 1))
                    for q in range(half * 4, half * 4 + 4):
                        wait(pool, summed, i * RING + (q + 1 - RING))
                        pool.sem_inc(sent, 1)
                        for s in range(2):
                            n = (q % 4) * 2 + s
                            pool.indirect_dma_start(rows[:, q, s, :], None, q_table,
                                                    bass.IndirectOffsetOnAxis(idxr[:, half, n:n + 1], 0)
                                                    ).then_inc(got[q], 16)
            peeled(pool, NSTEP, step)

        @block.vector
        def _(v):
            def build(i, u):
                j = i * BODYP + u
                wait(v, turned, j - 3)
                wait(v, widened, j - 3)
                nc.vector.tensor_tensor(
                    ohb[:, u % 4, :, :], C.f("iota_p").unsqueeze(1).to_broadcast([P, 2, P]),
                    loc[:, bass.ds(i * 16 + u * 2, 2)].unsqueeze(2).to_broadcast([P, 2, P]),
                    ALU.is_equal).then_inc(built, 1)

            def add(i, u):
                v.wait_ge(got[u], (i + 1) * 32)
                v.wait_ge(looked, i * BODYP + (u + 1))
                nc.vector.tensor_tensor(rows[:, u, :, :], rows[:, u, :, :], pP[:, u % 2, :, :],
                                        ALU.add).then_inc(summand, 1)

            def accumulate(i, u):
                j = i * BODYP + u
                b = v.value_load(pair_block[0:1, bass.ds(j, 1)], min_val=0, max_val=NB - 1)
                v.wait_ge(summed, j + 1)
                wait(v, added, j)
                a = flat(acc[:, bass.ds(b, 1), :])
                nc.vector.tensor_tensor(a, pS[:, u % 2, :], a, ALU.add).then_inc(added, 1)

            lagged(v, NSTEP, BODYP, [(0, build), (2, add), (4, accumulate)])

        @block.scalar
        def _(act):
            def evacuate(i, u):
                j = i * BODYP + u
                act.wait_ge(turned, j + 1)
                wait(act, looked, j - 1)
                nc.scalar.copy(ohT[:, u % 2, :, :], pT[:, u % 2, 0:2, :]).then_inc(turned_out, 1)
                wait(act, summed, j + (1 - RING))
                nc.scalar.copy(ohf[:, u, :, :], ohb[:, u % 4, :, :]).then_inc(widened, 1)

            def relu(i, u):
                act.wait_ge(summand, i * BODYP + (u + 1))
                nc.scalar.activation(rows[:, u, :, :], rows[:, u, :, :], ACT.Relu).then_inc(relued, 1)

            lagged(act, NSTEP, BODYP, [(0, evacuate), (2, relu)])

        @block.tensor
        def _(pe):
            def turn(i, u):
                j = i * BODYP + u
                pe.wait_ge(built, j + 1)
                wait(pe, turned_out, j - 1)
                for s in range(2):
                    ins = nc.tensor.transpose(pT[:, u % 2, s, :], ohb[:, u % 4, s, :], identb[:, :])
                ins.then_inc(turned, 1)

            def look(i, u):
                j = i * BODYP + u
                b = pe.value_load(pair_block[0:1, bass.ds(j, 1)], min_val=0, max_val=NB - 1)
                pe.wait_ge(turned_out, j + 1)
                wait(pe, summand, j - 1)
                for s in range(2):
                    for n in range(2):
                        ins = nc.tensor.matmul(pP[:, u % 2, s, :], ohT[:, u % 2, s, :],
                                               flat(p_parts[n][:, bass.ds(b, 1), :]), start=n == 0, stop=n == 1)
                ins.then_inc(looked, 1)

            def scatter(i, u):
                j = i * BODYP + u
                pe.wait_ge(widened, j + 1)
                pe.wait_ge(relued, j + 1)
                wait(pe, added, j - 1)
                for s in range(2):
                    ins = nc.tensor.matmul(pS[:, u % 2, :], ohf[:, u, s, :], rows[:, u, s, :],
                                           start=s == 0, stop=s == 1)
                ins.then_inc(summed, 1)

            lagged(pe, NSTEP, BODYP, [(0, turn), (1, look), (3, scatter)])


UPPER = -1 << 12


class BlockChain:

    def __init__(self, eng, sem, waited):
        self.eng, self.sem, self.waited, self.length = eng, sem, waited, None

    def begin(self, b):
        self.base, self.count = (0 if self.length is None else b * self.length), 0

    def end(self):
        if self.length is None:
            self.length = self.count
        assert self.length == self.count

    def __call__(self, ins):
        self.count += 1
        ins.then_inc(self.sem, 1)
        self.eng.wait_ge(self.sem, self.base + self.count)

    def take_wait(self):
        self.eng.sem_inc(self.waited, 1)


class Normal:

    def __init__(self, nc, ctx, sem, name, per_block):
        sb = lambda n, w: ctx.enter_context(nc.sbuf_tensor(f"{name}_{n}", [P, w], F32))
        self.nc, self.per_block = nc, per_block
        self.bn, self.mv, self.var, self.sd, self.rstd = sb("bn", 6), sb("mv", 2), sb("var", 1), sb("sd", 1), sb("rstd", 1)
        self.var_ready, self.sd_ready = sem("var_ready"), sem("sd_ready")

    def stats(self, link, v, b, n, src):
        nc = self.nc
        link.take_wait()
        link(nc.vector.bn_stats(self.bn[:, :], src))
        link.take_wait()
        link(nc.vector.bn_aggr(self.mv[:, :], self.bn[:, :]))
        nc.vector.tensor_scalar(self.var[:, :], self.mv[:, 1:2], 1e-5, None, ALU.add).then_inc(self.var_ready, 1)
        v.wait_ge(self.sd_ready, b * self.per_block + (n + 1))
        link(nc.vector.reciprocal(self.rstd[:, :], self.sd[:, :]))

    def apply(self, out, src):
        return self.nc.vector.tensor_scalar(out, src, self.mv[:, 0:1], self.rstd[:, 0:1], ALU.subtract, ALU.mult)

    def roots(self, act, b):
        for n in range(self.per_block):
            act.wait_ge(self.var_ready, b * self.per_block + (n + 1))
            self.nc.scalar.activation(self.sd[:, :], self.var[:, :], ACT.Sqrt).then_inc(self.sd_ready, 1)


def node_stage(nc, name, X, ident, prepare, n_stats, weights, save, targets, narrow=None,
               keep_xT=None, ahead=None):
    nw = len(weights)
    with ExitStack() as ctx:
        sb = lambda n, s, d: ctx.enter_context(nc.sbuf_tensor(f"{name}_{n}", s, d))
        sem = stage_semaphores(nc, ctx, name)
        xn = sb("x_block", [P, 2, D], F32)
        xt = sb("xT_block", [P, 2, 4, P], F32)
        yr = sb("y_ring", [P, 2, nw, D], F32)
        tmp, upper = sb("tmp", [P, D], F32), sb("upper_bits", [P, D], I32)
        nn = narrow[0].shape[2] if narrow else 0
        gates = sb("gates", [P, 2, REL], F32)
        pt = ctx.enter_context(nc.psum_tensor(f"{name}_pT", [P, 4, P], F32))
        py = ctx.enter_context(nc.psum_tensor(f"{name}_pY", [P, 2, nw, D], F32))
        pn = ctx.enter_context(nc.psum_tensor(f"{name}_pN", [P, 2, nn], F32)) if narrow else None
        normal = Normal(nc, ctx, sem, name, n_stats)
        s_dve, waited = sem("dve_chain"), sem("waited")
        normed, saved, transposed, xcopied = sem("normed"), sem("saved"), sem("transposed"), sem("xcopied")
        multiplied, dve_out, act_out, s_tmp = sem("multiplied"), sem("dve_out"), sem("act_out"), sem("s_tmp")
        gated = sem("gated")
        stored = [sem(f"stored{k}") for k in range(2)]
        on_dve = [w for w, (_, kind, _) in enumerate(weights) if kind == "bias_split"]
        on_act = [w for w, (_, kind, _) in enumerate(weights) if kind in ("table", "gated")]
        tabled = [w for w, (_, kind, _) in enumerate(weights) if not kind.startswith("bias")]
        n_dve = len(on_dve)
        begun, went_ahead, s_pool = sem("begun"), sem("went_ahead"), sem("pool_waited")
        block = ctx.enter_context(nc.Block())

        def two_behind(eng, first, second):
            def step(i):
                for k in range(2):
                    first(i * 2 + k, k)
                    if not is_first(i):
                        second(i * 2 + (k - 2), k, i - 1)
            peeled(eng, NB // 2, step, 2)
            for k in range(2):
                second(NB - 2 + k, k, NB // 2 - 1)

        @block.vector
        def _(v):
            link = BlockChain(v, s_dve, waited)
            if ahead:
                ahead[0](v, begun)

            def norm(b, k):
                wait(v, transposed, b - 1)
                if save:
                    wait(v, saved, b - 1)
                if ahead:
                    v.wait_ge(went_ahead, b + 1)
                link.begin(b)
                prepare(link, v, normal, b, xn[:, k, :], *([k] if ahead else [])).then_inc(normed, 1)
                link.end()

            def finish(b, k, rounds):
                v.wait_ge(multiplied, b + 1)
                for w in on_dve:
                    bias, parts = weights[w][2]
                    high, low = (flat(part[:, bass.ds(b, 1), :]) for part in parts)
                    wait(v, dve_out, b)
                    nc.vector.tensor_tensor(tmp[:, :], py[:, k, w, :], bias, ALU.add).then_inc(s_tmp, 1)
                    v.wait_ge(s_tmp, b * 2 + 1)
                    nc.vector.tensor_single_scalar(upper[:, :], tmp[:, :].bitcast(I32), UPPER, ALU.bitwise_and
                                                   ).then_inc(s_tmp, 1)
                    v.wait_ge(s_tmp, b * 2 + 2)
                    nc.vector.tensor_scalar(high, upper[:, :].bitcast(F32), 1.0, None, ALU.mult)
                    nc.vector.tensor_tensor(low, tmp[:, :], upper[:, :].bitcast(F32), ALU.subtract
                                            ).then_inc(dve_out, 1)

            two_behind(v, norm, finish)

        if ahead:
            @block.gpsimd
            def _(pool):
                def step(i):
                    for k in range(2):
                        b = i * 2 + k
                        wait(pool, normed, b - 1)
                        pool.sem_inc(s_pool, 1)
                        ahead[1](b, k).then_inc(went_ahead, 1)
                pool.wait_ge(begun, 1)
                peeled(pool, NB // 2, step, 2)

        @block.tensor
        def _(pe):
            def turn(b, k):
                pe.wait_ge(normed, b + 1)
                wait(pe, xcopied, b)
                for c in range(4):
                    ins = nc.tensor.transpose(pt[:, c, :], xn[:, k, c * P:(c + 1) * P], ident)
                ins.then_inc(transposed, 1)

            def multiply(b, k):
                pe.wait_ge(xcopied, b + 1)
                if n_dve:
                    wait(pe, dve_out, b - 1)
                wait(pe, act_out, b - 1)
                for w in range(nw):
                    for c in range(4):
                        ins = nc.tensor.matmul(py[:, k, w, :], xt[:, k, c, :], weights[w][0][:, c, :],
                                               start=c == 0, stop=c == 3)
                if narrow:
                    wait(pe, gated, b)
                    for c in range(4):
                        ins = nc.tensor.matmul(pn[:, k, :], xt[:, k, c, :], narrow[0][:, c, :],
                                               start=c == 0, stop=c == 3)
                ins.then_inc(multiplied, 1)

            def step(i):
                for k in range(2):
                    turn(i * 2 + k, k)
                    if k or not is_first(i):
                        multiply(i * 2 + (k - 1), 1 - k)
            peeled(pe, NB // 2, step, 2)
            multiply(NB - 1, 1)

        @block.scalar
        def _(act):
            def copy_x(b, k):
                act.wait_ge(transposed, b + 1)
                wait(act, multiplied, b - 1)
                if keep_xT is not None:
                    nc.scalar.copy(keep_xT[:, bass.ds(b, 1), :, :].rearrange("p a c n -> p (a c) n"), pt[:, :, :])
                nc.scalar.copy(xt[:, k, :, :], pt[:, :, :]).then_inc(xcopied, 1)
                if save:
                    nc.scalar.copy(flat(X[:, bass.ds(b, 1), :]), xn[:, k, :]).then_inc(saved, 1)

            def finish(b, k, rounds):
                act.wait_ge(multiplied, b + 1)
                if narrow and narrow[1] is None:
                    nc.scalar.activation(gates[:, k, :], pn[:, k, :], ACT.Sigmoid).then_inc(gated, 1)
                    act.wait_ge(gated, b + 1)
                elif narrow:
                    for m, half in enumerate(narrow[1]):
                        ins = nc.scalar.copy(flat(half[:, bass.ds(b, 1), :]), pn[:, k, m * nn // 2:(m + 1) * nn // 2])
                    ins.then_inc(gated, 1)
                if on_act:
                    wait(act, stored[k], rounds * (16 * len(tabled)))
                for w in on_act:
                    _, kind, extra = weights[w]
                    scale = gates[:, k, extra:extra + 1] if kind == "gated" else 1.0
                    ins = nc.scalar.activation(yr[:, k, w, :], py[:, k, w, :], ACT.Copy, scale=scale)
                ins.then_inc(act_out, 1)

            def step(i):
                for k in range(2):
                    normal.roots(act, i * 2 + k)
                    if not is_first(i):
                        finish(i * 2 + (k - 2), k, i - 1)
                    copy_x(i * 2 + k, k)
            peeled(act, NB // 2, step, 2)
            for k in range(2):
                finish(NB - 2 + k, k, NB // 2 - 1)

        @block.sync
        def _(sp):
            with sp.Fori(0, NB // 2) as i:
                for k in range(2):
                    b = i * 2 + k
                    rows = sp.snap(b * P)
                    if n_dve:
                        sp.wait_ge(dve_out, b + 1)
                    sp.wait_ge(act_out, b + 1)
                    for w in tabled:
                        sp.dma_start(targets[w][bass.ds(rows, P), :], yr[:, k, w, :]).then_inc(stored[k], 16)
            for k in range(2):
                sp.wait_ge(stored[k], NB // 2 * 16 * len(tabled))


def last_norm(nc, name, acc, held, out):
    with ExitStack() as ctx:
        sb = lambda n, s: ctx.enter_context(nc.sbuf_tensor(f"{name}_{n}", s, F32))
        sem = stage_semaphores(nc, ctx, name)
        bn, mv = sb("bn", [P, NB, 6]), sb("mv", [P, NB, 2])
        var, sd, rstd = sb("var", [P, NB]), sb("sd", [P, NB]), sb("rstd", [P, NB])
        added, measured, aggregated, waited = sem("added"), sem("measured"), sem("aggregated"), sem("waited")
        var_ready, sd_ready, rstd_ready, final, stored = (
            sem("var_ready"), sem("sd_ready"), sem("rstd_ready"), sem("final"), sem("stored"))
        block = ctx.enter_context(nc.Block())

        def rows_of(tile, b):
            return flat(tile[:, bass.ds(b, 1), :])

        @block.vector
        def _(v):
            def add(b, _):
                nc.vector.tensor_tensor(rows_of(acc, b), rows_of(acc, b), rows_of(held, b), ALU.add).then_inc(added, 1)

            def measure(b, _):
                v.wait_ge(added, b + 1)
                v.sem_inc(waited, 1)
                nc.vector.bn_stats(rows_of(bn, b), rows_of(acc, b)).then_inc(measured, 1)

            lagged(v, NB, 1, [(0, add), (1, measure)])
            v.wait_ge(measured, NB)
            for b in range(NB):
                ins = nc.vector.bn_aggr(mv[:, b, :], bn[:, b, :])
            ins.then_inc(aggregated, 1)
            v.wait_ge(aggregated, 1)
            nc.vector.tensor_scalar(var[:, :], mv[:, :, 1], 1e-5, None, ALU.add).then_inc(var_ready, 1)
            v.wait_ge(sd_ready, 1)
            nc.vector.reciprocal(rstd[:, :], sd[:, :]).then_inc(rstd_ready, 1)
            v.wait_ge(rstd_ready, 1)
            with v.Fori(0, NB) as b:
                nc.vector.tensor_scalar(rows_of(acc, b), rows_of(acc, b), mv[:, bass.ds(b, 1), 0],
                                        rstd[:, bass.ds(b, 1)], ALU.subtract, ALU.mult).then_inc(final, 1)

        @block.scalar
        def _(act):
            act.wait_ge(var_ready, 1)
            nc.scalar.activation(sd[:, :], var[:, :], ACT.Sqrt).then_inc(sd_ready, 1)

        @block.sync
        def _(sp):
            with sp.Fori(0, NB - 1) as b:
                at, n = sp.snap(b * P), sp.snap(b)
                sp.wait_ge(final, b + 1)
                sp.dma_start(out[bass.ds(at, P), :], flat(acc[:, bass.ds(n, 1), :])).then_inc(stored, 16)
            sp.wait_ge(final, NB)
            at = (NB - 1) * P
            sp.dma_start(out[at:N, :], acc[0:N - at, NB - 1, :]).then_inc(stored, 16)
            sp.wait_ge(stored, 16 * NB)


class TurnWeights:

    def __init__(self, nc, name, ident, pairs):
        self.nc, self.name, self.ident, self.pairs = nc, name, ident, pairs

    def begin(self, ctx, sem):
        nc = self.nc
        self.raw = ctx.enter_context(nc.sbuf_tensor(f"{self.name}_raw", [P, 2, 4, D], F32))
        self.pt = ctx.enter_context(nc.psum_tensor(f"{self.name}_pT", [P, 2, 4, P], F32))
        self.loaded = [sem(f"weights_loaded{k}") for k in range(2)]
        self.turned, self.copied = sem("weights_turned"), sem("weights_copied")

    def load(self, sp):
        for m, (w, _) in enumerate(self.pairs):
            wait(sp, self.turned, (m - 1) * 4)
            sp.dma_start(self.raw[:, m % 2, :, :], w.rearrange("(c p) i -> p c i", p=P)).then_inc(self.loaded[m % 2], 16)

    def turn(self, pe):
        for m in range(len(self.pairs)):
            pe.wait_ge(self.loaded[m % 2], (m // 2 + 1) * 16)
            for ic in range(4):
                g = m * 4 + ic
                wait(pe, self.copied, g - 1)
                for oc in range(4):
                    ins = self.nc.tensor.transpose(self.pt[:, g % 2, oc, :],
                                                   self.raw[:, m % 2, oc, ic * P:(ic + 1) * P], self.ident)
                ins.then_inc(self.turned, 1)

    def copy(self, act):
        for m, (_, out) in enumerate(self.pairs):
            for ic in range(4):
                g = m * 4 + ic
                act.wait_ge(self.turned, g + 1)
                self.nc.scalar.copy(out[:, ic, :], self.pt[:, g % 2, :, :].rearrange("p o n -> p (o n)")
                                    ).then_inc(self.copied, 1)


GS = 4


def split3(link, nc, out, src, rest):
    link(nc.vector.tensor_copy(out[0], src))
    link(nc.vector.tensor_tensor(rest, src, out[0], ALU.subtract))
    link(nc.vector.tensor_copy(out[1], rest))
    link(nc.vector.tensor_tensor(rest, rest, out[1], ALU.subtract))
    link(nc.vector.tensor_copy(out[2], rest))


def edge_scores(nc, name, C, identb, est, edt, src_lo, src_block, loc, pair_block, es_out, ed_out,
                emb, types, weight, factor):
    U = 4
    STEPS = SLOTS // GS // U
    with ExitStack() as ctx:
        sb = lambda n, s, d: ctx.enter_context(nc.sbuf_tensor(f"{name}_{n}", s, d))
        ps = lambda n, s, d: ctx.enter_context(nc.psum_tensor(f"{name}_{n}", s, d))
        sem = stage_semaphores(nc, ctx, name)
        s3, d3 = sb("source3", [P, 3, NB, H], BF16), sb("target3", [P, 3, NB, H], BF16)
        rest = sb("rest", [P, NB, H], F32)
        oh = sb("onehots", [P, 2, 2, GS, P], BF16)
        ohT = sb("onehotsT", [P, 2, 2, GS, P], BF16)
        ohb = sb("onehot_block", [P, U, GS, NB], F32)
        mine = sb("of_own_block", [P, 2, GS, H, NB], F32)
        embv = sb("emb", [P, 8, H], F32)
        of_type = sb("of_type", [P, 2, SLOTS], F32)
        part = sb("factor_part", [P, SLOTS, H], F32)
        emb_in, s_pool = sem("emb_in"), sem("pool_chain")
        pT = ps("pT", [P, 2, 2, GS, P], BF16)
        pl = ps("pLook", [P, 2, D], F32)
        ES, ED = GS * NB * H, GS * H
        s_dve, tables = sem("dve_chain"), sem("tables_ready")
        built, turned, copied, looked = sem("built"), sem("turned"), sem("copied"), sem("looked")
        masked, taken = sem("masked"), sem("taken")
        block = ctx.enter_context(nc.Block())

        @block.sync
        def _(sp):
            sp.dma_start(flat(embv[:, :, :]), emb.rearrange("t h -> (t h)").partition_broadcast(P)).then_inc(emb_in, 16)
            sp.wait_ge(emb_in, 16)

        @block.gpsimd
        def _(pool):
            link = chain(pool, s_pool)
            pool.wait_ge(emb_in, 16)
            link(nc.gpsimd.tensor_scalar(flat(embv[:, :, :]), flat(embv[:, :, :]), 1.0, None, ALU.add))
            for t in range(8):
                link(nc.gpsimd.tensor_scalar(of_type[:, 0, :], types, float(t), None, ALU.is_equal))
                link(nc.gpsimd.tensor_tensor(of_type[:, 1, :], of_type[:, 0, :], weight, ALU.mult))
                link(nc.gpsimd.tensor_tensor(
                    part[:, :, :] if t else factor[:, :, :],
                    of_type[:, 1, :].unsqueeze(2).to_broadcast([P, SLOTS, H]),
                    embv[:, t, :].unsqueeze(1).to_broadcast([P, SLOTS, H]), ALU.mult))
                if t:
                    link(nc.gpsimd.tensor_tensor(factor[:, :, :], factor[:, :, :], part[:, :, :], ALU.add))

        @block.vector
        def _(v):
            link = chain(v, s_dve)
            split3(link, nc, [s3[:, n, :, :] for n in range(3)], est[:, :, :], rest[:, :, :])
            split3(link, nc, [d3[:, n, :, :] for n in range(3)], edt[:, :, :], rest[:, :, :])
            v.sem_inc(tables, 1)

            def build(i, u):
                wait(v, turned, i * U + (u - 1))
                s = bass.ds((i * U + u) * GS, GS)
                for n, col in ((0, src_lo), (1, loc)):
                    nc.vector.tensor_tensor(oh[:, u % 2, n, :, :],
                                            C.f("iota_p").unsqueeze(1).to_broadcast([P, GS, P]),
                                            col[:, s].unsqueeze(2).to_broadcast([P, GS, P]),
                                            ALU.is_equal).then_inc(built, 1)
                wait(v, masked, i * U + (u - U + 1))
                nc.vector.tensor_tensor(ohb[:, u, :, :],
                                        C.f("iota_p")[:, 0:NB].unsqueeze(1).to_broadcast([P, GS, NB]),
                                        src_block[:, s].unsqueeze(2).to_broadcast([P, GS, NB]),
                                        ALU.is_equal).then_inc(built, 1)

            def mask(i, u):
                g = i * U + u
                v.wait_ge(built, g * 3 + 3)
                v.wait_ge(looked, g + 1)
                wait(v, taken, g - 1)
                nc.vector.tensor_copy(ed_out[:, bass.ds(g * GS, GS), :],
                                      pl[:, u % 2, ES:ES + ED].rearrange("p (s h) -> p s h", h=H))
                nc.vector.tensor_tensor(
                    mine[:, u % 2, :, :, :],
                    pl[:, u % 2, 0:ES].rearrange("p (s b h) -> p s h b", h=H, b=NB),
                    ohb[:, u, :, :].unsqueeze(2).to_broadcast([P, GS, H, NB]), ALU.mult).then_inc(masked, 1)

            def take(i, u):
                g = i * U + u
                v.wait_ge(masked, g + 1)
                nc.vector.tensor_reduce(es_out[:, bass.ds(g * GS, GS), :], mine[:, u % 2, :, :, :],
                                        AX.X, ALU.add).then_inc(taken, 1)

            def step(i):
                for u in range(U):
                    build(i, u)
                    for lag, work in ((2, mask), (3, take)):
                        if u >= lag:
                            work(i, u - lag)
                        elif not isinstance(i, int):
                            work(i - 1, U + u - lag)
            peeled(v, STEPS, step)
            mask(STEPS - 1, U - 2)
            take(STEPS - 1, U - 3)
            mask(STEPS - 1, U - 1)
            take(STEPS - 1, U - 2)
            take(STEPS - 1, U - 1)

        @block.scalar
        def _(act):
            def step(i):
                for u in range(U):
                    g = i * U + u
                    act.wait_ge(turned, g + 1)
                    wait(act, looked, g - 1)
                    nc.scalar.copy(ohT[:, u % 2, :, :, :], pT[:, u % 2, :, :, :]).then_inc(copied, 1)
            peeled(act, STEPS, step)

        @block.tensor
        def _(pe):
            pe.wait_ge(tables, 1)

            def turn(i, u):
                g = i * U + u
                pe.wait_ge(built, g * 3 + 2)
                wait(pe, copied, g - 1)
                for n in range(2):
                    for s in range(GS):
                        ins = nc.tensor.transpose(pT[:, u % 2, n, s, :], oh[:, u % 2, n, s, :], identb[:, :])
                ins.then_inc(turned, 1)

            def look(i, u):
                g = i * U + u
                blocks = [pe.value_load(pair_block[0:1, bass.ds(g * (GS // 2) + q, 1)], min_val=0,
                                        max_val=NB - 1) for q in range(GS // 2)]
                pe.wait_ge(copied, g + 1)
                wait(pe, masked, g - 1)
                for s in range(GS):
                    for n in range(3):
                        nc.tensor.matmul(pl[:, u % 2, s * NB * H:(s + 1) * NB * H], ohT[:, u % 2, 0, s, :],
                                         flat(s3[:, n, :, :]), start=n == 0, stop=n == 2)
                    for n in range(3):
                        ins = nc.tensor.matmul(pl[:, u % 2, ES + s * H:ES + (s + 1) * H], ohT[:, u % 2, 1, s, :],
                                               flat(d3[:, n, bass.ds(blocks[s // 2], 1), :]),
                                               start=n == 0, stop=n == 2)
                ins.then_inc(looked, 1)

            def step(i):
                for u in range(U):
                    turn(i, u)
                    if u:
                        look(i, u - 1)
                    elif not isinstance(i, int):
                        look(i - 1, U - 1)
            peeled(pe, STEPS, step)
            look(STEPS - 1, U - 1)


EC = H + 1
L = SLOTS // PAIRS * P


def attention_weights(nc, name, C, es, ed, factor, loc, block_f, wt, turner):
    with ExitStack() as ctx:
        sb = lambda n, s, d: ctx.enter_context(nc.sbuf_tensor(f"{name}_{n}", s, d))
        scored = sb("scored", [P, SLOTS, EC], F32)
        seq = sb("sequence", [PAIRS, EC, L], F32)
        e, key = seq[:, 0:H, :], seq[:, H, :]
        first = sb("e_and_carried", [PAIRS, H, L], F32)
        t1, t2 = sb("t1", [PAIRS, H, L], F32), sb("t2", [PAIRS, H, L], F32)
        same, same_n = sb("same", [PAIRS, H, L], F32), sb("same_next", [PAIRS, H, L], F32)
        mask = sb("mask", [P, SLOTS], F32)
        link_mask = sb("link_mask", [PAIRS, L], F32)
        one = sb("one_run", [PAIRS, 1], F32)
        cols = sb("cols", [PAIRS, 5, H], F32)
        row = sb("row", [H, 5, PAIRS + 2], F32)
        cont = sb("continues", [H, PAIRS + 2], F32)
        outr = sb("outr", [H, 2, PAIRS + 2], F32)
        carry = sb("carry", [H, 2, PAIRS], F32)
        pT = ctx.enter_context(nc.psum_tensor(f"{name}_pT", [P, 5, D], F32))
        pt_small = ctx.enter_context(nc.psum_tensor(f"{name}_pSmall", [P, D], F32))
        pr = pt_small[0:H, 0:5 * PAIRS].rearrange("p (n j) -> p n j", n=5)
        pc = pt_small[0:PAIRS, 5 * PAIRS:5 * PAIRS + 2 * H].rearrange("p (n h) -> p n h", n=2)
        sem = stage_semaphores(nc, ctx, name)
        turner.begin(ctx, sem)
        s_dve, scored_ready, laid, seq_out, first_out = (
            sem("dve_chain"), sem("scored_ready"), sem("laid"), sem("seq_out"), sem("first_out"))
        turned, cols_ready, exp_in, exp_done, back = (
            sem("turned"), sem("cols_ready"), sem("exp_in"), sem("exp_done"), sem("back"))
        block = ctx.enter_context(nc.Block())

        @block.sync
        def _(sp):
            turner.load(sp)

        @block.scalar
        def _(act):
            turner.copy(act)
            for m in range(5):
                n = min(2, EC - 2 * m)
                act.wait_ge(laid, m + 1)
                nc.scalar.copy(seq[:, 2 * m:2 * m + n, :].rearrange("p n l -> p (n l)"),
                               pT[0:PAIRS, m, 0:n * L]).then_inc(seq_out, 1)
            for m in range(4):
                nc.scalar.copy(first[:, 2 * m:2 * m + 2, :].rearrange("p n l -> p (n l)"),
                               pT[0:PAIRS, m, :]).then_inc(first_out, 1)
            act.wait_ge(exp_in, 1)
            nc.scalar.activation(t1[:, :, :], t1[:, :, :], ACT.Exp).then_inc(exp_done, 1)
            for m in range(4):
                act.wait_ge(back, m + 1)
                for q in range(2):
                    nc.scalar.copy(
                        wt[:, :, 2 * m:2 * m + 2].rearrange("p (j q) h -> p q h j", q=2)[:, q, :, :],
                        pT[:, m, 0:4 * PAIRS].rearrange("p (h q j) -> p q h j", h=2, q=2)[:, q, :, :])

        @block.vector
        def _(v):
            link = chain(v, s_dve)
            link(nc.vector.tensor_scalar(mask[:, :], loc, 0.0, float(P), ALU.is_ge, ALU.mult))
            link(nc.vector.tensor_tensor(
                mask[:, :].rearrange("p (j s) -> p j s", s=2), mask[:, :].rearrange("p (j s) -> p j s", s=2),
                block_f.unsqueeze(2).to_broadcast([P, PAIRS, 2]), ALU.mult))
            link(nc.vector.tensor_tensor(scored[:, :, H], mask[:, :], loc, ALU.add))
            link(nc.vector.tensor_tensor(es[:, :, :], es[:, :, :], ed[:, :, :], ALU.add))
            link(nc.vector.scalar_tensor_tensor(flat(es[:, :, :]), flat(es[:, :, :]), 0.2, flat(es[:, :, :]),
                                                ALU.mult, ALU.max))
            nc.vector.tensor_tensor(scored[:, :, 0:H], es[:, :, :], factor[:, :, :], ALU.mult).then_inc(scored_ready, 1)
            link(nc.vector.memset(link_mask[:, 0:1], 0.0))
            link(nc.vector.memset(same_n[:, :, L - 1:L], 0.0))
            link(nc.vector.memset(row[:, :, :], 0.0))
            link(nc.vector.memset(cont[:, :], 0.0))
            link(nc.vector.memset(outr[:, :, :], 0.0))
            v.wait_ge(seq_out, 5)
            link(nc.vector.tensor_tensor(link_mask[:, 1:L], key[:, 1:L], key[:, 0:L - 1], ALU.is_equal))
            link(nc.vector.tensor_copy(same[:, :, :], link_mask[:, :].unsqueeze(1).to_broadcast([PAIRS, H, L])))
            link(nc.vector.tensor_copy(same_n[:, :, 0:L - 1],
                                       link_mask[:, 1:L].unsqueeze(1).to_broadcast([PAIRS, H, L - 1])))
            link(nc.vector.tensor_reduce(one[:, :], link_mask[:, 1:L], AX.X, ALU.min))
            link(nc.vector.tensor_copy(cols[:, 2, :], one[:, :].to_broadcast([PAIRS, H])))
            link(nc.vector.tensor_copy(cols[:, 3, :], key[:, 0:1].to_broadcast([PAIRS, H])))
            link(nc.vector.tensor_copy(cols[:, 4, :], key[:, L - 1:L].to_broadcast([PAIRS, H])))

            def forward(src, out):
                link(nc.vector.tensor_tensor_scan(flat(out[:, :, :]), flat(same[:, :, :]), flat(src[:, :, :]), 0.0,
                                                  ALU.mult, ALU.max))

            def backward(src, out):
                link(nc.vector.tensor_tensor_scan(flat(out[:, :, :])[:, ::-1], flat(same_n[:, :, :])[:, ::-1],
                                                  flat(src[:, :, :])[:, ::-1], 0.0, ALU.mult, ALU.max))

            v.wait_ge(first_out, 4)
            forward(first, t1)
            backward(first, t2)
            link(nc.vector.tensor_copy(cols[:, 0, :], t1[:, :, L - 1]))
            nc.vector.tensor_copy(cols[:, 1, :], t2[:, :, 0]).then_inc(cols_ready, 1)
            v.wait_ge(turned, 1)
            mid = slice(1, PAIRS + 1)
            link(nc.vector.tensor_copy(row[:, :, mid], pr))
            tail, head, whole = (row[:, n, mid] for n in range(3))
            link(nc.vector.tensor_tensor(cont[:, 2:PAIRS + 1], row[:, 3, 2:PAIRS + 1], row[:, 4, 1:PAIRS], ALU.is_equal))
            link(nc.vector.tensor_tensor(carry[:, 0, :], whole, cont[:, mid], ALU.mult))
            link(nc.vector.tensor_tensor(carry[:, 1, :], whole, cont[:, 2:PAIRS + 2], ALU.mult))
            link(nc.vector.tensor_tensor_scan(outr[:, 0, mid], carry[:, 0, :], tail, 0.0, ALU.mult, ALU.max))
            link(nc.vector.tensor_tensor_scan(outr[:, 1, mid][:, ::-1], carry[:, 1, :][:, ::-1],
                                              head[:, ::-1], 0.0, ALU.mult, ALU.max))
            link(nc.vector.tensor_tensor(carry[:, 0, :], cont[:, mid], outr[:, 0, 0:PAIRS], ALU.mult))
            nc.vector.tensor_tensor(carry[:, 1, :], cont[:, 2:PAIRS + 2], outr[:, 1, 2:PAIRS + 2], ALU.mult
                                    ).then_inc(cols_ready, 1)
            v.wait_ge(turned, 2)
            link(nc.vector.tensor_tensor(first[:, :, 0], first[:, :, 0], pc[:, 0, :], ALU.max))
            link(nc.vector.tensor_tensor(first[:, :, L - 1], first[:, :, L - 1], pc[:, 1, :], ALU.max))
            forward(first, t1)
            backward(t1, t2)
            nc.vector.tensor_tensor(t1[:, :, :], e, t2[:, :, :], ALU.subtract).then_inc(exp_in, 1)

        @block.tensor
        def _(pe):
            turner.turn(pe)
            pe.wait_ge(scored_ready, 1)
            for c in range(EC):
                by_pair = scored[:, :, c].rearrange("p (j q) -> p q j", q=2)
                for q in range(2):
                    at = c % 2 * L + q * P
                    ins = nc.tensor.transpose(pT[0:PAIRS, c // 2, at:at + P], by_pair[:, q, :], C.f("ident"))
                if c % 2 or c == EC - 1:
                    ins.then_inc(laid, 1)
            pe.wait_ge(cols_ready, 1)
            for n in range(5):
                ins = nc.tensor.transpose(pr[:, n, :], cols[:, n, :], C.f("ident", PAIRS)[:, 0:PAIRS])
            ins.then_inc(turned, 1)
            pe.wait_ge(cols_ready, 2)
            for n in range(2):
                ins = nc.tensor.transpose(pc[:, n, :], carry[:, n, :], C.f("ident", H)[:, 0:H])
            ins.then_inc(turned, 1)
            pe.wait_ge(exp_done, 1)
            for h in range(H):
                for q in range(2):
                    at = (h % 2 * 2 + q) * PAIRS
                    ins = nc.tensor.transpose(pT[:, h // 2, at:at + PAIRS], t1[:, h, q * P:(q + 1) * P],
                                              C.f("ident", PAIRS)[:, 0:PAIRS])
                if h % 2:
                    ins.then_inc(back, 1)


def unpack(link, nc, packed, itmp, loc, outs):
    v = itmp[:, 0, :]
    link(nc.vector.tensor_copy(v, packed))
    link(nc.vector.tensor_single_scalar(itmp[:, 1, :], v, 255, ALU.bitwise_and))
    link(nc.vector.tensor_scalar(loc[:, :], itmp[:, 1, :], 1.0, None, ALU.subtract))
    for out, shift, mask in outs:
        link(nc.vector.tensor_scalar(itmp[:, 1, :], v, shift, mask, ALU.logical_shift_right, ALU.bitwise_and))
        link(nc.vector.tensor_copy(out, itmp[:, 1, :]))


def gnn(nc, ins, consts, out):
    dram = lambda n, s: nc.dram_tensor(n, s, F32, kind="Internal").ap()
    tab = {n: dram(f"tab_{n}", s) for n, s in {
        "q": [NP, D], "h": [NP, D], "n": [NP, D], "y": [REL * NP, D],
        "w1": [REL * BCH, D * D // BCH], "w2": [REL * BCH, D * D // BCH]}.items()}
    VECS = ["L0_gnn_b", "L1_gnn_ln_gamma", "L1_gnn_ln_beta", "L2_gnn_bias", "L2_gnn_gamma", "L2_gnn_beta",
            "L3_gnn_bias1", "L3_gnn_bias2"]
    with ExitStack() as top:
        keep = lambda n, s, d: top.enter_context(nc.sbuf_tensor(n, s, d))
        C = Const(keep("const_table", [P, CONSTS.shape[1]], F32))
        identb = keep("identb", [P, P], BF16)
        ends = ("src", "dst")
        pairs = {k: keep(f"pair_block_{k}", [1, PAIRS], I32) for k in ends}
        blocks = {k: keep(f"block_of_pair_{k}", [P, PAIRS], F32) for k in ends}
        loc = {k: keep(f"loc_{k}", [P, SLOTS], F32) for k in ends}
        idx = {k: keep(f"idx_{k}", [P, SLOTS], I32) for k in ("q", "rel", "h")}
        packed = {k: keep(f"packed_{k}", [P, SLOTS], F32) for k in ends}
        src_block, src_lo, types, weight = (keep(n, [P, SLOTS], F32) for n in ("src_block", "src_lo", "types", "weight"))

        basis = [Basis(nc, f"basis{l}", ins[f"L3_gnn_basis{l + 1}"], ins[f"L3_gnn_att{l + 1}"], tab[f"w{l + 1}"])
                 for l in range(2)]

        with ExitStack() as ctx:
            sb = lambda n, s, d: ctx.enter_context(nc.sbuf_tensor(n, s, d))
            raw = sb("edge_ints", [EP, 4, T], I32)
            fld = sb("edge_fields", [EP, 6, T], F32)
            SRC, DST, T2, T8, WT, REL1 = range(6)
            with ExitStack() as c1:
                sem = stage_semaphores(nc, c1, "load")
                const_in, edges_in, s_dve = sem("const_in"), sem("edges_in"), sem("load_chain")
                block = c1.enter_context(nc.Block())

                @block.sync
                def _(sp):
                    for n, k in enumerate(("src", "dst", "edge_type_2", "edge_type_8")):
                        sp.dma_start(raw[:, n, :], ins[k].rearrange("(p t) -> p t", t=T)).then_inc(edges_in, 16)
                    sp.dma_start(fld[:, WT, :], ins["edge_weight"].rearrange("(p t) -> p t", t=T)).then_inc(edges_in, 16)
                    sp.dma_start(C.t[:, :], consts).then_inc(const_in, 16)
                    sp.wait_ge(edges_in, 80)
                    sp.wait_ge(const_in, 16)

                @block.vector
                def _(v):
                    link = chain(v, s_dve)
                    v.wait_ge(edges_in, 80)
                    link(nc.vector.tensor_copy(fld[:, 0:4, :], raw[:, :, :]))
                    link(nc.vector.tensor_scalar(fld[:, REL1, :], fld[:, T2, :], 0.0, None, ALU.not_equal))
                    v.wait_ge(const_in, 16)
                    link(nc.vector.tensor_copy(identb[:, :], C.f("ident")))
            f = lambda n: fld[:, n, :]
            SH1, SH2 = 8, 19
            sort_edges(nc, "src", C, identb, f(SRC), [(f(DST), 1 << SH1), (f(REL1), 1 << SH2)], None,
                       pairs["src"][:, :], blocks["src"][:, :], [packed["src"][:, :]], basis[1])
            sort_edges(nc, "dst", C, identb, f(DST), [(f(SRC), 1 << SH1), (f(T8), 1 << SH2)], f(WT),
                       pairs["dst"][:, :], blocks["dst"][:, :], [packed["dst"][:, :], weight[:, :]], basis[0])

        X, acc = (keep(n, [P, NB, D], F32) for n in ("x", "acc"))
        vec = keep("vectors", [P, len(VECS), D], F32)
        V = {n: vec[:, k, :] for k, n in enumerate(VECS)}
        W = [keep(f"weights{n}", [P, 4, D], F32) for n in range(3)]
        gate_w = keep("gate_w", [P, 2, 4, REL], F32)
        score_w = keep("score_w", [P, 4, 2 * H], F32)
        side = keep("side", [P, NB, H + 1], F32)
        est, edt = keep("e_src", [P, NB, H], F32), keep("e_dst", [P, NB, H], F32)
        wt = keep("edge_weights", [P, SLOTS, H + 1], F32)

        with ExitStack() as ctx:
            sem = stage_semaphores(nc, ctx, "load")
            itmp = ctx.enter_context(nc.sbuf_tensor("unpack_tmp", [P, 2, SLOTS], I32))
            W0 = ins["L0_gnn_W"]
            turner = TurnWeights(nc, "w01", C.f("ident"), [(W0[:, 0:D], W[0]), (W0[:, D:2 * D], W[1]),
                                                           (ins["L1_gnn_W"], W[2])])
            turner.begin(ctx, sem)
            a_in = ctx.enter_context(nc.sbuf_tensor("a_in", [P, 4, 2], F32))
            a_heads = ctx.enter_context(nc.sbuf_tensor("a_by_head", [P, 4, 2, H], F32))
            pW = ctx.enter_context(nc.psum_tensor("pScoreW", [P, 4, 2 * H], F32))
            a_loaded, a_spread, score_w_out = sem("a_loaded"), sem("a_spread"), sem("score_w_out")
            vecs_in, x_in, x_zero, s_dve = sem("vecs_in"), sem("x_in"), sem("x_zero"), sem("in_chain")
            block = ctx.enter_context(nc.Block())

            @block.tensor
            def _(pe):
                turner.turn(pe)
                pe.wait_ge(a_spread, 1)
                for ic in range(4):
                    for oc in range(4):
                        ins = nc.tensor.matmul(pW[:, ic, :], turner.raw[:, 0, oc, ic * P:(ic + 1) * P],
                                               flat(a_heads[:, oc, :, :]), start=oc == 0, stop=oc == 3)
                ins.then_inc(score_w_out, 1)

            @block.scalar
            def _(act):
                turner.copy(act)
                act.wait_ge(score_w_out, 1)
                nc.scalar.copy(score_w[:, :, :], pW[:, :, :])

            @block.sync
            def _(sp):
                turner.load(sp)

            @block.gpsimd
            def _(pool):
                with nc.allow_non_contiguous_dma("scoring and gate weights, once"):
                    for n, end in enumerate(ends):
                        pool.dma_start(a_in[:, :, n], ins[f"L1_gnn_a_{end}"].rearrange("h d -> (h d)").rearrange(
                            "(c p) -> p c", p=P)).then_inc(a_loaded, 16)
                    for l in range(2):
                        for r in range(REL):
                            pool.dma_start(gate_w[:, l, :, r],
                                         ins[f"L3_gnn_gate_w{l + 1}"][r, :, :].rearrange("(c p) a -> p (c a)", p=P)
                                         ).then_inc(vecs_in, 16)
                for k, n in enumerate(VECS):
                    pool.dma_start(vec[:, k, :], ins[n].partition_broadcast(P)).then_inc(vecs_in, 16)
                full = N // P
                pool.dma_start(X[:, 0:full, :], ins["x"][0:full * P, :].rearrange("(b p) d -> p b d", p=P)).then_inc(x_in, 16)
                pool.wait_ge(x_zero, 1)
                pool.dma_start(X[0:N - full * P, full, :], ins["x"][full * P:N, :]).then_inc(x_in, 16)
                pool.wait_ge(x_in, 32)
                pool.wait_ge(vecs_in, 16 * (len(VECS) + 4))

            @block.vector
            def _(v):
                link = chain(v, s_dve)
                nc.vector.memset(X[:, NB - 1, :], 0.0).then_inc(x_zero, 1)
                link(nc.vector.memset(acc[:, :, :], 0.0))
                link(nc.vector.memset(wt[:, :, H:H + 1], 1.0))
                v.wait_ge(a_loaded, 32)
                nc.vector.tensor_tensor(
                    a_heads[:, :, :, :],
                    C.f("head_of_feature").rearrange("p (c h) -> p c h", c=4).unsqueeze(2).to_broadcast([P, 4, 2, H]),
                    a_in[:, :, :].unsqueeze(3).to_broadcast([P, 4, 2, H]), ALU.mult).then_inc(a_spread, 1)
                unpack(link, nc, packed["src"][:, :], itmp, loc["src"],
                       [(idx["q"][:, :], SH1, 2047), (idx["rel"][:, :], SH2, 1)])
                link(nc.vector.scalar_tensor_tensor(idx["rel"][:, :], idx["rel"][:, :], float(NP), idx["q"][:, :],
                                                    ALU.mult, ALU.add))
                unpack(link, nc, packed["dst"][:, :], itmp, loc["dst"],
                       [(idx["h"][:, :], SH1, 2047), (src_block[:, :], SH1 + 7, 15), (src_lo[:, :], SH1, P - 1),
                        (types[:, :], SH2, 7)])

        def rows_of(tile, b):
            return flat(tile[:, bass.ds(b, 1), :])

        def take_x(link, v, normal, b, x):
            link.take_wait()
            return nc.vector.tensor_copy(x, rows_of(X, b))

        with ExitStack() as ctx:
            p_parts = [ctx.enter_context(nc.sbuf_tensor(f"p_{n}", [P, NB, D], mybir.dt.float32r))
                       for n in ("high", "low")]
            node_stage(nc, "n0", X, C.f("ident"), take_x, 0,
                       [(W[0], "bias_split", (V["L0_gnn_b"], p_parts)), (W[1], "table", None)], False,
                       [None, tab["q"]])
            edge_convolution(nc, "e0", C, identb, p_parts, tab["q"], idx["q"], loc["src"], pairs["src"], acc)

        def norm_of_sum(link, v, normal, b, x):
            a = rows_of(acc, b)
            link(nc.vector.tensor_tensor(a, a, rows_of(X, b), ALU.add))
            normal.stats(link, v, b, 0, a)
            return normal.apply(x, a)

        node_stage(nc, "n1", X, C.f("ident"), norm_of_sum, 1, [(W[2], "table", None)], True, [tab["h"]],
                   narrow=(score_w, (est, edt)))
        with ExitStack() as ctx:
            es, ed, factor = (ctx.enter_context(nc.sbuf_tensor(f"edge_{n}", [P, SLOTS, H], F32))
                              for n in ("e_src", "e_dst", "factor"))
            edge_scores(nc, "scores", C, identb, est, edt, src_lo, src_block, loc["dst"], pairs["dst"], es, ed,
                        ins["L1_gnn_et_emb"], types[:, :], weight[:, :], factor)
            turner = TurnWeights(nc, "w2", C.f("ident"), [(ins["L2_gnn_W_neigh"], W[0]), (ins["L2_gnn_W_self"], W[1])])
            attention_weights(nc, "att", C, es, ed, factor, loc["dst"][:, :], blocks["dst"][:, :],
                              wt, turner)
        edge_pass(nc, "e1", C, tab["h"], idx["h"], loc["dst"], pairs["dst"], acc, wt, side)

        held = keep("held", [P, NB, D], F32)
        xT = keep("xT", [P, NB, 4, P], F32)

        extra = [keep(f"more_weights{n}", [P, 4, D], F32) for n in range(2)]

        def rel_tiles(l):
            return (W[0], W[2], extra[0]) if l == 0 else (W[1], extra[1], W[2])

        def rel_weights(l):
            w0, w1, root = rel_tiles(l)
            return [(w[:, :, :], tab[f"w{l + 1}"][r * BCH:(r + 1) * BCH, :].rearrange("c (p o) -> p c o", o=D))
                    for r, w in enumerate((w0, w1))] + [
                        (root[:, :, :], ins[f"L3_gnn_root{l + 1}"].rearrange("(c p) o -> p c o", p=P))]

        def norm_affine_norm(link, v, normal, b, x, a, gamma, shift):
            normal.stats(link, v, b, 0, a)
            link(nc.vector.scalar_tensor_tensor(a, a, normal.mv[:, 0:1], gamma, ALU.subtract, ALU.mult))
            link(nc.vector.scalar_tensor_tensor(a, a, normal.rstd[:, 0:1], shift, ALU.mult, ALU.add))
            normal.stats(link, v, b, 1, a)
            return normal.apply(x, a)

        with ExitStack() as ctx:
            s_inv = stage_semaphores(nc, ctx, "n2")("inverse")
            shifted = ctx.enter_context(nc.sbuf_tensor("x_plus_beta", [P, 2, D], F32))
            inverse = ctx.enter_context(nc.sbuf_tensor("inverse_sums", [P, NB, H], F32))

            def invert_sums(v, done):
                link = chain(v, s_inv)
                link(nc.vector.tensor_scalar(inverse[:, :, :], side[:, :, 0:H], 1e-10, None, ALU.add))
                nc.vector.reciprocal(inverse[:, :, :], inverse[:, :, :]).then_inc(done, 1)

            def scale_and_shift(b, k):
                ah = rows_of(acc, b).rearrange("p (h d) -> p h d", h=H)
                w = flat(inverse[:, bass.ds(b, 1), :])
                nc.gpsimd.tensor_tensor(ah, ah, w.unsqueeze(2).to_broadcast([P, H, DH]), ALU.mult)
                return nc.gpsimd.tensor_tensor(shifted[:, k, :], rows_of(X, b), V["L1_gnn_ln_beta"], ALU.add)

            def after_attention(link, v, normal, b, x, k):
                a = rows_of(acc, b)
                link(nc.vector.tensor_tensor(a, a, rows_of(X, b), ALU.add))
                return norm_affine_norm(link, v, normal, b, x, a, V["L1_gnn_ln_gamma"], shifted[:, k, :])

            node_stage(nc, "n2", X, C.f("ident"), after_attention, 2, [(W[0], "table", None)], True, [tab["n"]],
                       keep_xT=xT, ahead=(invert_sums, scale_and_shift))
        edge_pass(nc, "e2", C, tab["n"], idx["h"], loc["dst"], pairs["dst"], acc,
                  own=(xT, W[1], V["L2_gnn_bias"], held), fetch=rel_weights(0), shift=(X, V["L2_gnn_beta"]))

        def after_mean(link, v, normal, b, x):
            a, n = rows_of(acc, b), flat(side[:, bass.ds(b, 1), H:H + 1])
            link(nc.vector.tensor_scalar(n, n, 1.0, None, ALU.max))
            link.take_wait()
            link(nc.vector.reciprocal(n, n))
            link(nc.vector.scalar_tensor_tensor(a, a, n, rows_of(held, b), ALU.mult, ALU.add))
            return norm_affine_norm(link, v, normal, b, x, a, V["L2_gnn_gamma"], rows_of(X, b))

        def relu_of_sum(link, v, normal, b, x):
            a = rows_of(acc, b)
            link(nc.vector.tensor_tensor(a, a, rows_of(held, b), ALU.add))
            return nc.vector.tensor_scalar(x, a, 0.0, None, ALU.max)

        for l in range(2):
            w0, w1, root = rel_tiles(l)
            bias = V[f"L3_gnn_bias{l + 1}"]
            node_stage(nc, f"n{3 + l}", X, C.f("ident"), relu_of_sum if l else after_mean, 0 if l else 2,
                       [(w0, "gated", 0), (w1, "gated", 1)], l == 0,
                       [tab["y"][0:NP, :], tab["y"][NP:REL * NP, :]], narrow=(gate_w[:, l, :, :], None), keep_xT=xT)
            edge_pass(nc, f"e{3 + l}", C, tab["y"], idx["rel"], loc["src"], pairs["src"], acc,
                      own=(xT, root, X if l else bias, held), fetch=() if l else rel_weights(1),
                      shift=(X, bias) if l else None)

        last_norm(nc, "last", acc, held, out)


_INS = ["x", "src", "dst", "edge_type_2", "edge_type_8", "edge_weight", "L0_gnn_W", "L0_gnn_b", "L1_gnn_W",
        "L1_gnn_a_src", "L1_gnn_a_dst", "L1_gnn_et_emb", "L1_gnn_ln_gamma", "L1_gnn_ln_beta", "L2_gnn_W_self",
        "L2_gnn_W_neigh", "L2_gnn_bias", "L2_gnn_gamma", "L2_gnn_beta", "L3_gnn_basis1", "L3_gnn_att1",
        "L3_gnn_gate_w1", "L3_gnn_root1", "L3_gnn_bias1", "L3_gnn_basis2", "L3_gnn_att2", "L3_gnn_gate_w2",
        "L3_gnn_root2", "L3_gnn_bias2"]


def kernel(**inputs):
    import numpy as _np
    import concourse.bacc as _bacc
    from concourse import mybir as _mybir
    from concourse.bass_utils import run_bass_kernel_spmd as _run

    nc = _bacc.Bacc("TRN2", target_bir_lowering=False, num_devices=1)
    arrays, aps = {"constants": CONSTS}, {}
    consts = nc.dram_tensor("constants", CONSTS.shape, _mybir.dt.float32, kind="ExternalInput").ap()
    for name in _INS:
        a = _np.ascontiguousarray(inputs[name])
        arrays[f"in_{name}"] = a
        aps[name] = nc.dram_tensor(f"in_{name}", a.shape, _mybir.dt.from_np(a.dtype), kind="ExternalInput").ap()
    out = nc.dram_tensor("out", (N, D), _mybir.dt.float32, kind="ExternalOutput").ap()
    gnn(nc, aps, consts, out)
    r = _run(nc, [arrays], core_ids=[0])
    return r.results[0]["out"]
```
